# Optimizing a Trainium2 kernel written in Bass

```python
import numpy as np
import jax
import jax.numpy as jnp

def _softmax(x, axis=-1):
    return jax.nn.softmax(x, axis=axis)

def _gelu(x):
    return jax.nn.gelu(x, approximate=True)

def _silu(x):
    return jax.nn.silu(x)

def _sigmoid(x):
    return jax.nn.sigmoid(x)

def _layernorm(x, axis=-1, eps=1e-05):
    m = jnp.mean(x, axis=axis, keepdims=True)
    v = jnp.var(x, axis=axis, keepdims=True)
    return (x - m) / jnp.sqrt(v + eps)

def _scatter_add(tgt, idx, src, axis=0):
    return tgt.at[idx].add(src)

def _segment_sum(src, seg, n):
    return jax.ops.segment_sum(src, seg, n)
kernel_name = 'mk_perceiver_d2_seqx_r8_e91586'

def setup_inputs(seed: int=0):
    np.random.seed(seed)
    _w = jnp.asarray

    def _rec_inputs():
        import jax
        import jax.numpy as jnp
        _rk = jax.random.key(seed)
        x = -0.0005146 + 1 * jax.random.normal(jax.random.fold_in(_rk, 1), (16, 32, 512), jnp.float32)
        _lenS = 32 - jax.random.randint(jax.random.fold_in(_rk, 7), (16,), 0, max(1, 32 // 4) + 1, jnp.int32)
        _lenS2 = 512 - jax.random.randint(jax.random.fold_in(_rk, 8), (16,), 0, max(1, 512 // 4) + 1, jnp.int32)
        _ctx_4096P = jax.random.normal(jax.random.fold_in(_rk, 11), (16, 16, 512), jnp.float32)
        _ctx_4096c = jax.random.dirichlet(jax.random.fold_in(_rk, 511), 0.3 * jnp.ones((16,), jnp.float32), (16, 512))
        _ctx_4096t = jnp.einsum('bsk,bkd->bsd', _ctx_4096c, _ctx_4096P)
        _ctx_4096t = _ctx_4096t * jax.lax.rsqrt(jnp.mean(jnp.square(_ctx_4096t)) + 1e-12) * 0.953939
        ctx_4096 = -0.0142356 + 1.00583 * (_ctx_4096t + 0.3 * jax.random.normal(jax.random.fold_in(_rk, 611), (16, 512, 512), jnp.float32))
        return (x, ctx_4096)
    x, ctx_4096 = _rec_inputs()

    def _L0_xattn_setup():
        import jax, jax.numpy as jnp
        import numpy as np
        K = 10
        NUM_BITS = 10
        M_METHODS = 4

        def _quantize(coords, num_bits=NUM_BITS):
            cmin = coords.min(axis=1, keepdims=True)
            cmax = coords.max(axis=1, keepdims=True)
            scale = (2 ** num_bits - 1) / (cmax - cmin + 1e-06)
            q = jnp.floor((coords - cmin) * scale)
            return jnp.clip(q, 0, 2 ** num_bits - 1).astype(jnp.int32)

        def _morton_key(q):
            x, y, z = (q[..., 0], q[..., 1], q[..., 2])
            key = jnp.zeros(x.shape, dtype=jnp.int32)
            for b in range(NUM_BITS):
                key = key | (x >> b & 1) << 3 * b + 2 | (y >> b & 1) << 3 * b + 1 | (z >> b & 1) << 3 * b
            return key

        def _hilbert_key(q, num_bits=NUM_BITS):
            n = 3
            X = [q[..., i] for i in range(n)]
            M = 1 << num_bits - 1
            Q = M
            while Q > 1:
                P = Q - 1
                for i in range(n):
                    cond = X[i] & Q > 0
                    t = (X[0] ^ X[i]) & P
                    new_X0 = jnp.where(cond, X[0] ^ P, X[0] ^ t)
                    if i != 0:
                        X[i] = jnp.where(cond, X[i], X[i] ^ t)
                    X[0] = new_X0
                Q >>= 1
            for i in range(1, n):
                X[i] = X[i] ^ X[i - 1]
            t = jnp.zeros_like(X[0])
            Q = M
            while Q > 1:
                t = jnp.where(X[n - 1] & Q > 0, t ^ Q - 1, t)
                Q >>= 1
            X = [xi ^ t for xi in X]
            key = jnp.zeros(X[0].shape, dtype=jnp.int32)
            for b in range(num_bits - 1, -1, -1):
                for i in range(n):
                    key = key << 1 | X[i] >> b & 1
            return key

        def _sorted_indices(coords_bn3):
            q = _quantize(coords_bn3)
            qt = q[..., jnp.array([1, 0, 2])]
            keys = [_morton_key(q), _morton_key(qt), _hilbert_key(q), _hilbert_key(qt)]
            return [jnp.argsort(kk, axis=1) for kk in keys]

        def _window_inds(sorted_idx, k=K):
            B, N = sorted_idx.shape
            i = jnp.arange(N)
            start = jnp.maximum(0, i - k // 2)
            end = jnp.minimum(N, i + k // 2 + 1)
            pos = jnp.minimum(start[:, None] + jnp.arange(k)[None, :], (end - 1)[:, None])
            return jnp.take(sorted_idx, pos, axis=1)

        def _get_graph_features(feats, inds_list, perm, W_lin, b_lin, k=K):
            B, N, C = feats.shape
            center = feats[:, :, None, :]
            gather = jax.vmap(lambda f, idx: f[idx])
            per_method = []
            for inds in inds_list:
                neigh = gather(feats, inds)
                gf = jnp.concatenate([jnp.broadcast_to(center, (B, N, k, C)), neigh - center], axis=-1)
                per_method.append(gf)
            allf = jnp.stack(per_method, axis=-1)
            allf = allf[..., perm]
            total = 2 * C * M_METHODS
            x = allf.reshape(B * N, k, total)
            x16 = x.astype(jnp.float16).astype(jnp.float32)
            headdim = min(32, total)
            nheads = total // headdim
            qh = x16.reshape(B * N, k, nheads, headdim)
            scores = jnp.einsum('bihd,bjhd->bhij', qh, qh) / np.float32(np.sqrt(headdim))
            attn = jax.nn.softmax(scores, axis=-1)
            out = jnp.einsum('bhij,bjhd->bihd', attn, qh).reshape(B * N, k, total)
            fused = out @ W_lin.T + b_lin
            return fused.reshape(B, N, k, 64)

        def _instance_norm(x, axes):
            mu = x.mean(axis=axes, keepdims=True)
            var = x.var(axis=axes, keepdims=True)
            return (x - mu) / jnp.sqrt(var + 1e-05)

        def _lrelu(x):
            return jnp.where(x > 0, x, 0.2 * x)
        key = jax.random.key(seed)
        ks = jax.random.split(key, 8)
        B, N, C = (2, 512, 32)
        tot = M_METHODS * 2 * C
        s = 0.02
        return {'coords': jax.random.normal(ks[0], (B, 3, N), jnp.float32), 'feats': jax.random.normal(ks[1], (B, C, N), jnp.float32), 'W_lin1': jax.random.normal(ks[2], (64, tot), jnp.float32) * s, 'b_lin1': jnp.zeros((64,), jnp.float32), 'W_lin2': jax.random.normal(ks[3], (64, tot), jnp.float32) * s, 'b_lin2': jnp.zeros((64,), jnp.float32), 'W_conv1': jax.random.normal(ks[4], (C, 2 * C), jnp.float32) * s, 'W_conv2': jax.random.normal(ks[5], (2 * C, 2 * C), jnp.float32) * s, 'W_conv3': jax.random.normal(ks[6], (C, 4 * C), jnp.float32) * s}
    _L0_xattn_all = _L0_xattn_setup()
    _L0_xattn_in = {k: v for k, v in _L0_xattn_all.items() if k in ('W_lin1', 'b_lin1', 'W_lin2', 'b_lin2', 'W_conv1', 'W_conv2', 'W_conv3')}
    del _L0_xattn_all

    def _L0_attn_setup():
        import jax, jax.numpy as jnp
        import numpy as np
        HDC_DIM = 512
        N_HEADS = 4
        HEAD_DIM = HDC_DIM // N_HEADS

        def _ste_sign(w):
            alpha = jnp.mean(jnp.abs(w), axis=-1, keepdims=True)
            hard = alpha * jnp.sign(w)
            hard = jnp.where(hard == 0, alpha, hard)
            return jax.lax.stop_gradient(hard - w) + w
        key = jax.random.key(seed)
        kx, kq, kk, kv = jax.random.split(key, 4)
        B, T = (4, 256)
        x = jax.random.normal(kx, (B, T, HDC_DIM), dtype=jnp.float32)
        bv_q = jax.random.normal(kq, (N_HEADS, HEAD_DIM), dtype=jnp.float32) * 0.02
        bv_k = jax.random.normal(kk, (N_HEADS, HEAD_DIM), dtype=jnp.float32) * 0.02
        bv_v = jax.random.normal(kv, (N_HEADS, HEAD_DIM), dtype=jnp.float32) * 0.02
        return {'x': x, 'bv_q': bv_q, 'bv_k': bv_k, 'bv_v': bv_v}
    _L0_attn_all = _L0_attn_setup()
    _L0_attn_in = {k: v for k, v in _L0_attn_all.items() if k in ('bv_q', 'bv_k', 'bv_v')}
    del _L0_attn_all

    def _L0_ffn_setup():
        import jax, jax.numpy as jnp
        import numpy as np
        B, S, D_IN, D_OUT = (2, 256, 512, 512)
        E, K, R = (8, 2, 16)
        SCALING = 32.0 / 16.0
        key = jax.random.key(seed)
        ks = jax.random.split(key, 6)
        x = jax.random.normal(ks[0], (B, S, D_IN), dtype=jnp.float32)
        gate_w = jax.random.normal(ks[1], (E, D_IN), dtype=jnp.float32) * 0.02
        base_w = jax.random.normal(ks[2], (D_OUT, D_IN), dtype=jnp.float32) * 0.02
        base_b = jax.random.normal(ks[3], (D_OUT,), dtype=jnp.float32) * 0.02
        lora_A = jax.random.normal(ks[4], (E, R, D_IN), dtype=jnp.float32) * 0.02
        lora_B = jax.random.normal(ks[5], (E, D_OUT, R), dtype=jnp.float32) * 0.02
        return {'x': x, 'gate_w': gate_w, 'base_w': base_w, 'base_b': base_b, 'lora_A': lora_A, 'lora_B': lora_B}
    _L0_ffn_all = _L0_ffn_setup()
    _L0_ffn_in = {k: v for k, v in _L0_ffn_all.items() if k in ('gate_w', 'base_w', 'base_b', 'lora_A', 'lora_B')}
    del _L0_ffn_all

    def _L1_xattn_setup():
        import jax, jax.numpy as jnp
        import numpy as np
        HEADS = 32
        KV_HEADS = 8
        HEAD_DIM = 128
        EPS = 1e-06

        def rms_norm(x, w):
            var = jnp.mean(jnp.square(x.astype(jnp.float32)), axis=-1, keepdims=True)
            return (x.astype(jnp.float32) * jax.lax.rsqrt(var + EPS)).astype(x.dtype) * w
        key = jax.random.key(seed)
        ks = jax.random.split(key, 6)
        bsz, n_lat, seq, hidden = (8, 64, 512, 512)
        return {'latents': jax.random.normal(ks[0], (bsz, n_lat, hidden), jnp.float32), 'context': jax.random.normal(ks[1], (bsz, seq, hidden), jnp.float32), 'Wq': jax.random.normal(ks[2], (hidden, HEADS * HEAD_DIM), jnp.float32) * 0.02, 'Wk': jax.random.normal(ks[3], (hidden, KV_HEADS * HEAD_DIM), jnp.float32) * 0.02, 'Wv': jax.random.normal(ks[4], (hidden, KV_HEADS * HEAD_DIM), jnp.float32) * 0.02, 'Wo': jax.random.normal(ks[5], (HEADS * HEAD_DIM, hidden), jnp.float32) * 0.02, 'q_norm_w': jnp.ones((HEAD_DIM,), jnp.float32), 'k_norm_w': jnp.ones((HEAD_DIM,), jnp.float32)}
    _L1_xattn_all = _L1_xattn_setup()
    _L1_xattn_in = {k: v for k, v in _L1_xattn_all.items() if k in ('Wq', 'Wk', 'Wv', 'Wo', 'q_norm_w', 'k_norm_w')}
    del _L1_xattn_all

    def _L1_attn_setup():
        import jax, jax.numpy as jnp
        import numpy as np
        HID = 512
        DM = 128
        DIN = 2 * DM
        DST = 16
        HD = 64
        NH = DIN // HD
        DCONV = 7
        CONV_DIM = DIN + 2 * DST
        DIN_PROJ = 2 * DIN + 2 * DST + 2 * NH
        SEQ, BATCH = (256, 4)

        def _causal_conv(x, w, b):
            y = jax.lax.conv_general_dilated(jnp.transpose(x, (0, 2, 1)), w, (1,), [(DCONV - 1, 0)], feature_group_count=CONV_DIM, dimension_numbers=('NCH', 'OIH', 'NCH'))
            return jnp.transpose(y, (0, 2, 1)) + b

        def _ssm_scan(x, dt, A, B, C):
            dA = jnp.exp(dt * A)
            dBx = dt[..., None] * x

            def step(h, t):
                dA_t, dBx_t, B_t, C_t = t
                h = dA_t[:, :, None, None] * h + dBx_t[..., None] * B_t[:, None, None, :]
                y = jnp.einsum('bhpn,bn->bhp', h, C_t)
                return (h, y)
            h0 = jnp.zeros((x.shape[0], NH, HD, DST), x.dtype)
            _, ys = jax.lax.scan(step, h0, (jnp.moveaxis(dA, 1, 0), jnp.moveaxis(dBx, 1, 0), jnp.moveaxis(B, 1, 0), jnp.moveaxis(C, 1, 0)))
            return jnp.moveaxis(ys, 0, 1)

        def _hydra(u, in_w, conv_w, conv_b, dt_bias, A_log, D, fcD_w, norm_w, out_w):
            b, l, _ = u.shape
            zxbcdt = u @ in_w.T
            z = zxbcdt[..., :DIN]
            xBC = zxbcdt[..., DIN:DIN + CONV_DIM]
            dt2 = zxbcdt[..., DIN + CONV_DIM:]
            dt_fw = jax.nn.softplus(dt2[..., :NH] + dt_bias)
            dt_bw = jax.nn.softplus(jnp.flip(dt2[..., NH:], 1) + dt_bias)
            xBC = jax.nn.silu(_causal_conv(xBC, conv_w, conv_b))
            xs = xBC[..., :DIN]
            Bm = xBC[..., DIN:DIN + DST]
            Cm = xBC[..., DIN + DST:]
            A = -jnp.exp(A_log)
            x4 = xs.reshape(b, l, NH, HD)
            y_fw = _ssm_scan(x4, dt_fw, A, Bm, Cm).reshape(b, l, DIN)
            y_bw = jnp.flip(_ssm_scan(jnp.flip(x4, 1), dt_bw, A, jnp.flip(Bm, 1), jnp.flip(Cm, 1)).reshape(b, l, DIN), 1)
            zero = jnp.zeros((b, 1, DIN), u.dtype)
            y = jnp.concatenate([zero, y_fw[:, :-1]], 1) + jnp.concatenate([y_bw[:, 1:], zero], 1)
            y = y + xs * jnp.repeat(xs @ fcD_w.T + D, HD, axis=-1)
            yz = y * jax.nn.silu(z)
            y = yz * jax.lax.rsqrt(jnp.mean(jnp.square(yz), -1, keepdims=True) + 1e-05) * norm_w
            return y @ out_w.T
        key = jax.random.key(seed)
        ks = jax.random.split(key, 12)
        rn = lambda k, shape, s=0.02: jax.random.normal(k, shape, jnp.float32) * s
        dt = jnp.exp(jax.random.uniform(ks[5], (NH,), jnp.float32, np.log(0.001), np.log(0.1)))
        return dict(x=jax.random.normal(ks[0], (SEQ, BATCH, HID), jnp.float32), w_down=rn(ks[1], (DM, HID)), b_down=jnp.zeros((DM,), jnp.float32), w_up=rn(ks[2], (HID, DM)), b_up=jnp.zeros((HID,), jnp.float32), gate1=jnp.asarray(0.6, jnp.float32), hy_in_w=rn(ks[3], (DIN_PROJ, DM)), hy_conv_w=rn(ks[4], (CONV_DIM, 1, DCONV), 0.2), hy_conv_b=jnp.zeros((CONV_DIM,), jnp.float32), hy_dt_bias=jnp.log(jnp.expm1(dt)), hy_A_log=jnp.log(jax.random.uniform(ks[6], (NH,), jnp.float32, 1.0, 16.0)), hy_D=jnp.ones((NH,), jnp.float32), hy_fcD_w=rn(ks[7], (NH, DIN)), hy_norm_w=jnp.ones((DIN,), jnp.float32), hy_out_w=rn(ks[8], (DM, DIN)))
    _L1_attn_all = _L1_attn_setup()
    _L1_attn_in = {k: v for k, v in _L1_attn_all.items() if k in ('w_down', 'b_down', 'w_up', 'b_up', 'gate1', 'hy_in_w', 'hy_conv_w', 'hy_conv_b', 'hy_dt_bias', 'hy_A_log', 'hy_D', 'hy_fcD_w', 'hy_norm_w', 'hy_out_w')}
    del _L1_attn_all

    def _L1_ffn_setup():
        import jax, jax.numpy as jnp
        import numpy as np
        B, S, IN, OUT = (4, 256, 512, 512)
        E, K, R = (8, 2, 16)
        CAP_FACTOR = 3.0
        ALPHA = 1.0 / R
        LN_EPS = 1e-05
        key = jax.random.key(seed)
        ks = jax.random.split(key, 6)
        return {'x': jax.random.normal(ks[0], (B, S, IN), dtype=jnp.float32), 'weight': jax.random.normal(ks[1], (OUT, IN), dtype=jnp.float32) * 0.02, 'lora_A': jax.random.normal(ks[2], (E, IN, R), dtype=jnp.float32) / np.sqrt(R), 'lora_B': jax.random.normal(ks[3], (E, R, OUT), dtype=jnp.float32) * 0.02, 'gw1': jax.random.normal(ks[4], (4 * E, IN), dtype=jnp.float32) * 0.02, 'gb1': jnp.zeros((4 * E,), dtype=jnp.float32), 'ln_gamma': jnp.ones((4 * E,), dtype=jnp.float32), 'ln_beta': jnp.zeros((4 * E,), dtype=jnp.float32), 'gw2': jax.random.normal(ks[5], (E, 4 * E), dtype=jnp.float32) * 0.02, 'gb2': jnp.zeros((E,), dtype=jnp.float32)}
    _L1_ffn_all = _L1_ffn_setup()
    _L1_ffn_in = {k: v for k, v in _L1_ffn_all.items() if k in ('weight', 'lora_A', 'lora_B', 'gw1', 'gb1', 'ln_gamma', 'ln_beta', 'gw2', 'gb2')}
    del _L1_ffn_all
    return {'x': x, 'ctx_4096': ctx_4096, 'L0_xattn_W_lin1': _L0_xattn_in['W_lin1'], 'L0_xattn_b_lin1': _L0_xattn_in['b_lin1'], 'L0_xattn_W_lin2': _L0_xattn_in['W_lin2'], 'L0_xattn_b_lin2': _L0_xattn_in['b_lin2'], 'L0_xattn_W_conv1': _L0_xattn_in['W_conv1'], 'L0_xattn_W_conv2': _L0_xattn_in['W_conv2'], 'L0_xattn_W_conv3': _L0_xattn_in['W_conv3'], 'L0_attn_bv_q': _L0_attn_in['bv_q'], 'L0_attn_bv_k': _L0_attn_in['bv_k'], 'L0_attn_bv_v': _L0_attn_in['bv_v'], 'L0_ffn_gate_w': _L0_ffn_in['gate_w'], 'L0_ffn_base_w': _L0_ffn_in['base_w'], 'L0_ffn_base_b': _L0_ffn_in['base_b'], 'L0_ffn_lora_A': _L0_ffn_in['lora_A'], 'L0_ffn_lora_B': _L0_ffn_in['lora_B'], 'L1_xattn_Wq': _L1_xattn_in['Wq'], 'L1_xattn_Wk': _L1_xattn_in['Wk'], 'L1_xattn_Wv': _L1_xattn_in['Wv'], 'L1_xattn_Wo': _L1_xattn_in['Wo'], 'L1_xattn_q_norm_w': _L1_xattn_in['q_norm_w'], 'L1_xattn_k_norm_w': _L1_xattn_in['k_norm_w'], 'L1_attn_w_down': _L1_attn_in['w_down'], 'L1_attn_b_down': _L1_attn_in['b_down'], 'L1_attn_w_up': _L1_attn_in['w_up'], 'L1_attn_b_up': _L1_attn_in['b_up'], 'L1_attn_gate1': _L1_attn_in['gate1'], 'L1_attn_hy_in_w': _L1_attn_in['hy_in_w'], 'L1_attn_hy_conv_w': _L1_attn_in['hy_conv_w'], 'L1_attn_hy_conv_b': _L1_attn_in['hy_conv_b'], 'L1_attn_hy_dt_bias': _L1_attn_in['hy_dt_bias'], 'L1_attn_hy_A_log': _L1_attn_in['hy_A_log'], 'L1_attn_hy_D': _L1_attn_in['hy_D'], 'L1_attn_hy_fcD_w': _L1_attn_in['hy_fcD_w'], 'L1_attn_hy_norm_w': _L1_attn_in['hy_norm_w'], 'L1_attn_hy_out_w': _L1_attn_in['hy_out_w'], 'L1_ffn_weight': _L1_ffn_in['weight'], 'L1_ffn_lora_A': _L1_ffn_in['lora_A'], 'L1_ffn_lora_B': _L1_ffn_in['lora_B'], 'L1_ffn_gw1': _L1_ffn_in['gw1'], 'L1_ffn_gb1': _L1_ffn_in['gb1'], 'L1_ffn_ln_gamma': _L1_ffn_in['ln_gamma'], 'L1_ffn_ln_beta': _L1_ffn_in['ln_beta'], 'L1_ffn_gw2': _L1_ffn_in['gw2'], 'L1_ffn_gb2': _L1_ffn_in['gb2']}

def reference(x, ctx_4096, L0_xattn_W_lin1, L0_xattn_b_lin1, L0_xattn_W_lin2, L0_xattn_b_lin2, L0_xattn_W_conv1, L0_xattn_W_conv2, L0_xattn_W_conv3, L0_attn_bv_q, L0_attn_bv_k, L0_attn_bv_v, L0_ffn_gate_w, L0_ffn_base_w, L0_ffn_base_b, L0_ffn_lora_A, L0_ffn_lora_B, L1_xattn_Wq, L1_xattn_Wk, L1_xattn_Wv, L1_xattn_Wo, L1_xattn_q_norm_w, L1_xattn_k_norm_w, L1_attn_w_down, L1_attn_b_down, L1_attn_w_up, L1_attn_b_up, L1_attn_gate1, L1_attn_hy_in_w, L1_attn_hy_conv_w, L1_attn_hy_conv_b, L1_attn_hy_dt_bias, L1_attn_hy_A_log, L1_attn_hy_D, L1_attn_hy_fcD_w, L1_attn_hy_norm_w, L1_attn_hy_out_w, L1_ffn_weight, L1_ffn_lora_A, L1_ffn_lora_B, L1_ffn_gw1, L1_ffn_gb1, L1_ffn_ln_gamma, L1_ffn_ln_beta, L1_ffn_gw2, L1_ffn_gb2):
    import jax
    import jax.numpy as jnp

    def _L0_xattn_ref(coords, feats, W_lin1, b_lin1, W_lin2, b_lin2, W_conv1, W_conv2, W_conv3):
        import jax, jax.numpy as jnp
        import numpy as np
        K = 10
        NUM_BITS = 10
        M_METHODS = 4

        def _quantize(coords, num_bits=NUM_BITS):
            cmin = coords.min(axis=1, keepdims=True)
            cmax = coords.max(axis=1, keepdims=True)
            scale = (2 ** num_bits - 1) / (cmax - cmin + 1e-06)
            q = jnp.floor((coords - cmin) * scale)
            return jnp.clip(q, 0, 2 ** num_bits - 1).astype(jnp.int32)

        def _morton_key(q):
            x, y, z = (q[..., 0], q[..., 1], q[..., 2])
            key = jnp.zeros(x.shape, dtype=jnp.int32)
            for b in range(NUM_BITS):
                key = key | (x >> b & 1) << 3 * b + 2 | (y >> b & 1) << 3 * b + 1 | (z >> b & 1) << 3 * b
            return key

        def _hilbert_key(q, num_bits=NUM_BITS):
            n = 3
            X = [q[..., i] for i in range(n)]
            M = 1 << num_bits - 1
            Q = M
            while Q > 1:
                P = Q - 1
                for i in range(n):
                    cond = X[i] & Q > 0
                    t = (X[0] ^ X[i]) & P
                    new_X0 = jnp.where(cond, X[0] ^ P, X[0] ^ t)
                    if i != 0:
                        X[i] = jnp.where(cond, X[i], X[i] ^ t)
                    X[0] = new_X0
                Q >>= 1
            for i in range(1, n):
                X[i] = X[i] ^ X[i - 1]
            t = jnp.zeros_like(X[0])
            Q = M
            while Q > 1:
                t = jnp.where(X[n - 1] & Q > 0, t ^ Q - 1, t)
                Q >>= 1
            X = [xi ^ t for xi in X]
            key = jnp.zeros(X[0].shape, dtype=jnp.int32)
            for b in range(num_bits - 1, -1, -1):
                for i in range(n):
                    key = key << 1 | X[i] >> b & 1
            return key

        def _sorted_indices(coords_bn3):
            q = _quantize(coords_bn3)
            qt = q[..., jnp.array([1, 0, 2])]
            keys = [_morton_key(q), _morton_key(qt), _hilbert_key(q), _hilbert_key(qt)]
            return [jnp.argsort(kk, axis=1) for kk in keys]

        def _window_inds(sorted_idx, k=K):
            B, N = sorted_idx.shape
            i = jnp.arange(N)
            start = jnp.maximum(0, i - k // 2)
            end = jnp.minimum(N, i + k // 2 + 1)
            pos = jnp.minimum(start[:, None] + jnp.arange(k)[None, :], (end - 1)[:, None])
            return jnp.take(sorted_idx, pos, axis=1)

        def _get_graph_features(feats, inds_list, perm, W_lin, b_lin, k=K):
            B, N, C = feats.shape
            center = feats[:, :, None, :]
            gather = jax.vmap(lambda f, idx: f[idx])
            per_method = []
            for inds in inds_list:
                neigh = gather(feats, inds)
                gf = jnp.concatenate([jnp.broadcast_to(center, (B, N, k, C)), neigh - center], axis=-1)
                per_method.append(gf)
            allf = jnp.stack(per_method, axis=-1)
            allf = allf[..., perm]
            total = 2 * C * M_METHODS
            x = allf.reshape(B * N, k, total)
            x16 = x.astype(jnp.float16).astype(jnp.float32)
            headdim = min(32, total)
            nheads = total // headdim
            qh = x16.reshape(B * N, k, nheads, headdim)
            scores = jnp.einsum('bihd,bjhd->bhij', qh, qh) / np.float32(np.sqrt(headdim))
            attn = jax.nn.softmax(scores, axis=-1)
            out = jnp.einsum('bhij,bjhd->bihd', attn, qh).reshape(B * N, k, total)
            fused = out @ W_lin.T + b_lin
            return fused.reshape(B, N, k, 64)

        def _instance_norm(x, axes):
            mu = x.mean(axis=axes, keepdims=True)
            var = x.var(axis=axes, keepdims=True)
            return (x - mu) / jnp.sqrt(var + 1e-05)

        def _lrelu(x):
            return jnp.where(x > 0, x, 0.2 * x)
        inds_sorted = _sorted_indices(coords.transpose(0, 2, 1))
        inds_list = [_window_inds(s) for s in inds_sorted]
        perm1 = jnp.array([2, 0, 3, 1])
        perm2 = jnp.array([1, 3, 0, 2])
        f0 = feats.transpose(0, 2, 1)
        g1 = _get_graph_features(f0, inds_list, perm1, W_lin1, b_lin1)
        h1 = jnp.einsum('oc,bnkc->bonk', W_conv1, g1)
        h1 = _lrelu(_instance_norm(h1, (2, 3)))
        feats1 = h1.max(axis=-1)
        g2 = _get_graph_features(feats1.transpose(0, 2, 1), inds_list, perm2, W_lin2, b_lin2)
        h2 = jnp.einsum('oc,bnkc->bonk', W_conv2, g2)
        h2 = _lrelu(_instance_norm(h2, (2, 3)))
        feats2 = h2.max(axis=-1)
        f3 = jnp.concatenate([feats, feats1, feats2], axis=1)
        h3 = jnp.einsum('oc,bcn->bon', W_conv3, f3)
        return _lrelu(_instance_norm(h3, (2,)))

    def _L0_attn_ref(x, bv_q, bv_k, bv_v):
        import jax, jax.numpy as jnp
        import numpy as np
        HDC_DIM = 512
        N_HEADS = 4
        HEAD_DIM = HDC_DIM // N_HEADS

        def _ste_sign(w):
            alpha = jnp.mean(jnp.abs(w), axis=-1, keepdims=True)
            hard = alpha * jnp.sign(w)
            hard = jnp.where(hard == 0, alpha, hard)
            return jax.lax.stop_gradient(hard - w) + w
        B, T, D = x.shape
        H, HD = (N_HEADS, HEAD_DIM)
        scale = HD ** (-0.5)
        q_bind = _ste_sign(bv_q)
        k_bind = _ste_sign(bv_k)
        v_bind = _ste_sign(bv_v)
        xh = x.reshape(B, T, H, HD)
        Q = xh * q_bind
        K = xh * k_bind
        V = xh * v_bind
        scores = jnp.einsum('bthd,bshd->bhts', Q, K) * scale
        causal = jnp.tril(jnp.ones((T, T), dtype=bool))
        attn = jnp.where(causal, jax.nn.sigmoid(scores * 4.0), 0.0)
        out = jnp.einsum('bhts,bshd->bthd', attn, V)
        return out.reshape(B, T, D)

    def _L0_ffn_ref(x, gate_w, base_w, base_b, lora_A, lora_B):
        import jax, jax.numpy as jnp
        import numpy as np
        B, S, D_IN, D_OUT = (2, 256, 512, 512)
        E, K, R = (8, 2, 16)
        SCALING = 32.0 / 16.0
        gate_logits = jnp.einsum('bsd,ed->bse', x, gate_w)
        weights, selected = jax.lax.top_k(gate_logits, K)
        weights = jax.nn.softmax(weights.astype(jnp.float32), axis=2).astype(x.dtype)
        result = jnp.einsum('bsd,od->bso', x, base_w) + base_b
        w_full = jnp.sum(jax.nn.one_hot(selected, E, dtype=x.dtype) * weights[..., None], axis=2)
        low = jnp.einsum('bsd,erd->ebsr', x, lora_A)
        lora_out = jnp.einsum('ebsr,eor,bse->bso', low, lora_B, w_full)
        result = result + SCALING * lora_out
        return result

    def _L1_xattn_ref(latents, context, Wq, Wk, Wv, Wo, q_norm_w, k_norm_w):
        import jax, jax.numpy as jnp
        import numpy as np
        HEADS = 32
        KV_HEADS = 8
        HEAD_DIM = 128
        EPS = 1e-06

        def rms_norm(x, w):
            var = jnp.mean(jnp.square(x.astype(jnp.float32)), axis=-1, keepdims=True)
            return (x.astype(jnp.float32) * jax.lax.rsqrt(var + EPS)).astype(x.dtype) * w
        bsz, q_len, hidden = latents.shape
        kv = jnp.concatenate([context, latents], axis=1)
        kv_len = kv.shape[1]
        groups = HEADS // KV_HEADS
        q = (latents @ Wq).reshape(bsz, q_len, HEADS, HEAD_DIM).transpose(0, 2, 1, 3)
        k = (kv @ Wk).reshape(bsz, kv_len, KV_HEADS, HEAD_DIM).transpose(0, 2, 1, 3)
        v = (kv @ Wv).reshape(bsz, kv_len, KV_HEADS, HEAD_DIM).transpose(0, 2, 1, 3)
        q = rms_norm(q, q_norm_w)
        k = rms_norm(k, k_norm_w)
        qg = q.reshape(bsz, KV_HEADS, groups, q_len, HEAD_DIM)
        scale = 1.0 / np.sqrt(HEAD_DIM)
        scores = jnp.einsum('bhgqd,bhkd->bhgqk', qg, k) * scale
        probs = jax.nn.softmax(scores.astype(jnp.float32), axis=-1).astype(q.dtype)
        out = jnp.einsum('bhgqk,bhkd->bhgqd', probs, v)
        out = out.reshape(bsz, HEADS, q_len, HEAD_DIM).transpose(0, 2, 1, 3)
        out = out.reshape(bsz, q_len, HEADS * HEAD_DIM)
        return out @ Wo

    def _L1_attn_ref(x, w_down, b_down, w_up, b_up, gate1, hy_in_w, hy_conv_w, hy_conv_b, hy_dt_bias, hy_A_log, hy_D, hy_fcD_w, hy_norm_w, hy_out_w):
        import jax, jax.numpy as jnp
        import numpy as np
        HID = 512
        DM = 128
        DIN = 2 * DM
        DST = 16
        HD = 64
        NH = DIN // HD
        DCONV = 7
        CONV_DIM = DIN + 2 * DST
        DIN_PROJ = 2 * DIN + 2 * DST + 2 * NH
        SEQ, BATCH = (256, 4)

        def _causal_conv(x, w, b):
            y = jax.lax.conv_general_dilated(jnp.transpose(x, (0, 2, 1)), w, (1,), [(DCONV - 1, 0)], feature_group_count=CONV_DIM, dimension_numbers=('NCH', 'OIH', 'NCH'))
            return jnp.transpose(y, (0, 2, 1)) + b

        def _ssm_scan(x, dt, A, B, C):
            dA = jnp.exp(dt * A)
            dBx = dt[..., None] * x

            def step(h, t):
                dA_t, dBx_t, B_t, C_t = t
                h = dA_t[:, :, None, None] * h + dBx_t[..., None] * B_t[:, None, None, :]
                y = jnp.einsum('bhpn,bn->bhp', h, C_t)
                return (h, y)
            h0 = jnp.zeros((x.shape[0], NH, HD, DST), x.dtype)
            _, ys = jax.lax.scan(step, h0, (jnp.moveaxis(dA, 1, 0), jnp.moveaxis(dBx, 1, 0), jnp.moveaxis(B, 1, 0), jnp.moveaxis(C, 1, 0)))
            return jnp.moveaxis(ys, 0, 1)

        def _hydra(u, in_w, conv_w, conv_b, dt_bias, A_log, D, fcD_w, norm_w, out_w):
            b, l, _ = u.shape
            zxbcdt = u @ in_w.T
            z = zxbcdt[..., :DIN]
            xBC = zxbcdt[..., DIN:DIN + CONV_DIM]
            dt2 = zxbcdt[..., DIN + CONV_DIM:]
            dt_fw = jax.nn.softplus(dt2[..., :NH] + dt_bias)
            dt_bw = jax.nn.softplus(jnp.flip(dt2[..., NH:], 1) + dt_bias)
            xBC = jax.nn.silu(_causal_conv(xBC, conv_w, conv_b))
            xs = xBC[..., :DIN]
            Bm = xBC[..., DIN:DIN + DST]
            Cm = xBC[..., DIN + DST:]
            A = -jnp.exp(A_log)
            x4 = xs.reshape(b, l, NH, HD)
            y_fw = _ssm_scan(x4, dt_fw, A, Bm, Cm).reshape(b, l, DIN)
            y_bw = jnp.flip(_ssm_scan(jnp.flip(x4, 1), dt_bw, A, jnp.flip(Bm, 1), jnp.flip(Cm, 1)).reshape(b, l, DIN), 1)
            zero = jnp.zeros((b, 1, DIN), u.dtype)
            y = jnp.concatenate([zero, y_fw[:, :-1]], 1) + jnp.concatenate([y_bw[:, 1:], zero], 1)
            y = y + xs * jnp.repeat(xs @ fcD_w.T + D, HD, axis=-1)
            yz = y * jax.nn.silu(z)
            y = yz * jax.lax.rsqrt(jnp.mean(jnp.square(yz), -1, keepdims=True) + 1e-05) * norm_w
            return y @ out_w.T
        x_init = x
        h = x @ w_down.T + b_down
        h = jnp.transpose(h, (1, 0, 2))
        h = jax.nn.gelu(h, approximate=False)
        xmid = h
        hp = (hy_in_w, hy_conv_w, hy_conv_b, hy_dt_bias, hy_A_log, hy_D, hy_fcD_w, hy_norm_w, hy_out_w)
        h = _hydra(h, *hp)
        h = _hydra(h, *hp)
        alpha = jax.nn.sigmoid(gate1)
        h = alpha * xmid + (1.0 - alpha) * h
        h = xmid + h
        h = h @ w_up.T + b_up
        return x_init + jnp.transpose(h, (1, 0, 2))

    def _L1_ffn_ref(x, weight, lora_A, lora_B, gw1, gb1, ln_gamma, ln_beta, gw2, gb2):
        import jax, jax.numpy as jnp
        import numpy as np
        B, S, IN, OUT = (4, 256, 512, 512)
        E, K, R = (8, 2, 16)
        CAP_FACTOR = 3.0
        ALPHA = 1.0 / R
        LN_EPS = 1e-05
        orig_shape = x.shape
        xf = x.reshape(-1, orig_shape[-1])
        N = xf.shape[0]
        capacity = int(CAP_FACTOR * N / E)
        h = xf @ gw1.T + gb1
        mu = jnp.mean(h, axis=-1, keepdims=True)
        var = jnp.mean((h - mu) ** 2, axis=-1, keepdims=True)
        h = (h - mu) * jax.lax.rsqrt(var + LN_EPS) * ln_gamma + ln_beta
        h = jax.nn.relu(h)
        gates = h @ gw2.T + gb2
        top_v, top_i = jax.lax.top_k(gates, K)
        top_g = jax.nn.softmax(top_v, axis=-1)
        onehot = (top_i[..., None] == jnp.arange(E)).astype(xf.dtype)
        counts = onehot.sum(axis=0)
        allowed = (counts <= capacity).astype(xf.dtype)
        w = jnp.einsum('nke,nk,ke->ne', onehot, top_g, allowed)
        main = xf @ weight.T
        tmp = jnp.einsum('ni,eir->enr', xf, lora_A)
        tmp = tmp * w.T[:, :, None]
        lora = jnp.einsum('enr,ero->no', tmp, lora_B) * ALPHA
        out = main + lora
        return out.reshape(*orig_shape[:-1], weight.shape[0])
    x = x + _L0_xattn_ref(ctx_4096, _layernorm(x, axis=-1), L0_xattn_W_lin1, L0_xattn_b_lin1, L0_xattn_W_lin2, L0_xattn_b_lin2, L0_xattn_W_conv1, L0_xattn_W_conv2, L0_xattn_W_conv3)
    x = x + _L0_attn_ref(_layernorm(x, axis=-1), L0_attn_bv_q, L0_attn_bv_k, L0_attn_bv_v)
    x = x + _L0_ffn_ref(_layernorm(x, axis=-1), L0_ffn_gate_w, L0_ffn_base_w, L0_ffn_base_b, L0_ffn_lora_A, L0_ffn_lora_B)
    x = x + _L1_xattn_ref(_layernorm(x, axis=-1), ctx_4096, L1_xattn_Wq, L1_xattn_Wk, L1_xattn_Wv, L1_xattn_Wo, L1_xattn_q_norm_w, L1_xattn_k_norm_w)
    x = x + _L1_attn_ref(_layernorm(x, axis=-1), L1_attn_w_down, L1_attn_b_down, L1_attn_w_up, L1_attn_b_up, L1_attn_gate1, L1_attn_hy_in_w, L1_attn_hy_conv_w, L1_attn_hy_conv_b, L1_attn_hy_dt_bias, L1_attn_hy_A_log, L1_attn_hy_D, L1_attn_hy_fcD_w, L1_attn_hy_norm_w, L1_attn_hy_out_w)
    x = x + _L1_ffn_ref(_layernorm(x, axis=-1), L1_ffn_weight, L1_ffn_lora_A, L1_ffn_lora_B, L1_ffn_gw1, L1_ffn_gb1, L1_ffn_ln_gamma, L1_ffn_ln_beta, L1_ffn_gw2, L1_ffn_gb2)
    return x

_drawn_inputs = setup_inputs


def setup_inputs(seed=0):
    import zlib

    import numpy as np

    out = dict(_drawn_inputs(seed))
    spreads = {'L0_xattn_b_lin1': (0.0, 2.0),
     'L0_xattn_b_lin2': (0.0, 2.0),
     'L1_xattn_q_norm_w': (1.0, 0.6),
     'L1_xattn_k_norm_w': (1.0, 0.6),
     'L1_attn_b_down': (0.0, 0.775),
     'L1_attn_b_up': (0.0, 0.1),
     'L1_attn_hy_conv_b': (0.0, 0.8),
     'L1_attn_hy_D': (1.0, 0.6),
     'L1_attn_hy_norm_w': (1.0, 0.6),
     'L1_ffn_gb1': (0.0, 0.8),
     'L1_ffn_ln_gamma': (1.0, 0.6),
     'L1_ffn_ln_beta': (0.0, 0.8),
     'L1_ffn_gb2': (0.0, 0.8)}
    factors = {'L0_attn_bv_q': 41.319,
     'L0_attn_bv_k': 40.932,
     'L0_ffn_base_b': 3.957,
     'L1_attn_hy_in_w': 8.0,
     'L1_attn_hy_conv_w': 8.0,
     'L1_attn_hy_dt_bias': 8.0,
     'L1_attn_hy_A_log': 8.0,
     'L1_attn_hy_fcD_w': 8.0,
     'L1_attn_hy_out_w': 8.0,
     'L1_ffn_lora_A': 8.0,
     'L1_ffn_lora_B': 8.0,
     'L1_ffn_gw1': 8.0,
     'L1_ffn_gw2': 8.0}
    for name, (base, spread) in spreads.items():
        noise = np.random.default_rng([zlib.crc32(name.encode()), seed]).standard_normal(out[name].shape)
        drawn = base * np.exp(spread * noise) if base else spread * noise
        out[name] = jnp.asarray(drawn.astype(out[name].dtype))
    for name, factor in factors.items():
        out[name] = (out[name] * factor).astype(out[name].dtype)
    return out
```

```python
from contextlib import ExitStack

import numpy as np

import concourse.bass as bass
from concourse import mybir

F32 = mybir.dt.float32
F16 = mybir.dt.float16
BF16 = mybir.dt.bfloat16
I32 = mybir.dt.int32
U32 = mybir.dt.uint32
ALU = mybir.AluOpType
ACT = mybir.ActivationFunctionType
AX = mybir.AxisListType

P = 128
LAT, TOK, DIM = 16, 32, 512
ROWS = LAT * TOK
NT = ROWS // P
NCH = DIM // P
LN_EPS = 1e-5

BITS = 10
METHODS = 4
KNN = 10
C_IN = 32
HEADS = 4
HD = 32
U_ALL = 43
BATCH_U = (16, 16, 11)
U_MAX = 16
BLK = 3 * KNN
F_LEFT = KNN // 2
F_COLS = F_LEFT + DIM + 8
TAIL = KNN // 2 - 1
HEAD_POINTS = KNN // 2
EXTRA = TAIL + HEAD_POINTS * KNN
BIG = float(2 ** 20)
OUTS = (32, 64)
INV_SQRT_HD = float(1.0 / np.sqrt(np.float32(HD)))


def chain(eng, sem):
    count = [0]

    def link(ins):
        count[0] += 1
        ins.then_inc(sem, 1)
        eng.wait_ge(sem, count[0])
    return link


def named(items):
    return type("Named", (), {"all": items, **items})


def semaphores(nc, stack, stage, names):
    return named({n: stack.enter_context(nc.semaphore(f"{stage}_{n}")) for n in names.split()})


def tensors(nc, stack, stage, specs):
    return {n: stack.enter_context(nc.sbuf_tensor(f"{stage}_{n}", shape, dt)) for n, shape, dt in specs}


def release(nc, s):
    for sem in s.all.values():
        nc.sync.sem_clear(sem)
    nc.all_engine_barrier()


def custom(ap, offset, dims):
    return bass.AP(ap.tensor, ap.offset + offset, [list(ap.ap[0])] + dims)


def load_constants(nc, g, d):
    with ExitStack() as st:
        s = semaphores(nc, st, "const", "loaded step")
        tgt_f = st.enter_context(nc.sbuf_tensor("tgt_f", [P, DIM + EXTRA], F32))
        msk_f = st.enter_context(nc.sbuf_tensor("msk_f", [P, HD], F32))
        with nc.Block() as block:
            @block.sync
            def _(sp):
                sp.dma_start(g.ident[:, :], d.ident).then_inc(s.loaded, 16)
                sp.dma_start(tgt_f[:, :], d.targets.partition_broadcast(P)).then_inc(s.loaded, 16)
                sp.dma_start(msk_f[:, :], d.pointmask).then_inc(s.loaded, 16)
                sp.dma_start(g.avg1[:, :], d.avg1).then_inc(s.loaded, 16)
                sp.dma_start(g.avg2[:, :], d.avg2).then_inc(s.loaded, 16)
                for t in range(NT):
                    sp.dma_start(g.x[:, t, :], d.x[t * P:(t + 1) * P, :]).then_inc(s.loaded, 16)

            @block.vector
            def _(dve):
                dve.memset(g.eps[:, :], LN_EPS).then_inc(s.step, 1)
                dve.wait_ge(s.loaded, 16 * (5 + NT))
                dve.tensor_copy(g.identb[:, :], g.ident[:, :]).then_inc(s.step, 1)
                dve.tensor_copy(g.targets[:, :], tgt_f[:, :]).then_inc(s.step, 1)
                dve.tensor_copy(g.mask[:, :, :],
                                msk_f[:, None, :].broadcast_to([P, U_MAX, HD])).then_inc(s.step, 1)
        release(nc, s)


def layernorm_and_turn(nc, g, name):
    with ExitStack() as st:
        s = semaphores(nc, st, name, "step var root rstd normed turned copied")
        stats = st.enter_context(nc.sbuf_tensor(f"{name}_stats", [P, NT, 6], F32))
        mv = st.enter_context(nc.sbuf_tensor(f"{name}_mv", [P, NT, 2], F32))
        root = st.enter_context(nc.sbuf_tensor(f"{name}_root", [P, NT], F32))
        rstd = st.enter_context(nc.sbuf_tensor(f"{name}_rstd", [P, NT], F32))
        with nc.Block() as block:
            @block.vector
            def _(dve):
                for t in range(NT):
                    dve.bn_stats(stats[:, t, :], g.x[:, t, :]).then_inc(s.step, 1)
                for t in range(NT):
                    dve.wait_ge(s.step, t + 1)
                    dve.bn_aggr(mv[:, t, :], stats[:, t, :]).then_inc(s.var, 1)
                dve.wait_ge(s.root, 1)
                dve.wait_ge(s.var, NT)
                dve.reciprocal(rstd[:, :], root[:, :]).then_inc(s.rstd, 1)
                dve.wait_ge(s.rstd, 1)
                for t in range(NT):
                    dve.tensor_scalar(g.xn[:, t, :], g.x[:, t, :], mv[:, t, 0:1], rstd[:, t:t + 1],
                                      ALU.subtract, ALU.mult).then_inc(s.normed, 1)

            @block.scalar
            def _(act):
                act.wait_ge(s.var, NT)
                act.activation(root[:, :], mv[:, :, 1], ACT.Sqrt, bias=g.eps[:, 0:1]).then_inc(s.root, 1)
                for t in range(NT):
                    act.wait_ge(s.turned, t + 1)
                    act.copy(g.xnT[:, :, t * P:(t + 1) * P],
                             g.ps[:, t, :].rearrange("p (c r) -> p c r", c=NCH)).then_inc(s.copied, 1)

            @block.tensor
            def _(pe):
                for t in range(NT):
                    pe.wait_ge(s.normed, t + 1)
                    for c in range(NCH):
                        ins = pe.transpose(g.ps[:, t, c * P:(c + 1) * P], g.xn[:, t, c * P:(c + 1) * P],
                                           g.ident[:, :])
                    ins.then_inc(s.turned, 1)
        release(nc, s)


def curve_keys(nc, g, d):
    B, N8, NC8 = LAT, 8, DIM // 8
    with ExitStack() as st:
        def sb(name, shape, dt):
            return st.enter_context(nc.sbuf_tensor(name, shape, dt))
        s = semaphores(nc, st, "keys", "loaded step stored quantised reloaded keyed written back turned")
        co = sb("co", [B, 3, DIM], F32)
        lo = sb("c_lo", [B, 3], F32)
        hi = sb("c_hi", [B, 3], F32)
        w = sb("c_w", [B, 12, 3], F32)
        fl = sb("c_fl", [B, 3, DIM], F32)
        gt = sb("c_gt", [B, 3, DIM], F32)
        qi = sb("c_qi", [B, 3, DIM], I32)
        q = sb("q8", [P, 3, NC8], I32)
        nidx = sb("nidx", [P, NC8], I32)
        X = sb("hX", [P, 3, METHODS, NC8], I32)
        M = sb("hM", [P, 2, NC8], I32)
        N = sb("hN", [P, 2, NC8], I32)
        T = sb("hT", [P, 2, NC8], I32)
        S = sb("hS", [P, 3, METHODS, NC8], I32)
        K = sb("hK", [P, METHODS, NC8], I32)
        KH = sb("hKH", [P, METHODS, NC8], I32)
        KL = sb("hKL", [P, METHODS, NC8], I32)
        FH = sb("fH", [P, METHODS, NC8], F32)
        FL = sb("fL", [P, METHODS, NC8], F32)
        rows = sb("krows", [LAT * METHODS, 2, DIM], F32)
        with nc.Block() as block:
            @block.sync
            def _(sp):
                sp.dma_start(co[:, :, :], d.coords).then_inc(s.loaded, 16)
                sp.dma_start(nidx[:, :], d.nidx).then_inc(s.loaded, 16)
                sp.wait_ge(s.quantised, 1)
                sp.dma_start(d.q_scratch, qi[:, :, :]).then_inc(s.stored, 16)
                sp.wait_ge(s.stored, 16)
                for b in range(B):
                    sp.dma_start(q[b * N8:(b + 1) * N8, :, :],
                                 d.q_scratch[b].rearrange("c (a n) -> a c n", a=N8)).then_inc(s.reloaded, 16)
                sp.wait_ge(s.keyed, 1)
                for b in range(B):
                    sp.dma_start(d.keys_hi[b].rearrange("m (a n) -> a m n", a=N8),
                                 FH[b * N8:(b + 1) * N8, :, :]).then_inc(s.written, 16)
                    sp.dma_start(d.keys_lo[b].rearrange("m (a n) -> a m n", a=N8),
                                 FL[b * N8:(b + 1) * N8, :, :]).then_inc(s.written, 16)
                sp.wait_ge(s.written, 32 * B)
                sp.dma_start(rows[:, 0, :], d.keys_hi.rearrange("b m n -> (b m) n")).then_inc(s.back, 16)
                sp.dma_start(rows[:, 1, :], d.keys_lo.rearrange("b m n -> (b m) n")).then_inc(s.back, 16)

            @block.vector
            def _(dve):
                link = chain(dve, s.step)
                dve.wait_ge(s.loaded, 32)
                link(dve.tensor_reduce(lo[:, :], co[:, :, :], AX.X, ALU.min))
                link(dve.tensor_reduce(hi[:, :], co[:, :, :], AX.X, ALU.max))
                den, r, q0, qh, ql, dh, dl, e = (w[:, i, :] for i in range(8))
                link(dve.tensor_tensor(hi[:, :], hi[:, :], lo[:, :], ALU.subtract))
                link(dve.tensor_scalar(den, hi[:, :], 1e-6, None, ALU.add))
                link(dve.reciprocal(r, den))
                link(dve.tensor_scalar(q0, r, float(2 ** BITS - 1), None, ALU.mult))
                for whole, high, low in ((q0, qh, ql), (den, dh, dl)):
                    link(dve.tensor_scalar(high.bitcast(I32), whole.bitcast(I32), -4096, None,
                                           ALU.bitwise_and))
                    link(dve.tensor_tensor(low, whole, high, ALU.subtract))
                link(dve.tensor_tensor(e, qh, dh, ALU.mult))
                link(dve.tensor_scalar(e, e, -1.0, float(2 ** BITS - 1), ALU.mult, ALU.add))
                for a, b in ((qh, dl), (ql, dh), (ql, dl)):
                    link(dve.tensor_tensor(w[:, 8, :], a, b, ALU.mult))
                    link(dve.tensor_tensor(e, e, w[:, 8, :], ALU.subtract))
                link(dve.tensor_tensor(e, e, r, ALU.mult))
                link(dve.tensor_tensor(q0, q0, e, ALU.add))
                for c in range(3):
                    link(dve.tensor_scalar(co[:, c, :], co[:, c, :], lo[:, c:c + 1], w[:, 2, c:c + 1],
                                           ALU.subtract, ALU.mult))
                link(dve.tensor_copy(qi[:, :, :], co[:, :, :]))
                link(dve.tensor_copy(fl[:, :, :], qi[:, :, :]))
                link(dve.tensor_tensor(gt[:, :, :], fl[:, :, :], co[:, :, :], ALU.is_gt))
                link(dve.tensor_tensor(fl[:, :, :], fl[:, :, :], gt[:, :, :], ALU.subtract))
                link(dve.tensor_scalar(fl[:, :, :], fl[:, :, :], 0.0, float(2 ** BITS - 1), ALU.max, ALU.min))
                dve.tensor_copy(qi[:, :, :], fl[:, :, :]).then_inc(s.quantised, 1)
                dve.wait_ge(s.reloaded, 16 * B)
                for m in range(METHODS):
                    for c in range(3):
                        link(dve.tensor_copy(X[:, c, m, :], q[:, (1 - c if m % 2 and c < 2 else c), :]))
                H = [X[:, c, 2:4, :] for c in range(3)]

                def sign_of_bit(src, bit):
                    link(dve.tensor_scalar(M[:, :, :], src, 31 - bit, 31, ALU.logical_shift_left,
                                           ALU.arith_shift_right))

                for bit in range(BITS - 1, 0, -1):
                    low = (1 << bit) - 1
                    sign_of_bit(H[0], bit)
                    link(dve.scalar_tensor_tensor(H[0], M[:, :, :], low, H[0], ALU.bitwise_and, ALU.bitwise_xor))
                    for c in (1, 2):
                        sign_of_bit(H[c], bit)
                        link(dve.tensor_scalar(N[:, :, :], M[:, :, :], -1, low, ALU.bitwise_xor, ALU.bitwise_and))
                        link(dve.tensor_tensor(T[:, :, :], H[0], H[c], ALU.bitwise_xor))
                        link(dve.tensor_tensor(T[:, :, :], T[:, :, :], N[:, :, :], ALU.bitwise_and))
                        link(dve.scalar_tensor_tensor(M[:, :, :], M[:, :, :], low, H[0], ALU.bitwise_and,
                                                      ALU.bitwise_xor))
                        link(dve.tensor_tensor(H[0], M[:, :, :], T[:, :, :], ALU.bitwise_xor))
                        link(dve.tensor_tensor(H[c], H[c], T[:, :, :], ALU.bitwise_xor))
                link(dve.tensor_tensor(H[1], H[1], H[0], ALU.bitwise_xor))
                link(dve.tensor_tensor(H[2], H[2], H[1], ALU.bitwise_xor))
                link(dve.memset(T[:, :, :], 0))
                for bit in range(BITS - 1, 0, -1):
                    sign_of_bit(H[2], bit)
                    link(dve.scalar_tensor_tensor(T[:, :, :], M[:, :, :], (1 << bit) - 1, T[:, :, :],
                                                  ALU.bitwise_and, ALU.bitwise_xor))
                for c in range(3):
                    link(dve.tensor_tensor(H[c], H[c], T[:, :, :], ALU.bitwise_xor))
                for shift, keep in ((16, 0x030000FF), (8, 0x0300F00F), (4, 0x030C30C3), (2, 0x09249249)):
                    link(dve.scalar_tensor_tensor(S[:, :, :, :], X[:, :, :, :], shift, X[:, :, :, :],
                                                  ALU.logical_shift_left, ALU.bitwise_or))
                    link(dve.tensor_scalar(X[:, :, :, :], S[:, :, :, :], keep, None, ALU.bitwise_and))
                link(dve.scalar_tensor_tensor(K[:, :, :], X[:, 0, :, :], 1, X[:, 1, :, :],
                                              ALU.logical_shift_left, ALU.bitwise_or))
                link(dve.scalar_tensor_tensor(K[:, :, :], K[:, :, :], 1, X[:, 2, :, :],
                                              ALU.logical_shift_left, ALU.bitwise_or))
                link(dve.tensor_scalar(KH[:, :, :], K[:, :, :], 15, None, ALU.logical_shift_right))
                link(dve.tensor_scalar(KL[:, :, :], K[:, :, :], 32767, 9, ALU.bitwise_and,
                                       ALU.logical_shift_left))
                link(dve.tensor_tensor(KL[:, :, :], KL[:, :, :],
                                       nidx[:, None, :].broadcast_to([P, METHODS, NC8]), ALU.bitwise_or))
                link(dve.tensor_scalar(FH[:, :, :], KH[:, :, :], float(2 ** 24), None, ALU.mult))
                dve.tensor_scalar(FL[:, :, :], KL[:, :, :], -1.0, None, ALU.mult).then_inc(s.keyed, 1)

            @block.tensor
            def _(pe):
                pe.wait_ge(s.back, 32)
                n = LAT * METHODS
                for half in range(2):
                    for c in range(NCH):
                        ins = pe.transpose(g.ps[:, half, c * n:(c + 1) * n], rows[:, half, c * P:(c + 1) * P],
                                           g.ident[0:n, 0:n])
                ins.then_inc(s.turned, 1)

            @block.scalar
            def _(act):
                n = LAT * METHODS
                act.wait_ge(s.turned, 1)
                act.copy(g.key_hi[:, :, :], g.ps[:, 0, 0:NCH * n].rearrange("p (c n) -> p c n", c=NCH))
                act.mul(g.key_lo[:, :, :], g.ps[:, 1, 0:NCH * n].rearrange("p (c n) -> p c n", c=NCH), -1.0)
        release(nc, s)


def graph_weights(nc, g, d, w):
    with ExitStack() as st:
        s = semaphores(nc, st, "gw", "loaded step zeroed multiplied split")
        lin = [w.e[0:64, 256 * l:256 * (l + 1)].rearrange("p (a n) -> p a n", a=2) for l in range(2)]
        conv = [w.e[0:64, 512 + P * l:512 + P * (l + 1)] for l in range(2)]
        bias = [w.e[0:64, 768 + l:769 + l] for l in range(2)]
        wf = [w.eT[:, 256 * l:256 * l + HEADS * OUTS[l]].rearrange("p (h o) -> p h o", h=HEADS) for l in range(2)]
        cf = [w.eT[:, 512 * (l + 1):512 * (l + 2)].rearrange("p (c o) -> p c o", c=4) for l in range(2)]
        with nc.Block() as block:
            @block.sync
            def _(sp):
                for l in range(2):
                    sp.dma_start(lin[l], d.all[f"lin{l}"]).then_inc(s.loaded, 16)
                    sp.dma_start(conv[l], d.all[f"conv{l}"]).then_inc(s.loaded, 16)
                    sp.dma_start(bias[l], d.all[f"lbias{l}"]).then_inc(s.loaded, 16)
                sp.dma_start(w.w3a[:, :], d.w3a).then_inc(s.loaded, 16)
                sp.dma_start(w.w3b[:, :], d.w3b).then_inc(s.loaded, 16)
                sp.dma_start(w.w3c[:, :, :], d.w3c).then_inc(s.loaded, 16)

            @block.gpsimd
            def _(pool):
                for t in (wf[0], wf[1], cf[0], cf[1], w.spread, w.x16, w.sorted, w.centre[0], w.centre[1],
                          w.centre16, w.cenx, w.vals[0], w.vals[1]):
                    pool.memset(flat(t), 0.0).then_inc(s.zeroed, 1)

            @block.tensor
            def _(pe):
                pe.wait_ge(s.loaded, 16 * 9)
                for l in range(2):
                    for half in range(2):
                        pe.matmul(g.ps[:, 2 * l + half, 0:OUTS[l]], lin[l][:, half, :], conv[l][:, 0:OUTS[l]],
                                  start=True, stop=True)
                    ins = pe.matmul(g.ps[:, 4 + l, 0:1], conv[l], bias[l], start=True, stop=True)
                ins.then_inc(s.multiplied, 1)

            @block.vector
            def _(dve):
                link = chain(dve, s.step)
                dve.wait_ge(s.multiplied, 1)
                dve.wait_ge(s.zeroed, 13)
                for l in range(2):
                    o = OUTS[l]
                    link(dve.tensor_copy(w.bias[:, l:l + 1], g.ps[:, 4 + l, 0:1]))
                    for h in range(HEADS):
                        rows = slice(HD * h, HD * (h + 1))
                        link(dve.tensor_copy(wf[l][rows, h, :], g.ps[rows, 2 * l + 1, 0:o]))
                        at = (h * o) % P
                        link(dve.tensor_copy(cf[l][:, h, at:at + o], g.ps[:, 2 * l, 0:o]))
                    for whole, parts in ((flat(wf[l]), w.wnei[l]), (flat(cf[l]), w.wcen[l])):
                        for p in range(3):
                            link(dve.tensor_copy(flat(parts[:, p]), whole))
                            if p < 2:
                                link(dve.tensor_tensor(whole, whole, flat(parts[:, p]), ALU.subtract))
        release(nc, s)


def flat(t):
    ap = t if isinstance(t, bass.AP) else t[tuple([slice(None)] * len(t.shape))]
    names = "abcdef"[:len(ap.shape) - 1]
    return ap if len(names) == 1 else ap.rearrange(f"p {' '.join(names)} -> p ({' '.join(names)})")


def graph_layers(nc, g, d):
    with ExitStack() as st:
        w = named(tensors(nc, st, "a", (
                ("w3a", [P, 32], F32), ("w3b", [P, 32], F32), ("w3c", [P, 2, 32], F32), ("bias", [P, 2], F32),
                ("spread", [P, 3, NCH, METHODS, P], BF16),
                ("x16", [P, 2, U_MAX, 4, HD], F16),
                ("sorted", [P, F_COLS], F32),
                ("first", [P, HEAD_POINTS, KNN], F32),
                ("centre16", [P, DIM + 8], F16), ("cenx", [P, 4, U_MAX, HD], F16),
                ("perm", [P, METHODS, NCH, DIM + EXTRA], BF16),
                ("key_b", [P, 2, NCH, METHODS], F32), ("less", [P, 2, DIM], BF16),
                ("rank", [P, METHODS * NCH], F32),
                ("fn", [P, NCH, C_IN], F32), ("rest", [P, NCH, C_IN], F32), ("parts", [P, 3, NCH, C_IN], BF16),
                ("e", [P, HEADS * U_MAX * HD], F32), ("eT", [P, HEADS * U_MAX * HD], F32),
                ("rmax", [P, HEADS * U_MAX], F32), ("rsum", [P, HEADS * U_MAX], F32),
                ("stats", [P, 2, 4, 6], F32), ("mv", [P, 2, 2], F32), ("mean", [P, 1], F32), ("meanb", [P, 1], F32),
                ("dev", [P, 2, 2], F32), ("root", [P, 1], F32), ("rstd", [P, 1], F32),
                ("peak", [P, 2, 3 * (U_ALL + 1)], F32), ("f", [P, 2, P], F32),
                ("st3", [32, 6], F32), ("mv3", [32, 2], F32), ("r3", [32, 2], F32))))
        w.centre = [st.enter_context(nc.sbuf_tensor(f"a_centre{l}", [P, DIM + 8], F32)) for l in range(2)]
        w.wnei = [st.enter_context(nc.sbuf_tensor(f"a_wnei{l}", [P, 3, HEADS * OUTS[l]], BF16)) for l in range(2)]
        w.wcen = [st.enter_context(nc.sbuf_tensor(f"a_wcen{l}", [P, 3, 4, P], BF16)) for l in range(2)]
        w.vals = [st.enter_context(nc.sbuf_tensor(f"a_vals{l}", [P, U_MAX, HEADS, 4 * OUTS[l]], F32))
                  for l in range(2)]
        w.row_hi = w.e[:, :].rearrange("p (m n) -> p m n", m=METHODS)
        w.row_lo = w.eT[:, :].rearrange("p (m n) -> p m n", m=METHODS)
        w.o32 = w.e[0:32, 0:2 * DIM].rearrange("p (a n) -> p a n", a=2)
        w.above = g.xn
        graph_weights(nc, g, d, w)
        s = semaphores(nc, st, "graph", "rows keyb above ranked dstep pstep perm parts spread gathered sorted x16 cenx "
                 "scored shifted exped attn projected vals mixed stats moments mean dev var root turned f2 "
                 "convolved root3 out stored")
        with nc.Fori(0, LAT) as b:
            graph_batch(nc, g, d, w, s, b)


def per_bank(l):
    return 512 // (HEADS * OUTS[l])


def value_groups():
    out = []
    for q in range(6):
        l, nu = q // 3, BATCH_U[q % 3]
        out += [(q, u, min(per_bank(l), nu - u)) for u in range(0, nu, per_bank(l))]
    return out


def graph_batch(nc, g, d, w, s, b):
    groups = value_groups()
    upto = [sum(x[0] < q for x in groups) for q in range(7)]
    first_u = [sum(BATCH_U[:q % 3]) for q in range(6)]

    with nc.Block() as block:
        @block.sync
        def _(sp):
            sp.dma_start(w.row_hi[:, :, :], bcast_rows(d.keys_hi, b)).then_inc(s.rows, 16)
            sp.dma_start(w.row_lo[:, :, :], bcast_rows(d.keys_lo, b)).then_inc(s.rows, 16)
            sp.wait_ge(s.out, 1)
            sp.dma_start(d.xatt[bass.ds(b * 32, 32), :], w.o32[:, 1, :]).then_inc(s.stored, 16)
            sp.wait_ge(s.stored, 16)

        @block.gpsimd
        def _(pool):
            link = chain(pool, s.pstep)
            pool.wait_ge(s.rows, 32)
            pool.wait_ge(s.keyb, 2)
            for m in range(METHODS):
                for c in range(NCH):
                    i = m * NCH + c
                    if i >= 4:
                        pool.wait_ge(s.ranked, i - 3)
                    pool.tensor_scalar(w.above[:, i % 4, :], w.row_hi[:, m, :], w.key_b[:, 0, c, m:m + 1], None,
                                       ALU.subtract).then_inc(s.above, 1)
            for l in range(2):
                pool.wait_ge(s.parts, l + 1)
                for p in range(3):
                    for m in range(METHODS):
                        dst = custom(w.spread[:, p], m * P + m * 8, [[METHODS * P, NCH], [32, HEADS], [1, 8]])
                        src = custom(w.parts[:, p], 0, [[C_IN, NCH], [8, HEADS], [1, 8]])
                        ins = pool.tensor_copy(dst, src)
                ins.then_inc(s.spread, 1)
                for k in range(3):
                    q = 3 * l + k
                    nu, at = BATCH_U[k], 3 * first_u[q]
                    if k == 0:
                        pool.wait_ge(s.sorted, l + 1)
                    if q >= 2:
                        pool.wait_ge(s.projected, upto[q - 1])
                    for c in range(4):
                        ins = pool.tensor_tensor(
                            custom(w.x16[:, q % 2], HD * c, [[4 * HD, nu], [KNN, 3], [1, KNN]]),
                            custom(w.sorted[:, :], P * c + at, [[3, nu], [1, 3], [1, KNN]]),
                            custom(w.centre[l][:, :], P * c + at, [[3, nu], [1, 3], [0, KNN]]), ALU.subtract)
                    if k == 0:
                        link(ins)
                        for u, n in ((0, 3), (1, HEAD_POINTS - 3)):
                            ins = pool.tensor_tensor(
                                custom(w.x16[:, q % 2], 4 * HD * u, [[KNN, n], [1, KNN]]),
                                w.first[:, 3 * u:3 * u + n, :],
                                custom(w.centre[l][:, :], 3 * u, [[1, n], [0, KNN]]), ALU.subtract)
                    ins.then_inc(s.x16, 1)
                    if q >= 1:
                        pool.wait_ge(s.mixed, q)
                    for c in range(4):
                        ins = pool.tensor_copy(
                            custom(w.cenx[:, c], 0, [[HD, nu], [KNN, 3], [1, KNN]]),
                            custom(w.centre16[:, :], P * c + at, [[3, nu], [1, 3], [0, KNN]]))
                    ins.then_inc(s.cenx, 1)

        @block.scalar
        def _(act):
            gi = 0
            for l in range(2):
                act.wait_ge(s.gathered, l + 1)
                act.copy(w.sorted[:, F_LEFT:F_LEFT + DIM], g.ps[:, 4, :])
                act.copy(w.sorted[:, F_LEFT + DIM:F_LEFT + DIM + TAIL], g.ps[:, 5, 0:TAIL])
                act.copy(flat(w.first), g.ps[:, 5, TAIL:EXTRA])
                act.copy(w.centre16[:, 0:DIM], g.ps[:, 6, :])
                act.copy(w.centre[l][:, 0:DIM], g.ps[:, 6, :]).then_inc(s.sorted, 1)
                for k in range(3):
                    q = 3 * l + k
                    n = HEADS * BATCH_U[k] * HD
                    act.wait_ge(s.shifted, q + 1)
                    act.activation(w.e[:, 0:n], w.e[:, 0:n], ACT.Exp, scale=INV_SQRT_HD).then_inc(s.exped, 1)
                    o = OUTS[l]
                    for _, u, nu in [x for x in groups if x[0] == q]:
                        act.wait_ge(s.projected, gi + 1)
                        if u == 0 and q >= 1:
                            act.wait_ge(s.mixed, q)
                        for c in range(4):
                            rows = slice(HD * c, HD * (c + 1))
                            ins = act.copy(w.vals[l][rows, u:u + nu, :, c * o:(c + 1) * o]
                                           .rearrange("p u h o -> p (u h) o"),
                                           g.ps[rows, 4 + gi % 2, 0:nu * HEADS * o]
                                           .rearrange("p (x o) -> p x o", o=o))
                        ins.then_inc(s.vals, 1)
                        gi += 1
                act.wait_ge(s.var, l + 1)
                act.activation(w.root[:, :], g.ps[:, 5, 1:2], ACT.Sqrt, bias=g.eps[:, 0:1]).then_inc(s.root, 1)
            act.wait_ge(s.moments, 3)
            act.activation(w.r3[:, 0:1], w.mv3[:, 1:2], ACT.Sqrt, bias=g.eps[0:32, 0:1]).then_inc(s.root3, 1)

        @block.tensor
        def _(pe):
            gi = [0]

            def gather(l):
                pe.wait_ge(s.spread, l + 1)
                if l == 0:
                    pe.wait_ge(s.perm, METHODS * NCH)
                else:
                    pe.wait_ge(s.vals, upto[3])
                    pe.wait_ge(s.f2, 1)
                steps = [(p, m, c) for p in range(3) for m in range(METHODS) for c in range(NCH)]
                for i, (p, m, c) in enumerate(steps):
                    for bank, a, n in ((4, 0, DIM), (5, DIM, EXTRA)):
                        pe.matmul(g.ps[:, bank, 0:n], w.spread[:, p, c, m, :], w.perm[:, m, c, a:a + n],
                                  start=(i == 0), stop=(i == len(steps) - 1))
                steps = [(p, m) for p in range(3) for m in range(METHODS)]
                for c in range(NCH):
                    for i, (p, m) in enumerate(steps):
                        ins = pe.matmul(g.ps[:, 6, c * P:(c + 1) * P], w.spread[:, p, c, m, :], g.identb[:, :],
                                        start=(i == 0), stop=(i == len(steps) - 1))
                ins.then_inc(s.gathered, 1)

            def scores(q):
                nu = BATCH_U[q % 3]
                pe.wait_ge(s.x16, q + 1)
                if q >= 1:
                    pe.wait_ge(s.shifted, q)
                for h in range(HEADS):
                    pe.matmul(g.ps[:, h, 0:nu * HD], g.identb[:, :], flat(g.mask[:, 0:nu, :]),
                              start=True, stop=False, skip_group_check=True)
                for u in range(nu):
                    for c in range(4):
                        for h in range(HEADS):
                            x = w.x16[HD * h:HD * (h + 1), q % 2, u, c, :]
                            ins = pe.matmul(g.ps[HD * c:HD * (c + 1), h, HD * u:HD * (u + 1)], x, x,
                                            start=False, stop=(u == nu - 1), skip_group_check=True)
                ins.then_inc(s.scored, 1)

            def values(q):
                l = q // 3
                n = HEADS * OUTS[l]
                for _, u0, nu in [x for x in groups if x[0] == q]:
                    if gi[0] >= 2:
                        pe.wait_ge(s.vals, gi[0] - 1)
                    if u0 == 0:
                        pe.wait_ge(s.sorted, l + 1)
                    for u in range(u0, u0 + nu):
                        lhs = flat(w.x16[:, q % 2, u])
                        for p in range(3):
                            ins = pe.matmul(g.ps[:, 4 + gi[0] % 2, (u - u0) * n:(u - u0 + 1) * n], lhs,
                                            w.wnei[l][:, p, :], start=(p == 0), stop=(p == 2))
                    ins.then_inc(s.projected, 1)
                    gi[0] += 1

            def mix(q):
                l, nu = q // 3, BATCH_U[q % 3]
                pe.wait_ge(s.cenx, q + 1)
                pe.wait_ge(s.attn, q + 1)
                pe.wait_ge(s.vals, upto[q + 1])
                if q % 3 == 0:
                    pe.wait_ge(s.sorted, l + 1)
                if q >= 1:
                    pe.wait_ge(s.stats, q)
                eT = w.eT[:, 0:HEADS * nu * HD].rearrange("p (h u i) -> p h u i", h=HEADS, u=nu)
                for half in range(l + 1):
                    quads = range(4) if l == 0 else (2 * half, 2 * half + 1)
                    out = g.ps[:, 6 + half, :]
                    steps = [(p, c) for p in range(3) for c in quads]
                    for i, (p, c) in enumerate(steps):
                        pe.matmul(out[:, 0:nu * HD], w.wcen[l][:, p, c, :], flat(w.cenx[:, c, 0:nu, :]),
                                  start=(i == 0), stop=False, skip_group_check=True)
                    for u in range(nu):
                        for h in range(HEADS):
                            ins = pe.matmul(out[:, u * HD:(u + 1) * HD], w.vals[l][:, u, h, P * half:P * (half + 1)],
                                            eT[:, h, u, :], start=False, stop=(u == nu - 1 and h == HEADS - 1),
                                            skip_group_check=True)
                ins.then_inc(s.mixed, 1)

            def average(l, src, col, sem):
                avg = g.avg2 if l else g.avg1
                for half in range(l + 1):
                    ins = pe.matmul(g.ps[:, 5, col:col + 1], avg[:, :], src(half), start=(half == 0), stop=(half == l))
                ins.then_inc(sem, 1)

            for l in range(2):
                gather(l)
                q = 3 * l
                scores(q)
                values(q)
                scores(q + 1)
                mix(q)
                values(q + 1)
                scores(q + 2)
                mix(q + 1)
                values(q + 2)
                mix(q + 2)
                pe.wait_ge(s.moments, l + 1)
                pe.wait_ge(s.vals, upto[q + 3])
                average(l, lambda half: w.mv[:, half, 0:1], 0, s.mean)
                pe.wait_ge(s.dev, l + 1)
                average(l, lambda half: w.dev[:, half, 1:2], 1, s.var)
                if l == 0:
                    pe.wait_ge(s.turned, 1)
                    pe.transpose(g.ps[:, 7, 0:P], w.f[:, 0, :], g.ident[:, :]).then_inc(s.turned, 1)
            pe.wait_ge(s.turned, 3)
            out = g.ps[0:32, 4, :]
            pe.matmul(out, w.w3a[:, :], w.centre[0][:, 0:DIM], start=True, stop=False, skip_group_check=True)
            pe.matmul(out, w.w3b[:, :], w.centre[1][:, 0:DIM], start=False, stop=False, skip_group_check=True)
            for half in range(2):
                for c in range(2):
                    at = P * (2 * half + c)
                    ins = pe.matmul(out[:, at:at + P], w.w3c[:, c, :], w.f[:, half, :], start=False,
                                    stop=(half == 1 and c == 1), skip_group_check=True)
            ins.then_inc(s.convolved, 1)

        @block.vector
        def _(dve):
            link = chain(dve, s.dstep)
            for i, key in enumerate((g.key_hi, g.key_lo)):
                dve.tensor_copy(w.key_b[:, i, :, :], key[:, :, bass.ds(b * METHODS, METHODS)]).then_inc(s.keyb, 1)
            link(dve.tensor_copy(w.fn[:, :, :], g.xnT[:, :, bass.ds(b * C_IN, C_IN)]))

            def split():
                src = w.fn
                for p in range(3):
                    ins = dve.tensor_copy(flat(w.parts[:, p]), flat(src))
                    if p == 2:
                        ins.then_inc(s.parts, 1)
                        return
                    link(ins)
                    link(dve.tensor_tensor(flat(w.rest), flat(src), flat(w.parts[:, p]), ALU.subtract))
                    src = w.rest

            split()
            dve.wait_ge(s.keyb, 2)
            dve.wait_ge(s.rows, 32)
            for m in range(METHODS):
                for c in range(NCH):
                    i = m * NCH + c
                    dve.wait_ge(s.above, i + 1)
                    dve.scalar_tensor_tensor(w.less[:, i % 2, :], w.above[:, i % 4, :], w.key_b[:, 1, c, m:m + 1],
                                             w.row_lo[:, m, :], ALU.subtract, ALU.is_lt,
                                             accum_out=w.rank[:, i:i + 1]).then_inc(s.ranked, 1)
                    dve.wait_ge(s.ranked, i + 1)
                    dve.tensor_scalar(w.perm[:, m, c, :], g.targets[:, :], w.rank[:, i:i + 1], None,
                                      ALU.is_equal).then_inc(s.perm, 1)

            def dims(q):
                return HEADS, BATCH_U[q % 3]

            def shift(q):
                H, nu = dims(q)
                sc = g.ps[:, 0:H, 0:nu * HD].rearrange("p h (u j) -> p h u j", u=nu)
                e = w.e[:, 0:H * nu * HD].rearrange("p (h u j) -> p h u j", h=H, u=nu)
                mx = w.rmax[:, 0:H * nu].rearrange("p (h u) -> p h u", h=H)
                dve.wait_ge(s.scored, q + 1)
                link(dve.tensor_reduce(mx, sc, AX.X, ALU.max))
                dve.tensor_tensor(e, sc, mx[:, :, :, None].broadcast_to([P, H, nu, HD]),
                                  ALU.subtract).then_inc(s.shifted, 1)

            def normalise(q):
                H, nu = dims(q)
                n = H * nu
                e = w.e[:, 0:n * HD].rearrange("p (x j) -> p x j", j=HD)
                dve.wait_ge(s.exped, q + 1)
                link(dve.tensor_reduce(w.rsum[:, 0:n], e, AX.X, ALU.add))
                link(dve.reciprocal(w.rsum[:, 0:n], w.rsum[:, 0:n]))
                link(dve.tensor_tensor(e, e, w.rsum[:, 0:n, None].broadcast_to([P, n, HD]), ALU.mult))
                if q >= 1:
                    dve.wait_ge(s.mixed, q)
                dve.transpose(w.eT[:, 0:n * HD], w.e[:, 0:n * HD]).then_inc(s.attn, 1)

            def stats(q):
                l, k = q // 3, q % 3
                nu, u0 = BATCH_U[k], first_u[q]
                dve.wait_ge(s.mixed, q + 1)
                for half in range(l + 1):
                    base = g.ps[:, 6 + half, :]
                    whole = nu if k < 2 else nu - 1
                    dve.bn_stats(w.stats[:, half, k, :], custom(base, 0, [[HD, whole], [1, BLK]]))
                    if k == 2:
                        dve.bn_stats(w.stats[:, half, 3, :], custom(base, whole * HD, [[1, 2 * KNN]]))
                    ins = dve.tensor_reduce(custom(w.peak[:, half], 3 * u0, [[3, nu], [1, 3]]),
                                            custom(base, 0, [[HD, nu], [KNN, 3], [1, KNN]]), AX.X, ALU.max)
                ins.then_inc(s.stats, 1)

            for l in range(2):
                q = 3 * l
                shift(q)
                normalise(q)
                shift(q + 1)
                stats(q)
                normalise(q + 1)
                shift(q + 2)
                stats(q + 1)
                normalise(q + 2)
                stats(q + 2)
                dve.wait_ge(s.stats, q + 3)
                for half in range(l + 1):
                    ins = dve.bn_aggr(w.mv[:, half, :], flat(w.stats[:, half]))
                    if half < l:
                        link(ins)
                ins.then_inc(s.moments, 1)
                dve.wait_ge(s.moments, l + 1)
                dve.wait_ge(s.mean, l + 1)
                link(dve.tensor_copy(w.mean[:, :], g.ps[:, 5, 0:1]))
                link(dve.tensor_scalar(w.dev[:, 0:l + 1, 0], w.mv[:, 0:l + 1, 0], w.mean[:, 0:1], None, ALU.subtract))
                link(dve.tensor_tensor(w.dev[:, 0:l + 1, 0], w.dev[:, 0:l + 1, 0], w.dev[:, 0:l + 1, 0], ALU.mult))
                dve.tensor_tensor(w.dev[:, 0:l + 1, 1], w.dev[:, 0:l + 1, 0], w.mv[:, 0:l + 1, 1],
                                  ALU.add).then_inc(s.dev, 1)
                link(dve.tensor_scalar(w.meanb[:, :], w.mean[:, :], w.bias[:, l:l + 1], None, ALU.add))
                link(dve.tensor_scalar(w.f[:, 0:l + 1, :], w.peak[:, 0:l + 1, 0:P], w.bias[:, l:l + 1],
                                       w.meanb[:, 0:1], ALU.add, ALU.subtract))
                dve.wait_ge(s.root, l + 1)
                link(dve.reciprocal(w.rstd[:, :], w.root[:, :]))
                link(dve.tensor_scalar(w.f[:, 0:l + 1, :], w.f[:, 0:l + 1, :], w.rstd[:, 0:1], None, ALU.mult))
                dve.scalar_tensor_tensor(flat(w.f[:, 0:l + 1, :]), flat(w.f[:, 0:l + 1, :]), 0.2,
                                         flat(w.f[:, 0:l + 1, :]), ALU.mult, ALU.max).then_inc(s.turned, 1)
                if l == 0:
                    dve.wait_ge(s.turned, 2)
                    dve.tensor_copy(flat(w.fn), g.ps[:, 7, 0:P]).then_inc(s.f2, 1)
                    dve.wait_ge(s.f2, 1)
                    split()
            dve.wait_ge(s.convolved, 1)
            link(dve.bn_stats(w.st3[:, :], g.ps[0:32, 4, :]))
            dve.bn_aggr(w.mv3[:, :], w.st3[:, :]).then_inc(s.moments, 1)
            dve.wait_ge(s.moments, 3)
            dve.wait_ge(s.root3, 1)
            link(dve.reciprocal(w.r3[:, 1:2], w.r3[:, 0:1]))
            link(dve.tensor_scalar(w.o32[:, 0, :], g.ps[0:32, 4, :], w.mv3[:, 0:1], w.r3[:, 1:2],
                                   ALU.subtract, ALU.mult))
            dve.scalar_tensor_tensor(w.o32[:, 1, :], w.o32[:, 0, :], 0.2, w.o32[:, 0, :], ALU.mult,
                                     ALU.max).then_inc(s.out, 1)
    release(nc, s)


def bcast_rows(keys, b):
    return keys[bass.ds(b, 1), :, :].rearrange("a m n -> (a m) n").partition_broadcast(P)


def add_point_attention(nc, g, d):
    with ExitStack() as st:
        s = semaphores(nc, st, "addp", "loaded added")
        y = st.enter_context(nc.sbuf_tensor("addp_y", [P, NT, DIM], F32))
        with nc.Block() as block:
            @block.sync
            def _(sp):
                for t in range(NT):
                    sp.dma_start(y[:, t, :], d.xatt[t * P:(t + 1) * P, :]).then_inc(s.loaded, 16)

            @block.vector
            def _(dve):
                dve.wait_ge(s.loaded, 16 * NT)
                dve.tensor_tensor(flat(g.x), flat(g.x), flat(y), ALU.add).then_inc(s.added, 1)
        release(nc, s)


def bound_attention(nc, g, d):
    with ExitStack() as st:
        def sb(name, shape, dt=F32):
            return st.enter_context(nc.sbuf_tensor("ba_" + name, shape, dt))
        s = semaphores(nc, st, "ba", "loaded step signs bound turned query values scored gate masked mixed added")
        vec = sb("vec", [NCH, 3, P])
        sgn = sb("sgn", [NCH, 3, P])
        zero = sb("zero", [NCH, 3, P])
        alpha = sb("alpha", [NCH, 3])
        sel = sb("sel", [NCH, NCH, P])
        causal = sb("causal", [P, P])
        qk = sb("qk", [P, NCH])
        qc = sb("qc", [P, NCH])
        query = sb("query", [P, NCH, ROWS])
        value = sb("value", [P, NT, DIM])
        gate = sb("gate", [P, NT, NCH, P])
        with nc.Block() as block:
            @block.sync
            def _(sp):
                sp.dma_start(vec[:, :, :], d.bind).then_inc(s.loaded, 16)
                sp.dma_start(sel[:, :, :], d.sel4).then_inc(s.loaded, 16)
                sp.dma_start(causal[:, :], d.causal).then_inc(s.loaded, 16)

            @block.scalar
            def _(act):
                act.wait_ge(s.loaded, 48)
                act.sign(sgn[:, :, :], vec[:, :, :]).then_inc(s.signs, 1)
                for t in range(NT):
                    act.wait_ge(s.scored, t + 1)
                    act.activation(flat(gate[:, t]), g.ps[:, 2 + t, :], ACT.Sigmoid,
                                   scale=4.0 * float(P) ** -0.5).then_inc(s.gate, 1)

            @block.tensor
            def _(pe):
                pe.wait_ge(s.bound, 1)
                pe.transpose(g.ps[:, 0, 0:NCH], vec[:, 0, :], g.ident[0:NCH, 0:NCH])
                pe.transpose(g.ps[:, 0, NCH:2 * NCH], vec[:, 1, :], g.ident[0:NCH, 0:NCH])
                for h in range(NCH):
                    ins = pe.matmul(g.ps[:, 1, h * P:(h + 1) * P], sel[:, h, :], vec[:, 2, :], start=True, stop=True)
                ins.then_inc(s.turned, 1)
                for t in range(NT):
                    pe.wait_ge(s.query, NCH)
                    for h in range(NCH):
                        ins = pe.matmul(g.ps[:, 2 + t, h * P:(h + 1) * P], g.xnT[:, h, t * P:(t + 1) * P],
                                        query[:, h, t * P:(t + 1) * P], start=True, stop=True)
                    ins.then_inc(s.scored, 1)
                for t in range(NT):
                    pe.wait_ge(s.masked, t + 1)
                    pe.wait_ge(s.values, NT)
                    if t >= 2:
                        pe.wait_ge(s.added, t - 1)
                    for h in range(NCH):
                        ins = pe.matmul(g.ps[:, 6 + t % 2, h * P:(h + 1) * P], gate[:, t, h, :],
                                        value[:, t, h * P:(h + 1) * P], start=True, stop=True)
                    ins.then_inc(s.mixed, 1)

            @block.vector
            def _(dve):
                link = chain(dve, s.step)
                dve.wait_ge(s.loaded, 48)
                link(dve.tensor_reduce(alpha[:, :], vec[:, :, :], AX.X, ALU.add, apply_absolute_value=True))
                link(dve.tensor_scalar(alpha[:, :], alpha[:, :], 1.0 / P, None, ALU.mult))
                dve.wait_ge(s.signs, 1)
                mean = alpha[:, :, None].broadcast_to([NCH, 3, P])
                link(dve.tensor_tensor(sgn[:, :, :], sgn[:, :, :], mean, ALU.mult))
                link(dve.tensor_scalar(zero[:, :, :], sgn[:, :, :], 0.0, None, ALU.is_equal))
                link(dve.tensor_tensor(zero[:, :, :], zero[:, :, :], mean, ALU.mult))
                link(dve.tensor_tensor(sgn[:, :, :], sgn[:, :, :], zero[:, :, :], ALU.add))
                link(dve.tensor_tensor(sgn[:, :, :], sgn[:, :, :], vec[:, :, :], ALU.subtract))
                dve.tensor_tensor(vec[:, :, :], sgn[:, :, :], vec[:, :, :], ALU.add).then_inc(s.bound, 1)
                dve.wait_ge(s.turned, 1)
                link(dve.tensor_copy(qc[:, :], g.ps[:, 0, 0:NCH]))
                link(dve.tensor_tensor(qk[:, :], qc[:, :], g.ps[:, 0, NCH:2 * NCH], ALU.mult))
                for h in range(NCH):
                    dve.tensor_scalar(query[:, h, :], g.xnT[:, h, :], qk[:, h:h + 1], None,
                                      ALU.mult).then_inc(s.query, 1)
                for t in range(NT):
                    dve.tensor_tensor(value[:, t, :], g.xn[:, t, :], g.ps[:, 1, :], ALU.mult).then_inc(s.values, 1)
                for t in range(NT):
                    dve.wait_ge(s.gate, t + 1)
                    dve.tensor_tensor(gate[:, t], gate[:, t], causal[:, None, :].broadcast_to([P, NCH, P]),
                                      ALU.mult).then_inc(s.masked, 1)
                for t in range(NT):
                    dve.wait_ge(s.mixed, t + 1)
                    dve.tensor_tensor(g.x[:, t, :], g.x[:, t, :], g.ps[:, 6 + t % 2, :], ALU.add).then_inc(s.added, 1)
        release(nc, s)


EXPERTS, RANK = 8, 16


def experts(nc, g, d, name, hidden, scale, capacity):
    G = hidden or EXPERTS
    n_rows = 4 if hidden else 1
    with ExitStack() as st:
        def sb(nm, shape, dt=F32):
            return st.enter_context(nc.sbuf_tensor(f"{name}_{nm}", shape, dt))
        s = semaphores(nc, st, name, "loaded step projected hmom hroot hidden hturned hback gates top expo chosen counted "
                 "weighted turned low out added")
        wa = sb("wa", [P, NCH, G + P])
        wb = sb("wb", [P, NCH, DIM])
        lb = sb("lb", [P, DIM])
        brow = sb("brow", [1, DIM])
        ones = sb("ones", [P, P])
        iota = sb("iota", [P, EXPERTS])
        low = sb("low", [P, NT, P])
        lowT = sb("lowT", [P, NT, P])
        lg = sb("lg", [P, NT, EXPERTS])
        top = sb("top", [P, NT, 8])
        idx = sb("idx", [P, NT, 8], U32)
        idf = sb("idf", [P, NT, 8])
        hot = sb("hot", [P, NT, 2, EXPERTS])
        dlt = sb("dlt", [P, NT])
        ex = sb("ex", [P, NT])
        w01 = sb("w01", [P, NT, 2])
        ok = sb("ok", [P, 2, EXPERTS])
        w2 = sb("w2", [P, NT, 2, EXPERTS])
        wfull = sb("wfull", [P, NT, EXPERTS])
        if hidden:
            rowv = sb("rowv", [P, 3, hidden])
            gb2 = sb("gb2", [P, EXPERTS])
            gw2 = sb("gw2", [hidden, EXPERTS])
            hh = sb("hh", [P, NT, hidden])
            hst = sb("hst", [P, NT, 6])
            hmv = sb("hmv", [P, NT, 2])
            hr = sb("hr", [P, NT])
            hT = sb("hT", [hidden, NT, P])
        with nc.Block() as block:
            @block.sync
            def _(sp):
                sp.dma_start(wa[:, :, :], d.all[name + "_wa"]).then_inc(s.loaded, 16)
                sp.dma_start(iota[:, :], d.iota8.partition_broadcast(P)).then_inc(s.loaded, 16)
                sp.dma_start(brow[:, :], d.all[name + "_bias"]).then_inc(s.loaded, 16)
                sp.dma_start(wb[:, :, :], d.all[name + "_wb"]).then_inc(s.loaded, 16)
                sp.dma_start(lb[:, :], d.all[name + "_lb"]).then_inc(s.loaded, 16)
                if hidden:
                    sp.dma_start(rowv[:, :, :], d.all[name + "_rows"].partition_broadcast(P)).then_inc(s.loaded, 16)
                    sp.dma_start(gb2[:, :], d.all[name + "_gb2"].partition_broadcast(P)).then_inc(s.loaded, 16)
                    sp.dma_start(gw2[:, :], d.all[name + "_gw2"]).then_inc(s.loaded, 16)

            loads = 16 * (8 if hidden else 5)

            @block.tensor
            def _(pe):
                pe.wait_ge(s.loaded, loads)
                for t in range(NT):
                    for c in range(NCH):
                        ins = pe.matmul(g.ps[:, t, 0:G + P], g.xnT[:, c, t * P:(t + 1) * P], wa[:, c, :],
                                        start=(c == 0), stop=(c == NCH - 1))
                    ins.then_inc(s.projected, 1)
                if hidden:
                    pe.wait_ge(s.hidden, 1)
                    for t in range(NT):
                        ins = pe.transpose(g.ps[0:hidden, 4, t * P:(t + 1) * P], hh[:, t, :], g.ident[:, :])
                    ins.then_inc(s.hturned, 1)
                    pe.wait_ge(s.hback, 1)
                    for t in range(NT):
                        ins = pe.matmul(g.ps[:, 5, t * EXPERTS:(t + 1) * EXPERTS], hT[:, t, :], gw2[:, :],
                                        start=True, stop=True)
                    ins.then_inc(s.gates, 1)
                if capacity:
                    pe.wait_ge(s.chosen, 1)
                    for t in range(NT):
                        ins = pe.matmul(g.ps[:, 6, 0:2 * EXPERTS], ones[:, :], flat(hot[:, t]),
                                        start=(t == 0), stop=(t == NT - 1))
                    ins.then_inc(s.counted, 1)
                for t in range(NT):
                    pe.wait_ge(s.weighted, t + 1)
                    pe.transpose(g.ps[:, 7, t * P:(t + 1) * P], low[:, t, :], g.ident[:, :]).then_inc(s.turned, 1)
                for t in range(NT):
                    for c in range(NCH):
                        pe.matmul(g.ps[:, t, :], g.xnT[:, c, t * P:(t + 1) * P], wb[:, c, :],
                                  start=(c == 0), stop=False)
                    pe.matmul(g.ps[:, t, :], ones[0:1, :], brow[:, :], start=False, stop=False)
                    pe.wait_ge(s.low, 1)
                    pe.matmul(g.ps[:, t, :], lowT[:, t, :], lb[:, :], start=False, stop=True).then_inc(s.out, 1)

            @block.scalar
            def _(act):
                if hidden:
                    act.wait_ge(s.hmom, 1)
                    act.activation(hr[:, :], hmv[:, :, 1], ACT.Sqrt, bias=g.eps[:, 0:1]).then_inc(s.hroot, 1)
                    act.wait_ge(s.hturned, 1)
                    act.copy(flat(hT), g.ps[0:hidden, 4, :]).then_inc(s.hback, 1)
                act.wait_ge(s.top, 1)
                act.activation(ex[:, :], dlt[:, :], ACT.Exp).then_inc(s.expo, 1)
                act.wait_ge(s.turned, NT)
                act.copy(flat(lowT), g.ps[:, 7, :]).then_inc(s.low, 1)

            @block.vector
            def _(dve):
                link = chain(dve, s.step)
                link(dve.memset(ones[:, :], 1.0))
                dve.wait_ge(s.loaded, loads)
                dve.wait_ge(s.projected, NT)
                if hidden:
                    link(dve.tensor_tensor(hh[:, :, :], g.ps[:, 0:NT, 0:G],
                                           rowv[:, 0:1, :].broadcast_to([P, NT, G]), ALU.add))
                    for t in range(NT):
                        link(dve.bn_stats(hst[:, t, :], hh[:, t, :]))
                    for t in range(NT):
                        ins = dve.bn_aggr(hmv[:, t, :], hst[:, t, :])
                        if t < NT - 1:
                            link(ins)
                    ins.then_inc(s.hmom, 1)
                    dve.wait_ge(s.hmom, 1)
                    dve.wait_ge(s.hroot, 1)
                    link(dve.reciprocal(hr[:, :], hr[:, :]))
                    for t in range(NT):
                        link(dve.tensor_scalar(hh[:, t, :], hh[:, t, :], hmv[:, t, 0:1], hr[:, t:t + 1],
                                               ALU.subtract, ALU.mult))
                    link(dve.tensor_tensor(hh[:, :, :], hh[:, :, :], rowv[:, 1:2, :].broadcast_to([P, NT, G]), ALU.mult))
                    link(dve.tensor_tensor(hh[:, :, :], hh[:, :, :], rowv[:, 2:3, :].broadcast_to([P, NT, G]), ALU.add))
                    dve.tensor_scalar(hh[:, :, :], hh[:, :, :], 0.0, None, ALU.max).then_inc(s.hidden, 1)
                    dve.wait_ge(s.gates, 1)
                    link(dve.tensor_tensor(lg[:, :, :], g.ps[:, 5, 0:NT * EXPERTS].rearrange("p (t e) -> p t e", t=NT),
                                           gb2[:, None, :].broadcast_to([P, NT, EXPERTS]), ALU.add))
                else:
                    link(dve.tensor_copy(lg[:, :, :], g.ps[:, 0:NT, 0:G]))
                for t in range(NT):
                    link(dve.max(top[:, t, :], lg[:, t, :]))
                for t in range(NT):
                    link(dve.max_index(idx[:, t, :], top[:, t, :], lg[:, t, :]))
                dve.tensor_tensor(dlt[:, :], top[:, :, 1], top[:, :, 0], ALU.subtract).then_inc(s.top, 1)
                link(dve.tensor_copy(idf[:, :, :], idx[:, :, :]))
                ins = dve.tensor_tensor(hot[:, :, :, :], iota[:, None, None, :].broadcast_to([P, NT, 2, EXPERTS]),
                                        idf[:, :, 0:2, None].broadcast_to([P, NT, 2, EXPERTS]), ALU.is_equal)
                ins.then_inc(s.chosen, 1)
                dve.wait_ge(s.chosen, 1)
                dve.wait_ge(s.expo, 1)
                link(dve.tensor_scalar(w01[:, :, 0], ex[:, :], 1.0, None, ALU.add))
                link(dve.reciprocal(w01[:, :, 0], w01[:, :, 0]))
                link(dve.tensor_scalar(w01[:, :, 0], w01[:, :, 0], scale, None, ALU.mult))
                link(dve.tensor_tensor(w01[:, :, 1], w01[:, :, 0], ex[:, :], ALU.mult))
                if capacity:
                    dve.wait_ge(s.counted, 1)
                    link(dve.tensor_scalar(flat(ok), g.ps[:, 6, 0:2 * EXPERTS], float(capacity), None, ALU.is_le))
                    for t in range(NT):
                        link(dve.tensor_tensor(hot[:, t], hot[:, t], ok[:, :, :], ALU.mult))
                link(dve.tensor_tensor(w2[:, :, :, :], hot[:, :, :, :],
                                       w01[:, :, :, None].broadcast_to([P, NT, 2, EXPERTS]), ALU.mult))
                link(dve.tensor_tensor(wfull[:, :, :], w2[:, :, 0, :], w2[:, :, 1, :], ALU.add))
                for t in range(NT):
                    dve.tensor_tensor(low[:, t, :].rearrange("p (e r) -> p e r", e=EXPERTS),
                                      g.ps[:, t, G:G + P].rearrange("p (e r) -> p e r", e=EXPERTS),
                                      wfull[:, t, :, None].broadcast_to([P, EXPERTS, RANK]),
                                      ALU.mult).then_inc(s.weighted, 1)
                for t in range(NT):
                    dve.wait_ge(s.out, t + 1)
                    dve.tensor_tensor(g.x[:, t, :], g.x[:, t, :], g.ps[:, t, :], ALU.add).then_inc(s.added, 1)
        release(nc, s)


Q_HEADS, KV_HEADS, GROUP = 32, 8, 4
CTX = 512
KV = CTX + TOK
RMS_EPS = 1e-6
ATT_SCALE = float(P) ** -0.5


def cross_attention(nc, g, d):
    with ExitStack() as st:
        def sb(name, shape, dt=F32):
            return st.enter_context(nc.sbuf_tensor("ca_" + name, shape, dt))
        w = named({})
        w.qT = sb("qT", [P, Q_HEADS, ROWS])
        w.klat = sb("klat", [P, KV_HEADS, ROWS])
        w.wk = sb("wk", [P, NCH, KV_HEADS * P])
        w.wv = sb("wv", [P, NCH, KV_HEADS * P])
        w.mean = sb("mean", [P, P])
        w.nw = sb("nw", [P, 3])
        w.eps = sb("eps", [P, 1])
        with ExitStack() as s1:
            project_latents(nc, g, d, w, s1)
        with ExitStack() as s2:
            attend(nc, g, d, w, s2)
        with ExitStack() as s3:
            project_out(nc, g, d, w, s3)


def project_latents(nc, g, d, w, st):
    def sb(name, shape, dt=F32):
        return st.enter_context(nc.sbuf_tensor("pl_" + name, shape, dt))
    s = semaphores(nc, st, "pl", "kw q0 q1 consts step q sq ms root rstd done kv kvout vst0 vst1")
    wq = sb("wq", [P, 2, NCH, GROUP * P])
    sq = sb("sq", [P, 2, ROWS])
    root = sb("root", [P, 2, ROWS])
    vout = sb("vout", [P, 2, 512])
    s_q, s_v = (s.q0, s.q1), (s.vst0, s.vst1)
    n_kv = KV_HEADS + NT * 2
    with nc.Block() as block:
        @block.sync
        def _(sp):
            sp.dma_start(w.mean[:, :], d.mean128).then_inc(s.kw, 16)
            sp.dma_start(w.nw[:, 0:2], d.qk_norm).then_inc(s.kw, 16)
            for k in range(KV_HEADS):
                if k >= 2:
                    sp.wait_ge(s.q, GROUP * (k - 1))
                sp.dma_start(wq[:, k % 2, :, :], d.wq[:, :, k * GROUP * P:(k + 1) * GROUP * P]).then_inc(s_q[k % 2], 16)
            sp.dma_start(w.wk[:, :, :], d.wk).then_inc(s.kw, 16)
            sp.dma_start(w.wv[:, :, :], d.wv).then_inc(s.kw, 16)
            for i in range(NT * 2):
                sp.wait_ge(s.kvout, KV_HEADS + i + 1)
                t, half = i // 2, i % 2
                sp.dma_start(d.v_lat[t * P:(t + 1) * P, half * 512:(half + 1) * 512], vout[:, i % 2, :]).then_inc(s_v[i % 2], 16)
            for sem in s_v:
                sp.wait_ge(sem, 16 * NT)

        @block.tensor
        def _(pe):
            pe.wait_ge(s.kw, 32)

            def mean_square(h):
                pe.wait_ge(s.sq, h + 1)
                if h >= 2:
                    pe.wait_ge(s.root, h - 1)
                pe.matmul(g.ps[:, 3 + h % 2, :], w.mean[:, :], sq[:, h % 2, :], start=True, stop=True).then_inc(s.ms, 1)

            for h in range(Q_HEADS):
                k = h // GROUP
                if h % GROUP == 0:
                    pe.wait_ge(s_q[k % 2], 16 * (k // 2 + 1))
                if h >= 3:
                    pe.wait_ge(s.done, h - 2)
                for c in range(NCH):
                    ins = pe.matmul(g.ps[:, h % 3, :], wq[:, k % 2, c, (h % GROUP) * P:(h % GROUP + 1) * P],
                                    g.xnT[:, c, :], start=(c == 0), stop=(c == NCH - 1))
                ins.then_inc(s.q, 1)
                if h >= 1:
                    mean_square(h - 1)
            mean_square(Q_HEADS - 1)
            pe.wait_ge(s.kw, 64)
            for i in range(n_kv):
                if i >= 2:
                    pe.wait_ge(s.kvout, i - 1)
                for c in range(NCH):
                    if i < KV_HEADS:
                        lhs, rhs = w.wk[:, c, i * P:(i + 1) * P], g.xnT[:, c, :]
                    else:
                        t, half = (i - KV_HEADS) // 2, i % 2
                        lhs, rhs = g.xnT[:, c, t * P:(t + 1) * P], w.wv[:, c, half * 512:(half + 1) * 512]
                    ins = pe.matmul(g.ps[:, 5 + i % 2, :], lhs, rhs, start=(c == 0), stop=(c == NCH - 1))
                ins.then_inc(s.kv, 1)

        @block.scalar
        def _(act):
            act.wait_ge(s.consts, 1)
            for h in range(Q_HEADS + 1):
                if h < Q_HEADS:
                    act.wait_ge(s.q, h + 1)
                    if h >= 2:
                        act.wait_ge(s.ms, h - 1)
                    act.activation(sq[:, h % 2, :], g.ps[:, h % 3, :], ACT.Square).then_inc(s.sq, 1)
                if h >= 1:
                    act.wait_ge(s.ms, h)
                    if h >= 3:
                        act.wait_ge(s.done, h - 2)
                    act.activation(root[:, (h - 1) % 2, :], g.ps[:, 3 + (h - 1) % 2, :], ACT.Sqrt,
                                   bias=w.eps[:, 0:1]).then_inc(s.root, 1)
            for i in range(n_kv):
                act.wait_ge(s.kv, i + 1)
                if i < KV_HEADS:
                    dst = w.klat[:, i, :]
                else:
                    j = i - KV_HEADS
                    if j >= 2:
                        act.wait_ge(s_v[j % 2], 16 * (j // 2))
                    dst = vout[:, j % 2, :]
                act.copy(dst, g.ps[:, 5 + i % 2, :]).then_inc(s.kvout, 1)

        @block.vector
        def _(dve):
            link = chain(dve, s.step)
            link(dve.memset(w.eps[:, :], RMS_EPS))
            dve.wait_ge(s.kw, 32)
            dve.tensor_tensor(w.nw[:, 2:3], w.nw[:, 0:1], w.nw[:, 1:2], ALU.mult).then_inc(s.consts, 1)
            dve.wait_ge(s.consts, 1)
            for h in range(Q_HEADS):
                dve.wait_ge(s.root, h + 1)
                link(dve.reciprocal(root[:, h % 2, :], root[:, h % 2, :]))
                dve.scalar_tensor_tensor(w.qT[:, h, :], g.ps[:, h % 3, :], w.nw[:, 2:3], root[:, h % 2, :],
                                         ALU.mult, ALU.mult).then_inc(s.done, 1)
    release(nc, s)


def attend(nc, g, d, w, st):
    def sb(name, shape, dt=F32):
        return st.enter_context(nc.sbuf_tensor("at_" + name, shape, dt))
    s = semaphores(nc, st, "at", "ctx vl step qb kl klsq k kc sq ms msl root rootl rstd v vc s scaled nmax expd norm prob "
             "turned pt mixed ot zero")
    t = named({})
    t.ctx = g.xn
    t.kT = sb("kT", [P, KV_HEADS, KV])
    t.R = sb("R", [P, KV_HEADS, KV])
    t.V = sb("V", [P, CTX // P + 1, KV_HEADS * P])
    t.sq = sb("sq", [P, 2, CTX])
    t.sql = sb("sql", [P, KV_HEADS, TOK])
    t.qb = sb("qb", [P, KV_HEADS, GROUP, TOK])
    t.pr = sb("pr", [P, 2, KV])
    t.mx = sb("mx", [P, 2, 2])
    t.sum = sb("sum", [P, 2, 2])
    t.PT = sb("PT", [P, CTX // P + 1, P])
    NB = CTX // P
    with nc.Block() as block:
        @block.gpsimd
        def _(pool):
            pool.memset(t.V[:, NB, :], 0.0)
            pool.memset(t.PT[:, NB, :], 0.0)
    release(nc, s)
    with nc.Fori(0, LAT) as b:
        with nc.Block() as block:
            @block.sync
            def _(sp):
                sp.dma_start(t.ctx[:, :, :], d.ctxT[bass.ds(b, 1), :, :, :].rearrange("b p c n -> (b p) c n")).then_inc(s.ctx, 16)
                sp.dma_start(t.V[0:TOK, NB, :], d.v_lat[bass.ds(b * TOK, TOK), :]).then_inc(s.vl, 16)

            @block.gpsimd
            def _(pool):
                pool.tensor_copy(flat_heads(t.qb), w.qT[:, :, bass.ds(b * TOK, TOK)]).then_inc(s.qb, 1)
                pool.tensor_copy(t.kT[:, :, CTX:KV], w.klat[:, :, bass.ds(b * TOK, TOK)]).then_inc(s.kl, 1)
                pool.wait_ge(s.kl, 1)
                pool.tensor_tensor(t.sql[:, :, :], t.kT[:, :, CTX:KV], t.kT[:, :, CTX:KV], ALU.mult).then_inc(s.klsq, 1)
                for h in range(KV_HEADS):
                    pool.wait_ge(s.norm, h + 1)
                    pool.tensor_scalar(t.pr[:, h % 2, :], t.pr[:, h % 2, :], t.sum[:, h % 2, 1:2], None,
                                       ALU.mult).then_inc(s.prob, 1)

            @block.tensor
            def _(pe):
                def mean_square(h):
                    pe.wait_ge(s.sq, h + 1)
                    if h >= 1:
                        pe.wait_ge(s.root, h)
                    pe.matmul(g.ps[:, 2, :], w.mean[:, :], t.sq[:, h % 2, :], start=True, stop=True).then_inc(s.ms, 1)

                pe.wait_ge(s.ctx, 16)
                for h in range(KV_HEADS):
                    if h >= 2:
                        pe.wait_ge(s.sq, h - 1)
                    for c in range(NCH):
                        ins = pe.matmul(g.ps[:, h % 2, :], w.wk[:, c, h * P:(h + 1) * P], t.ctx[:, c, :],
                                        start=(c == 0), stop=(c == NCH - 1))
                    ins.then_inc(s.k, 1)
                    if h == 0:
                        pe.wait_ge(s.klsq, 1)
                        pe.matmul(g.ps[:, 3, 0:KV_HEADS * TOK], w.mean[:, :], flat(t.sql), start=True,
                                  stop=True).then_inc(s.msl, 1)
                    else:
                        mean_square(h - 1)
                mean_square(KV_HEADS - 1)

                def score(h):
                    pe.wait_ge(s.qb, 1)
                    pe.wait_ge(s.kc, h + 1)
                    if h >= 1:
                        pe.wait_ge(s.scaled, h)
                    pe.matmul(g.ps[:, 4, :], flat(t.qb[:, h]), t.kT[:, h, 0:CTX], start=True, stop=True)
                    pe.matmul(g.ps[:, 5, 0:TOK], flat(t.qb[:, h]), t.kT[:, h, CTX:KV], start=True,
                              stop=True).then_inc(s.s, 1)

                def value(i):
                    n, half = i // 2, i % 2
                    if i < 2:
                        pe.wait_ge(s.sq, KV_HEADS)
                    else:
                        pe.wait_ge(s.vc, i - 1)
                    for c in range(NCH):
                        ins = pe.matmul(g.ps[:, i % 2, :], t.ctx[:, c, n * P:(n + 1) * P],
                                        w.wv[:, c, half * 512:(half + 1) * 512], start=(c == 0), stop=(c == NCH - 1))
                    ins.then_inc(s.v, 1)

                def turn(h):
                    pe.wait_ge(s.prob, h + 1)
                    if h >= 1:
                        pe.wait_ge(s.ot, h)
                    for n in range(NB):
                        pe.transpose(g.ps[:, 6, n * P:(n + 1) * P], t.pr[:, h % 2, n * P:(n + 1) * P], g.ident[:, :])
                    pe.transpose(g.ps[0:TOK, 7, 0:P], t.pr[:, h % 2, CTX:KV], g.ident[:, :]).then_inc(s.turned, 1)

                def mix(h):
                    pe.wait_ge(s.pt, h + 1)
                    if h == 0:
                        pe.wait_ge(s.vc, 2 * NB)
                        pe.wait_ge(s.vl, 16)
                    for n in range(NB + 1):
                        ins = pe.matmul(g.ps[:, 7, P:2 * P], t.V[:, n, h * P:(h + 1) * P], t.PT[:, n, :],
                                        start=(n == 0), stop=(n == NB))
                    ins.then_inc(s.mixed, 1)

                score(0)
                for i in range(NB * 2):
                    value(i)
                for h in range(KV_HEADS):
                    if h + 1 < KV_HEADS:
                        score(h + 1)
                    turn(h)
                    mix(h)

            @block.scalar
            def _(act):
                def copy_key(h):
                    act.wait_ge(s.k, h + 1)
                    act.copy(t.kT[:, h, 0:CTX], g.ps[:, h % 2, :]).then_inc(s.kc, 1)
                    if h >= 2:
                        act.wait_ge(s.ms, h - 1)
                    act.activation(t.sq[:, h % 2, :], g.ps[:, h % 2, :], ACT.Square).then_inc(s.sq, 1)

                def root(h):
                    act.wait_ge(s.ms, h + 1)
                    act.activation(t.R[:, h, 0:CTX], g.ps[:, 2, :], ACT.Sqrt, bias=w.eps[:, 0:1]).then_inc(s.root, 1)

                def copy_turned(h):
                    act.wait_ge(s.turned, h + 1)
                    if h >= 1:
                        act.wait_ge(s.mixed, h)
                    act.copy(flat(t.PT[:, 0:NB]), g.ps[:, 6, :])
                    act.copy(t.PT[0:TOK, NB, :], g.ps[0:TOK, 7, 0:P]).then_inc(s.pt, 1)

                copy_key(0)
                act.wait_ge(s.msl, 1)
                act.activation(t.R[:, :, CTX:KV], g.ps[:, 3, 0:KV_HEADS * TOK].rearrange("p (h n) -> p h n", n=TOK),
                               ACT.Sqrt, bias=w.eps[:, 0:1]).then_inc(s.rootl, 1)
                for h in range(1, KV_HEADS):
                    copy_key(h)
                    root(h - 1)
                root(KV_HEADS - 1)
                for i in range(NB * 2):
                    n, half = i // 2, i % 2
                    act.wait_ge(s.v, i + 1)
                    act.copy(t.V[:, n, half * 512:(half + 1) * 512], g.ps[:, i % 2, :]).then_inc(s.vc, 1)
                for h in range(KV_HEADS):
                    act.wait_ge(s.nmax, h + 1)
                    act.activation(t.pr[:, h % 2, :], t.pr[:, h % 2, :], ACT.Exp, bias=t.mx[:, h % 2, 1:2],
                                   scale=ATT_SCALE, accum_out=t.sum[:, h % 2, 0:1]).then_inc(s.expd, 1)
                    if h >= 1:
                        copy_turned(h - 1)
                copy_turned(KV_HEADS - 1)

            @block.vector
            def _(dve):
                link = chain(dve, s.step)
                dve.wait_ge(s.rootl, 1)
                for h in range(KV_HEADS):
                    dve.wait_ge(s.root, h + 1)
                    dve.reciprocal(t.R[:, h, :], t.R[:, h, :]).then_inc(s.rstd, 1)

                def scale(h):
                    dve.wait_ge(s.rstd, h + 1)
                    dve.wait_ge(s.s, h + 1)
                    if h >= 2:
                        dve.wait_ge(s.turned, h - 1)
                    link(dve.tensor_tensor(t.pr[:, h % 2, CTX:KV], g.ps[:, 5, 0:TOK], t.R[:, h, CTX:KV], ALU.mult))
                    dve.tensor_tensor(t.pr[:, h % 2, 0:CTX], g.ps[:, 4, :], t.R[:, h, 0:CTX],
                                      ALU.mult).then_inc(s.scaled, 1)
                    dve.wait_ge(s.scaled, h + 1)
                    link(dve.tensor_reduce(t.mx[:, h % 2, 0:1], t.pr[:, h % 2, :], AX.X, ALU.max))
                    dve.tensor_scalar(t.mx[:, h % 2, 1:2], t.mx[:, h % 2, 0:1], -ATT_SCALE, None,
                                      ALU.mult).then_inc(s.nmax, 1)

                def store(h):
                    dve.wait_ge(s.mixed, h + 1)
                    dve.tensor_copy(w.qT[:, h * GROUP:(h + 1) * GROUP, bass.ds(b * TOK, TOK)],
                                    g.ps[:, 7, P:2 * P].rearrange("p (a q) -> p a q", a=GROUP)).then_inc(s.ot, 1)

                scale(0)
                for h in range(KV_HEADS):
                    dve.wait_ge(s.expd, h + 1)
                    dve.reciprocal(t.sum[:, h % 2, 1:2], t.sum[:, h % 2, 0:1]).then_inc(s.norm, 1)
                    if h + 1 < KV_HEADS:
                        scale(h + 1)
                    store(h)
        release(nc, s)


def flat_heads(t):
    return t[:, :, :, :].rearrange("p k a q -> p (k a) q")


def project_out(nc, g, d, w, st):
    s = semaphores(nc, st, "po", "w0 w1 used out added")
    wo = st.enter_context(nc.sbuf_tensor("po_wo", [P, 2, GROUP, DIM], F32))
    s_w = (s.w0, s.w1)
    with nc.Block() as block:
        @block.sync
        def _(sp):
            for k in range(KV_HEADS):
                if k >= 2:
                    sp.wait_ge(s.used, k - 1)
                sp.dma_start(wo[:, k % 2, :, :], d.wo[:, k * GROUP:(k + 1) * GROUP, :]).then_inc(s_w[k % 2], 16)

        @block.tensor
        def _(pe):
            for k in range(KV_HEADS):
                pe.wait_ge(s_w[k % 2], 16 * (k // 2 + 1))
                for t in range(NT):
                    for a in range(GROUP):
                        h = k * GROUP + a
                        ins = pe.matmul(g.ps[:, t, :], w.qT[:, h, t * P:(t + 1) * P], wo[:, k % 2, a, :],
                                        start=(h == 0), stop=(h == Q_HEADS - 1))
                ins.then_inc(s.used, 1)

        @block.vector
        def _(dve):
            dve.wait_ge(s.used, KV_HEADS)
            for t in range(NT):
                dve.tensor_tensor(g.x[:, t, :], g.x[:, t, :], g.ps[:, t, :], ALU.add).then_inc(s.added, 1)
    release(nc, s)


HM, HIN, NST, NHH, HP, TAPS = 128, 256, 16, 4, 64, 7
SEQ, NSEQ = LAT, TOK
PAD = TAPS - 1
HYDRA_EPS = 1e-5


def hydra(nc, g, d):
    with ExitStack() as st:
        def sb(name, shape, dt=F32):
            return st.enter_context(nc.sbuf_tensor("hy_" + name, shape, dt))
        w = named({name: sb(name, shape) for name, shape in (
                            ("wd", [P, NCH, HM]), ("bd", [P, 1]), ("gate", [P, 1]), ("wu", [HM, DIM]), ("bu", [1, DIM]),
                            ("wx", [HM, HIN]), ("wbc", [HM, 48]), ("wz", [HM, HIN + 2 * NHH]), ("cw", [P, 3, TAPS]),
                            ("cb", [P, 3]), ("dtb", [P, 2 * NHH]), ("alog", [P, 2 * NHH]), ("D", [P, NHH]),
                            ("fcD", [P, 2, NHH]), ("nw", [P, 2]), ("wo", [P, 2, HM]), ("same", [P, P]),
                            ("at", [P, 2, SEQ]), ("past", [P, 2, SEQ]))})
        names = list(w.all)
        w.ones = sb("ones", [1, P])
        w.xmid = sb("xmid", [HM, ROWS])
        w.u = sb("u", [HM, ROWS])
        w.A = sb("A", [P, 2 * NHH])
        w.alpha = sb("alpha", [P, 1])
        w.cp = sb("cp", [P, 3, NSEQ, PAD + SEQ])
        w.acc = sb("acc", [P, 3, ROWS])
        w.c0 = sb("c0", [NST, ROWS])
        w.xtok = sb("xtok", [P, NT, HIN])
        w.sz = sb("sz", [P, NT, HIN])
        w.yz = sb("yz", [P, NT, HIN])
        w.y2 = sb("y2", [P, NT, HIN])
        w.ynT = sb("ynT", [P, 2, ROWS])
        w.dt = sb("dt", [P, NT, 2 * NHH])
        w.sp = sb("sp", [P, 4, NT * 2 * NHH])
        w.dA = sb("dA", [P, NT, 2 * NHH])
        w.spread = sb("spread", [P, NT, 2, NHH, SEQ])
        w.d0 = sb("d0", [P, NT, 2, NHH, SEQ])
        w.d1 = sb("d1", [P, NT, 2, NHH, SEQ])
        w.L = sb("L", [P, NT, 2, NHH, SEQ])
        w.Gm = sb("Gm", [P, NT, P])
        w.Mf = sb("Mf", [P, 2, NHH, P])
        w.Mb = sb("Mb", [P, 2, NHH, P])
        w.f = sb("f", [P, NT, NHH])
        w.ms = sb("ms", [P, NT])
        w.eps = sb("eps", [P, 1])

        s = semaphores(nc, st, "hy0", "loaded step down gelu consts")
        with nc.Block() as block:
            @block.sync
            def _(sp):
                for n in names:
                    src = d.all["hy_" + n]
                    if n in ("gate", "dtb", "alog", "D"):
                        src = src.partition_broadcast(P)
                    t = w.all[n]
                    sp.dma_start(t[tuple([slice(None)] * len(t.shape))], src).then_inc(s.loaded, 16)

            @block.gpsimd
            def _(pool):
                for t in (w.cp, w.Mf, w.Mb):
                    pool.memset(flat(t), 0.0)
                pool.memset(w.ones[:, :], 1.0)
                pool.memset(w.eps[:, :], HYDRA_EPS)

            @block.tensor
            def _(pe):
                pe.wait_ge(s.loaded, 16 * len(names))
                for c in range(NCH):
                    ins = pe.matmul(g.ps[:, 0, :], w.wd[:, c, :], g.xnT[:, c, :], start=(c == 0), stop=(c == NCH - 1))
                ins.then_inc(s.down, 1)

            @block.scalar
            def _(act):
                act.wait_ge(s.loaded, 16 * len(names))
                act.activation(w.A[:, :], w.alog[:, :], ACT.Exp).then_inc(s.consts, 1)
                act.activation(w.alpha[:, :], w.gate[:, :], ACT.Sigmoid).then_inc(s.consts, 1)
                act.wait_ge(s.down, 1)
                act.activation(w.xmid[:, :].rearrange("p (b l) -> p b l", b=NSEQ),
                               g.ps[:, 0, :].rearrange("p (l b) -> p b l", b=NSEQ), ACT.Gelu,
                               bias=w.bd[:, 0:1]).then_inc(s.gelu, 1)

            @block.vector
            def _(dve):
                dve.wait_ge(s.consts, 1)
                dve.tensor_scalar(w.A[:, :], w.A[:, :], -1.0, None, ALU.mult).then_inc(s.step, 1)
        release(nc, s)
        hydra_pass(nc, g, w, "hy1", w.xmid)
        hydra_pass(nc, g, w, "hy2", w.u)

        s = semaphores(nc, st, "hy3", "step blended up added")
        with nc.Block() as block:
            @block.vector
            def _(dve):
                link = chain(dve, s.step)
                link(dve.tensor_scalar(w.ynT[:, 0, :], w.xmid[:, :], w.alpha[:, 0:1], None, ALU.mult))
                link(dve.tensor_scalar(w.ms[:, 0:1], w.alpha[:, :], -1.0, 1.0, ALU.mult, ALU.add))
                link(dve.scalar_tensor_tensor(w.ynT[:, 1, :], w.u[:, :], w.ms[:, 0:1], w.ynT[:, 0, :],
                                              ALU.mult, ALU.add))
                dve.tensor_tensor(w.ynT[:, 0, :].rearrange("p (l b) -> p b l", b=NSEQ),
                                  w.ynT[:, 1, :].rearrange("p (b l) -> p b l", b=NSEQ),
                                  w.xmid[:, :].rearrange("p (b l) -> p b l", b=NSEQ), ALU.add).then_inc(s.blended, 1)
                link(dve.tensor_tensor(flat(g.x), flat(g.x), flat(g.xn), ALU.add))
                for t in range(NT):
                    dve.wait_ge(s.up, t + 1)
                    dve.tensor_tensor(g.x[:, t, :], g.x[:, t, :], g.ps[:, t, :], ALU.add).then_inc(s.added, 1)

            @block.tensor
            def _(pe):
                pe.wait_ge(s.blended, 1)
                for t in range(NT):
                    pe.matmul(g.ps[:, t, :], w.ynT[:, 0, t * P:(t + 1) * P], w.wu[:, :], start=True, stop=False)
                    pe.matmul(g.ps[:, t, :], w.ones[:, :], w.bu[:, :], start=False, stop=True).then_inc(s.up, 1)
        release(nc, s)


def hydra_pass(nc, g, w, name, src):
    with ExitStack() as st:
        s = semaphores(nc, st, name, "step xbc z dt cp e1 e2 sp da spread dab conv silu c0 xst xtok sz gram masked mat "
                 "y gated ms root yn yt ynT out")
        lanes = (P, P, 48)
        with nc.Block() as block:
            @block.tensor
            def _(pe):
                for i in range(2):
                    pe.matmul(g.ps[:, i, :], w.wx[:, i * P:(i + 1) * P], src[:, :], start=True,
                              stop=True).then_inc(s.xbc, 1)
                pe.matmul(g.ps[0:48, 2, :], w.wbc[:, :], src[:, :], start=True, stop=True).then_inc(s.xbc, 1)
                for t in range(NT):
                    pe.matmul(g.ps[:, 4 + t, 0:HIN + 2 * NHH], src[:, t * P:(t + 1) * P], w.wz[:, :], start=True,
                              stop=True).then_inc(s.z, 1)
                pe.wait_ge(s.spread, 1)
                pe.matmul(g.ps[:, 3, :], w.same[:, :], flat(w.spread), start=True, stop=True).then_inc(s.dab, 1)
                pe.wait_ge(s.silu, 2)
                for t in range(NT):
                    for i in range(2):
                        ins = pe.transpose(g.ps[:, t // 2, (t % 2) * HIN + i * P:(t % 2) * HIN + (i + 1) * P],
                                           w.acc[:, i, t * P:(t + 1) * P], g.ident[:, :])
                ins.then_inc(s.xst, 1)
                pe.wait_ge(s.c0, 1)
                for t in range(NT):
                    ins = pe.matmul(g.ps[:, 2, t * P:(t + 1) * P], w.acc[0:NST, 2, t * P:(t + 1) * P],
                                    w.c0[:, t * P:(t + 1) * P], start=True, stop=True)
                ins.then_inc(s.gram, 1)
                pe.wait_ge(s.sz, NT)
                pe.wait_ge(s.xtok, 1)
                for t in range(NT):
                    for i in range(2):
                        pe.matmul(g.ps[:, 4 + t, HIN:HIN + NHH], w.acc[:, i, t * P:(t + 1) * P], w.fcD[:, i, :],
                                  start=(i == 0), stop=(i == 1))
                    pe.wait_ge(s.mat, t + 1)
                    for h in range(NHH):
                        for n, M in enumerate((w.Mf, w.Mb)):
                            ins = pe.matmul(g.ps[:, 4 + t, h * HP:(h + 1) * HP], M[:, t % 2, h, :],
                                            w.xtok[:, t, h * HP:(h + 1) * HP], start=(n == 0), stop=(n == 1))
                    ins.then_inc(s.y, 1)
                for t in range(NT):
                    pe.wait_ge(s.yn, t + 1)
                    for i in range(2):
                        ins = pe.transpose(g.ps[:, i, t * P:(t + 1) * P], w.yz[:, t, i * P:(i + 1) * P], g.ident[:, :])
                ins.then_inc(s.yt, 1)
                for i in range(2):
                    pe.wait_ge(s.ynT, i + 1)
                    ins = pe.matmul(g.ps[:, 2, :], w.wo[:, i, :], w.ynT[:, i, :], start=(i == 0), stop=(i == 1))
                ins.then_inc(s.out, 1)

            @block.scalar
            def _(act):
                for i, n in enumerate(lanes):
                    act.wait_ge(s.xbc, i + 1)
                    act.copy(w.cp[0:n, i, :, PAD:], g.ps[0:n, i, :].rearrange("p (b l) -> p b l", l=SEQ)).then_inc(s.cp, 1)
                act.wait_ge(s.e1, 1)
                act.activation(w.sp[:, 1, :], w.sp[:, 0, :], ACT.Exp, scale=-1.0).then_inc(s.e2, 1)
                act.wait_ge(s.sp, 1)
                act.activation(flat(w.dA), w.sp[:, 3, :], ACT.Exp).then_inc(s.da, 1)
                act.wait_ge(s.dt, 1)
                for t in range(NT):
                    act.activation(w.sz[:, t, :], g.ps[:, 4 + t, 0:HIN], ACT.Silu).then_inc(s.sz, 1)
                for i, n in ((0, P), (1, P), (2, 48)):
                    act.wait_ge(s.conv, i + 1)
                    act.activation(w.acc[0:n, i, :], w.acc[0:n, i, :], ACT.Silu, bias=w.cb[0:n, i:i + 1]).then_inc(s.silu, 1)
                act.wait_ge(s.silu, 3)
                act.copy(w.c0[:, :], w.acc[32:32 + NST, 2, :]).then_inc(s.c0, 1)
                act.wait_ge(s.xst, 1)
                act.copy(w.xtok[:, :, :].rearrange("p (a t) n -> p a (t n)", a=2), g.ps[:, 0:2, :]).then_inc(s.xtok, 1)
                act.wait_ge(s.ms, 1)
                act.activation(w.ms[:, :], w.ms[:, :], ACT.Sqrt, scale=1.0 / HIN, bias=w.eps[:, 0:1]).then_inc(s.root, 1)
                act.wait_ge(s.yt, 1)
                for i in range(2):
                    act.activation(w.ynT[:, i, :], g.ps[:, i, :], ACT.Copy, scale=w.nw[:, i:i + 1]).then_inc(s.ynT, 1)
                act.wait_ge(s.out, 1)
                act.copy(w.u[:, :], g.ps[:, 2, :])

            @block.vector
            def _(dve):
                link = chain(dve, s.step)
                n8 = 2 * NHH
                rows = [w.sp[:, i, :] for i in range(4)]
                tiled = [r.rearrange("p (t k) -> p t k", t=NT) for r in rows]
                dve.wait_ge(s.z, NT)
                dve.tensor_tensor(w.dt[:, :, :], g.ps[:, 4:8, HIN:HIN + n8],
                                  w.dtb[:, None, :].broadcast_to([P, NT, n8]), ALU.add).then_inc(s.dt, 1)
                dve.wait_ge(s.dt, 1)
                dve.scalar_tensor_tensor(rows[0], flat(w.dt), -1.0, flat(w.dt), ALU.mult, ALU.max).then_inc(s.e1, 1)
                dve.wait_ge(s.e2, 1)
                link(dve.tensor_scalar(rows[2], rows[1], 2.0, None, ALU.add))
                link(dve.reciprocal(rows[2], rows[2]))
                link(dve.tensor_tensor(rows[1], rows[1], rows[2], ALU.mult))
                link(dve.tensor_tensor(rows[2], rows[1], rows[1], ALU.mult))
                link(dve.tensor_scalar(rows[3], rows[2], 1.0 / 15, 1.0 / 13, ALU.mult, ALU.add))
                for k in (11, 9, 7, 5, 3, 1):
                    link(dve.tensor_tensor(rows[3], rows[3], rows[2], ALU.mult))
                    link(dve.tensor_scalar(rows[3], rows[3], 1.0 / k, None, ALU.add))
                link(dve.scalar_tensor_tensor(rows[3], rows[3], 2.0, rows[1], ALU.mult, ALU.mult))
                link(dve.scalar_tensor_tensor(flat(w.dt), flat(w.dt), 0.0, rows[3], ALU.max, ALU.add))
                dve.tensor_tensor(tiled[3], w.dt[:, :, :], w.A[:, None, :].broadcast_to([P, NT, n8]),
                                  ALU.mult).then_inc(s.sp, 1)
                dve.wait_ge(s.da, 1)
                for way in range(2):
                    ins = dve.tensor_tensor(
                        w.spread[:, :, way, :, :],
                        w.dA[:, :, way * NHH:(way + 1) * NHH, None].broadcast_to([P, NT, NHH, SEQ]),
                        w.at[:, way:way + 1, None, :].broadcast_to([P, NT, NHH, SEQ]), ALU.mult)
                    if way == 0:
                        link(ins)
                ins.then_inc(s.spread, 1)
                for i, n in enumerate(lanes):
                    dve.wait_ge(s.cp, i + 1)
                    acc = w.acc[0:n, i, :].rearrange("p (b l) -> p b l", l=SEQ)
                    link(dve.tensor_scalar(acc, w.cp[0:n, i, :, 0:SEQ], w.cw[0:n, i, 0:1], None, ALU.mult))
                    for k in range(1, TAPS):
                        ins = dve.scalar_tensor_tensor(acc, w.cp[0:n, i, :, k:k + SEQ], w.cw[0:n, i, k:k + 1], acc,
                                                       ALU.mult, ALU.add)
                        if k < TAPS - 1:
                            link(ins)
                    ins.then_inc(s.conv, 1)
                dve.wait_ge(s.dab, 1)
                dab = g.ps[:, 3, :].rearrange("p (t w h l) -> p t w h l", t=NT, w=2, h=NHH)
                for way in range(2):
                    link(dve.tensor_tensor(w.d0[:, :, way, :, :], dab[:, :, way, :, :],
                                           w.past[:, way:way + 1, None, :].broadcast_to([P, NT, NHH, SEQ]), ALU.mult))
                    link(dve.tensor_tensor(
                        w.d1[:, :, way, :, :],
                        w.dt[:, :, way * NHH:(way + 1) * NHH, None].broadcast_to([P, NT, NHH, SEQ]),
                        w.at[:, way:way + 1, None, :].broadcast_to([P, NT, NHH, SEQ]), ALU.mult))
                link(dve.tensor_tensor_scan(flat(w.L), flat(w.d0), flat(w.d1), 0.0, ALU.mult, ALU.add))
                dve.wait_ge(s.gram, 1)
                dve.tensor_tensor(w.Gm[:, :, :], g.ps[:, 2, :].rearrange("p (t n) -> p t n", t=NT),
                                  w.same[:, None, :].broadcast_to([P, NT, P]), ALU.mult).then_inc(s.masked, 1)
                dve.wait_ge(s.masked, 1)
                for t in range(NT):
                    if t >= 2:
                        dve.wait_ge(s.y, t - 1)
                    dims = [NHH, 8, SEQ - 1]
                    dve.tensor_tensor(custom(w.Mf[:, t % 2], 1, [[P, NHH], [SEQ, 8], [1, SEQ - 1]]),
                                      custom(w.Gm[:, t], 0, [[0, NHH], [SEQ, 8], [1, SEQ - 1]]),
                                      custom(w.L[:, t, 0], 0, [[SEQ, NHH], [0, 8], [1, SEQ - 1]]), ALU.mult)
                    dve.tensor_tensor(custom(w.Mb[:, t % 2], 0, [[P, NHH], [SEQ, 8], [1, SEQ - 1]]),
                                      custom(w.Gm[:, t], 1, [[0, NHH], [SEQ, 8], [1, SEQ - 1]]),
                                      custom(w.L[:, t, 1], SEQ - 2, [[SEQ, NHH], [0, 8], [-1, SEQ - 1]]),
                                      ALU.mult).then_inc(s.mat, 1)
                dve.wait_ge(s.y, NT)
                dve.wait_ge(s.xtok, 1)
                dve.wait_ge(s.sz, NT)
                heads = lambda a: a.rearrange("p t (h n) -> p (t h) n", h=NHH)
                link(dve.tensor_tensor(w.f[:, :, :], g.ps[:, 4:8, HIN:HIN + NHH],
                                       w.D[:, None, :].broadcast_to([P, NT, NHH]), ALU.add))
                link(dve.tensor_tensor(heads(w.yz[:, :, :]), heads(w.xtok[:, :, :]),
                                       flat(w.f)[:, :, None].broadcast_to([P, NT * NHH, HP]), ALU.mult))
                link(dve.tensor_tensor(w.yz[:, :, :], w.yz[:, :, :], g.ps[:, 4:8, 0:HIN], ALU.add))
                link(dve.tensor_tensor(w.yz[:, :, :], w.yz[:, :, :], w.sz[:, :, :], ALU.mult))
                link(dve.tensor_tensor(w.y2[:, :, :], w.yz[:, :, :], w.yz[:, :, :], ALU.mult))
                dve.tensor_reduce(w.ms[:, :], w.y2[:, :, :], AX.X, ALU.add).then_inc(s.ms, 1)
                dve.wait_ge(s.root, 1)
                link(dve.reciprocal(w.ms[:, :], w.ms[:, :]))
                for t in range(NT):
                    dve.tensor_scalar(w.yz[:, t, :], w.yz[:, t, :], w.ms[:, t:t + 1], None, ALU.mult).then_inc(s.yn, 1)
        release(nc, s)


def store_result(nc, g, d):
    with ExitStack() as st:
        s = semaphores(nc, st, "fin", "stored")
        with nc.Block() as block:
            @block.sync
            def _(sp):
                for t in range(NT):
                    sp.dma_start(d.out[t * P:(t + 1) * P, :], g.x[:, t, :]).then_inc(s.stored, 16)
                sp.wait_ge(s.stored, 16 * NT)


_SCRATCH = {
    "q_scratch": ((LAT, 3, DIM), "int32"),
    "keys_hi": ((LAT, METHODS, DIM), "float32"),
    "keys_lo": ((LAT, METHODS, DIM), "float32"),
    "xatt": ((ROWS, DIM), "float32"),
    "v_lat": ((ROWS, KV_HEADS * P), "float32"),
}


def program(nc, d):
    with ExitStack() as st:
        shared = tensors(nc, st, "g", (("x", [P, NT, DIM], F32), ("xn", [P, NT, DIM], F32), ("xnT", [P, NCH, ROWS], F32),
                                ("ident", [P, P], F32), ("identb", [P, P], BF16), ("eps", [P, 1], F32)))
        shared["ps"] = st.enter_context(nc.psum_tensor("ps", [P, 8, 512], F32))
        with ExitStack() as sa:
            g = named(shared | tensors(nc, sa, "g", (("targets", [P, DIM + EXTRA], F16), ("mask", [P, U_MAX, HD], BF16),
                                    ("avg1", [P, P], F32), ("avg2", [P, P], F32),
                                    ("key_hi", [P, NCH, LAT * METHODS], F32),
                                    ("key_lo", [P, NCH, LAT * METHODS], F32))))
            load_constants(nc, g, d)
            layernorm_and_turn(nc, g, "ln0")
            curve_keys(nc, g, d)
            graph_layers(nc, g, d)
        g = named(shared)
        add_point_attention(nc, g, d)
        layernorm_and_turn(nc, g, "ln1")
        bound_attention(nc, g, d)
        layernorm_and_turn(nc, g, "ln2")
        experts(nc, g, d, "e0", 0, 2.0, None)
        layernorm_and_turn(nc, g, "ln3")
        cross_attention(nc, g, d)
        layernorm_and_turn(nc, g, "ln4")
        hydra(nc, g, d)
        layernorm_and_turn(nc, g, "ln5")
        experts(nc, g, d, "e1", 4 * EXPERTS, 1.0 / RANK, 3 * ROWS // EXPERTS)
        store_result(nc, g, d)


def _layout(i):
    f = np.float32
    out = {}
    out["x"] = np.asarray(i["x"]).reshape(ROWS, DIM)
    out["coords"] = np.ascontiguousarray(np.asarray(i["ctx_4096"])[:, 0:3, :])
    out["ident"] = np.eye(P, dtype=f)
    t = list(range(DIM)) + [DIM - 1] * TAIL
    for n in range(HEAD_POINTS):
        t += [min(j, n + KNN // 2) for j in range(KNN)]
    out["targets"] = np.array(t, f)
    j = np.arange(HD) // KNN
    out["pointmask"] = np.where(j[np.arange(P) % HD][:, None] == j[None, :], 0.0, -BIG).astype(f)
    q = np.arange(P)
    out["avg1"] = (0.25 * (q[:, None] % 32 == q[None, :] % 32)).astype(f)
    out["avg2"] = (0.25 * (q[:, None] % 64 == q[None, :] % 64)).astype(f)
    out["nidx"] = ((q % 8)[:, None] * 64 + np.arange(64)[None, :]).astype(np.int32)
    for l, (perm, name) in enumerate((([2, 0, 3, 1], "1"), ([1, 3, 0, 2], "2"))):
        place = [perm.index(m) for m in range(METHODS)]
        lin = np.asarray(i[f"L0_xattn_W_lin{name}"]).reshape(64, 2, HEADS, 8, METHODS)
        out[f"lin{l}"] = np.ascontiguousarray(lin[:, :, :, :, place].transpose(0, 1, 2, 4, 3).reshape(64, 2, P))
        conv = np.asarray(i[f"L0_xattn_W_conv{name}"])
        out[f"conv{l}"] = np.ascontiguousarray(np.tile(conv.T, (1, P // OUTS[l])))
        out[f"lbias{l}"] = np.asarray(i[f"L0_xattn_b_lin{name}"]).reshape(64, 1)
    w3 = np.asarray(i["L0_xattn_W_conv3"])
    for name, at in (("w3a", 0), ("w3b", 32)):
        z = np.zeros((HEADS, METHODS, 8, 32), f)
        z[:, 0] = w3[:, at:at + 32].T.reshape(HEADS, 8, 32)
        out[name] = z.reshape(P, 32)
    z = np.zeros((2, 64, 2, 32), f)
    for c in range(2):
        z[c, :, c, :] = w3[:, 64:].T
    out["w3c"] = z.reshape(P, 2, 32)
    A = lambda n: np.asarray(i[n])

    def chunked(wt):
        return np.ascontiguousarray(wt.reshape(NCH, P, -1).transpose(1, 0, 2))

    out["bind"] = np.ascontiguousarray(np.stack([A("L0_attn_bv_q"), A("L0_attn_bv_k"), A("L0_attn_bv_v")], 1))
    out["sel4"] = np.ascontiguousarray(np.broadcast_to(np.eye(NCH, dtype=f)[:, :, None], (NCH, NCH, P)))
    out["causal"] = ((q[:, None] // TOK == q[None, :] // TOK) & (q[:, None] <= q[None, :])).astype(f)
    out["iota8"] = np.arange(EXPERTS).astype(f)
    out["e0_wa"] = chunked(np.concatenate([A("L0_ffn_gate_w").T, A("L0_ffn_lora_A").reshape(P, DIM).T], 1))
    out["e0_wb"] = chunked(A("L0_ffn_base_w").T)
    out["e0_bias"] = A("L0_ffn_base_b").reshape(1, DIM)
    out["e0_lb"] = np.ascontiguousarray(A("L0_ffn_lora_B").transpose(0, 2, 1).reshape(P, DIM))
    out["e1_wa"] = chunked(np.concatenate([A("L1_ffn_gw1").T, A("L1_ffn_lora_A").transpose(1, 0, 2).reshape(DIM, P)], 1))
    out["e1_wb"] = chunked(A("L1_ffn_weight").T)
    out["e1_bias"] = np.zeros((1, DIM), f)
    out["e1_lb"] = np.ascontiguousarray(A("L1_ffn_lora_B").reshape(P, DIM))
    out["e1_rows"] = np.stack([A("L1_ffn_gb1"), A("L1_ffn_ln_gamma"), A("L1_ffn_ln_beta")])
    out["e1_gb2"] = A("L1_ffn_gb2")
    out["e1_gw2"] = np.ascontiguousarray(A("L1_ffn_gw2").T)
    out["ctxT"] = np.ascontiguousarray(A("ctx_4096").transpose(0, 2, 1).reshape(LAT, NCH, P, CTX).transpose(0, 2, 1, 3))
    out["wq"], out["wk"], out["wv"] = (chunked(A("L1_xattn_" + n)) for n in ("Wq", "Wk", "Wv"))
    out["wo"] = np.ascontiguousarray(A("L1_xattn_Wo").reshape(Q_HEADS, P, DIM).transpose(1, 0, 2))
    out["qk_norm"] = np.ascontiguousarray(np.stack([A("L1_xattn_q_norm_w"), A("L1_xattn_k_norm_w")], 1))
    out["mean128"] = np.full((P, P), 1.0 / P, f)
    H = lambda n: A("L1_attn_" + n)
    out["hy_wd"] = chunked(H("w_down").T)
    out["hy_bd"] = H("b_down").reshape(HM, 1)
    out["hy_gate"] = H("gate1").reshape(1)
    out["hy_wu"] = np.ascontiguousarray(H("w_up").T)
    out["hy_bu"] = H("b_up").reshape(1, DIM)
    win = H("hy_in_w").T
    X0, B0, C0, D0 = HIN, 2 * HIN, 2 * HIN + NST, 2 * HIN + 2 * NST
    gap = np.zeros((HM, 32 - NST), f)
    out["hy_wx"] = np.ascontiguousarray(win[:, X0:B0])
    out["hy_wbc"] = np.concatenate([win[:, B0:C0], gap, win[:, C0:D0]], 1)
    out["hy_wz"] = np.concatenate([win[:, 0:X0], win[:, D0:]], 1)

    def channels(v):
        z = np.zeros((P, 3, v.shape[1]), f)
        z[:, 0], z[:, 1] = v[0:P], v[P:2 * P]
        z[0:NST, 2], z[32:32 + NST, 2] = v[HIN:HIN + NST], v[HIN + NST:]
        return z
    out["hy_cw"] = channels(H("hy_conv_w")[:, 0, :])
    out["hy_cb"] = channels(H("hy_conv_b")[:, None])[:, :, 0]
    out["hy_dtb"] = np.tile(H("hy_dt_bias"), 2)
    out["hy_alog"] = np.tile(H("hy_A_log"), 2)
    out["hy_D"] = H("hy_D")
    out["hy_fcD"] = np.ascontiguousarray(H("hy_fcD_w").T.reshape(2, P, NHH).transpose(1, 0, 2))
    out["hy_nw"] = np.ascontiguousarray(H("hy_norm_w").reshape(2, P).T)
    out["hy_wo"] = np.ascontiguousarray(H("hy_out_w").T.reshape(2, P, HM).transpose(1, 0, 2))
    out["hy_same"] = (q[:, None] // SEQ == q[None, :] // SEQ).astype(f)
    pos, col = (q % SEQ)[:, None], np.arange(SEQ)[None, :]
    out["hy_at"] = np.stack([pos == col, pos == SEQ - 1 - col], 1).astype(f)
    out["hy_past"] = np.stack([col > pos, SEQ - 1 - col < pos], 1).astype(f)
    return out


def kernel(**inputs):
    import concourse.bacc as _bacc
    from concourse.bass_utils import run_bass_kernel_spmd as _run

    nc = _bacc.Bacc("TRN2", target_bir_lowering=False, num_devices=1)
    tensor, arrays = {}, {}
    for name, a in _layout(inputs).items():
        arrays["in_" + name] = a
        tensor[name] = nc.dram_tensor("in_" + name, a.shape, mybir.dt.from_np(a.dtype), kind="ExternalInput").ap()
    for name, (shape, dt) in _SCRATCH.items():
        tensor[name] = nc.dram_tensor("scratch_" + name, shape, mybir.dt.from_np(np.dtype(dt)), kind="Internal").ap()
    tensor["out"] = nc.dram_tensor("out_0_dram", (ROWS, DIM), F32, kind="ExternalOutput").ap()
    program(nc, named(tensor))
    r = _run(nc, [arrays], core_ids=[0])
    return r.results[0]["out_0_dram"].reshape(LAT, TOK, DIM)
```

```python
from contextlib import ExitStack

import numpy as np

import concourse.bass as bass
from concourse import mybir

F32 = mybir.dt.float32
F16 = mybir.dt.float16
BF16 = mybir.dt.bfloat16
I32 = mybir.dt.int32
U32 = mybir.dt.uint32
ALU = mybir.AluOpType
ACT = mybir.ActivationFunctionType
AX = mybir.AxisListType

P = 128
LAT, TOK, DIM = 16, 32, 512
ROWS = LAT * TOK
NT = ROWS // P
NCH = DIM // P
LN_EPS = 1e-5

BITS = 10
METHODS = 4
KNN = 10
C_IN = 32
HEADS = 4
HD = 32
NS = 2
U_ALL = 43
BATCH_U = (8, 8, 8, 8, 8, 3)
U_MAX = 8
NB = len(BATCH_U)
SC = HEADS * U_MAX * HD
BLK = 3 * KNN
F_LEFT = KNN // 2
F_COLS = F_LEFT + DIM + 8
TAIL = KNN // 2 - 1
HEAD_POINTS = KNN // 2
EXTRA = TAIL + HEAD_POINTS * KNN
BIG = float(2 ** 20)
OUTS = (32, 64)
INV_SQRT_HD = float(1.0 / np.sqrt(np.float32(HD)))


def chain(eng, sem):
    count = [0]

    def link(ins):
        count[0] += 1
        ins.then_inc(sem, 1)
        eng.wait_ge(sem, count[0])
    return link


def named(items):
    return type("Named", (), {"all": items, **items})


def semaphores(nc, stack, stage, names):
    return named({n: stack.enter_context(nc.semaphore(f"{stage}_{n}")) for n in names.split()})


def tensors(nc, stack, stage, specs):
    return {n: stack.enter_context(nc.sbuf_tensor(f"{stage}_{n}", shape, dt)) for n, shape, dt in specs}


def release(nc, s):
    for sem in s.all.values():
        nc.sync.sem_clear(sem)
    nc.all_engine_barrier()


def custom(ap, offset, dims):
    return bass.AP(ap.tensor, ap.offset + offset, [list(ap.ap[0])] + dims)


def load_constants(nc, g, d):
    with ExitStack() as st:
        s = semaphores(nc, st, "const", "loaded step")
        tgt_f = st.enter_context(nc.sbuf_tensor("tgt_f", [P, DIM + EXTRA], F32))
        msk_f = st.enter_context(nc.sbuf_tensor("msk_f", [P, HD], F32))
        with nc.Block() as block:
            @block.sync
            def _(sp):
                sp.dma_start(g.ident[:, :], d.ident).then_inc(s.loaded, 16)
                sp.dma_start(tgt_f[:, :], d.targets.partition_broadcast(P)).then_inc(s.loaded, 16)
                sp.dma_start(msk_f[:, :], d.pointmask).then_inc(s.loaded, 16)
                sp.dma_start(g.avg1[:, :], d.avg1).then_inc(s.loaded, 16)
                sp.dma_start(g.avg2[:, :], d.avg2).then_inc(s.loaded, 16)
                for t in range(NT):
                    sp.dma_start(g.x[:, t, :], d.x[t * P:(t + 1) * P, :]).then_inc(s.loaded, 16)

            @block.vector
            def _(dve):
                dve.memset(g.eps[:, :], LN_EPS).then_inc(s.step, 1)
                dve.wait_ge(s.loaded, 16 * (5 + NT))
                dve.tensor_copy(g.identb[:, :], g.ident[:, :]).then_inc(s.step, 1)
                dve.tensor_copy(g.ident16[:, :], g.ident[:, :]).then_inc(s.step, 1)
                dve.tensor_copy(g.targets[:, :], tgt_f[:, :]).then_inc(s.step, 1)
                dve.tensor_copy(g.mask[:, :, :],
                                msk_f[:, None, :].broadcast_to([P, 2 * U_MAX, HD])).then_inc(s.step, 1)
        release(nc, s)


def layernorm_and_turn(nc, g, name):
    with ExitStack() as st:
        s = semaphores(nc, st, name, "step var root rstd normed turned copied")
        stats = st.enter_context(nc.sbuf_tensor(f"{name}_stats", [P, NT, 6], F32))
        mv = st.enter_context(nc.sbuf_tensor(f"{name}_mv", [P, NT, 2], F32))
        root = st.enter_context(nc.sbuf_tensor(f"{name}_root", [P, NT], F32))
        rstd = st.enter_context(nc.sbuf_tensor(f"{name}_rstd", [P, NT], F32))
        with nc.Block() as block:
            @block.vector
            def _(dve):
                for t in range(NT):
                    dve.bn_stats(stats[:, t, :], g.x[:, t, :]).then_inc(s.step, 1)
                for t in range(NT):
                    dve.wait_ge(s.step, t + 1)
                    dve.bn_aggr(mv[:, t, :], stats[:, t, :]).then_inc(s.var, 1)
                dve.wait_ge(s.root, 1)
                dve.wait_ge(s.var, NT)
                dve.reciprocal(rstd[:, :], root[:, :]).then_inc(s.rstd, 1)
                dve.wait_ge(s.rstd, 1)
                for t in range(NT):
                    dve.tensor_scalar(g.xn[:, t, :], g.x[:, t, :], mv[:, t, 0:1], rstd[:, t:t + 1],
                                      ALU.subtract, ALU.mult).then_inc(s.normed, 1)

            @block.scalar
            def _(act):
                act.wait_ge(s.var, NT)
                act.activation(root[:, :], mv[:, :, 1], ACT.Sqrt, bias=g.eps[:, 0:1]).then_inc(s.root, 1)
                for t in range(NT):
                    act.wait_ge(s.turned, t + 1)
                    act.copy(g.xnT[:, :, t * P:(t + 1) * P],
                             g.ps[:, t, :].rearrange("p (c r) -> p c r", c=NCH)).then_inc(s.copied, 1)

            @block.tensor
            def _(pe):
                for t in range(NT):
                    pe.wait_ge(s.normed, t + 1)
                    for c in range(NCH):
                        ins = pe.transpose(g.ps[:, t, c * P:(c + 1) * P], g.xn[:, t, c * P:(c + 1) * P],
                                           g.ident[:, :])
                    ins.then_inc(s.turned, 1)
        release(nc, s)


def curve_keys(nc, g, d):
    B, N8, NC8 = LAT, 8, DIM // 8
    with ExitStack() as st:
        def sb(name, shape, dt):
            return st.enter_context(nc.sbuf_tensor(name, shape, dt))
        s = semaphores(nc, st, "keys", "loaded step stored quantised reloaded keyed written back turned")
        co = sb("co", [B, 3, DIM], F32)
        lo = sb("c_lo", [B, 3], F32)
        hi = sb("c_hi", [B, 3], F32)
        w = sb("c_w", [B, 12, 3], F32)
        fl = sb("c_fl", [B, 3, DIM], F32)
        gt = sb("c_gt", [B, 3, DIM], F32)
        qi = sb("c_qi", [B, 3, DIM], I32)
        q = sb("q8", [P, 3, NC8], I32)
        nidx = sb("nidx", [P, NC8], I32)
        X = sb("hX", [P, 3, METHODS, NC8], I32)
        M = sb("hM", [P, 2, NC8], I32)
        N = sb("hN", [P, 2, NC8], I32)
        T = sb("hT", [P, 2, NC8], I32)
        S = sb("hS", [P, 3, METHODS, NC8], I32)
        K = sb("hK", [P, METHODS, NC8], I32)
        KH = sb("hKH", [P, METHODS, NC8], I32)
        KL = sb("hKL", [P, METHODS, NC8], I32)
        FH = sb("fH", [P, METHODS, NC8], F32)
        FL = sb("fL", [P, METHODS, NC8], F32)
        rows = sb("krows", [LAT * METHODS, 2, DIM], F32)
        with nc.Block() as block:
            @block.sync
            def _(sp):
                sp.dma_start(co[:, :, :], d.coords).then_inc(s.loaded, 16)
                sp.dma_start(nidx[:, :], d.nidx).then_inc(s.loaded, 16)
                sp.wait_ge(s.quantised, 1)
                sp.dma_start(d.q_scratch, qi[:, :, :]).then_inc(s.stored, 16)
                sp.wait_ge(s.stored, 16)
                for b in range(B):
                    sp.dma_start(q[b * N8:(b + 1) * N8, :, :],
                                 d.q_scratch[b].rearrange("c (a n) -> a c n", a=N8)).then_inc(s.reloaded, 16)
                sp.wait_ge(s.keyed, 1)
                for b in range(B):
                    sp.dma_start(d.keys_hi[b].rearrange("m (a n) -> a m n", a=N8),
                                 FH[b * N8:(b + 1) * N8, :, :]).then_inc(s.written, 16)
                    sp.dma_start(d.keys_lo[b].rearrange("m (a n) -> a m n", a=N8),
                                 FL[b * N8:(b + 1) * N8, :, :]).then_inc(s.written, 16)
                sp.wait_ge(s.written, 32 * B)
                sp.dma_start(rows[:, 0, :], d.keys_hi.rearrange("b m n -> (b m) n")).then_inc(s.back, 16)
                sp.dma_start(rows[:, 1, :], d.keys_lo.rearrange("b m n -> (b m) n")).then_inc(s.back, 16)

            @block.vector
            def _(dve):
                link = chain(dve, s.step)
                dve.wait_ge(s.loaded, 32)
                link(dve.tensor_reduce(lo[:, :], co[:, :, :], AX.X, ALU.min))
                link(dve.tensor_reduce(hi[:, :], co[:, :, :], AX.X, ALU.max))
                den, r, q0, qh, ql, dh, dl, e = (w[:, i, :] for i in range(8))
                link(dve.tensor_tensor(hi[:, :], hi[:, :], lo[:, :], ALU.subtract))
                link(dve.tensor_scalar(den, hi[:, :], 1e-6, None, ALU.add))
                link(dve.reciprocal(r, den))
                link(dve.tensor_scalar(q0, r, float(2 ** BITS - 1), None, ALU.mult))
                for whole, high, low in ((q0, qh, ql), (den, dh, dl)):
                    link(dve.tensor_scalar(high.bitcast(I32), whole.bitcast(I32), -4096, None,
                                           ALU.bitwise_and))
                    link(dve.tensor_tensor(low, whole, high, ALU.subtract))
                link(dve.tensor_tensor(e, qh, dh, ALU.mult))
                link(dve.tensor_scalar(e, e, -1.0, float(2 ** BITS - 1), ALU.mult, ALU.add))
                for a, b in ((qh, dl), (ql, dh), (ql, dl)):
                    link(dve.tensor_tensor(w[:, 8, :], a, b, ALU.mult))
                    link(dve.tensor_tensor(e, e, w[:, 8, :], ALU.subtract))
                link(dve.tensor_tensor(e, e, r, ALU.mult))
                link(dve.tensor_tensor(q0, q0, e, ALU.add))
                for c in range(3):
                    link(dve.tensor_scalar(co[:, c, :], co[:, c, :], lo[:, c:c + 1], w[:, 2, c:c + 1],
                                           ALU.subtract, ALU.mult))
                link(dve.tensor_copy(qi[:, :, :], co[:, :, :]))
                link(dve.tensor_copy(fl[:, :, :], qi[:, :, :]))
                link(dve.tensor_tensor(gt[:, :, :], fl[:, :, :], co[:, :, :], ALU.is_gt))
                link(dve.tensor_tensor(fl[:, :, :], fl[:, :, :], gt[:, :, :], ALU.subtract))
                link(dve.tensor_scalar(fl[:, :, :], fl[:, :, :], 0.0, float(2 ** BITS - 1), ALU.max, ALU.min))
                dve.tensor_copy(qi[:, :, :], fl[:, :, :]).then_inc(s.quantised, 1)
                dve.wait_ge(s.reloaded, 16 * B)
                for m in range(METHODS):
                    for c in range(3):
                        link(dve.tensor_copy(X[:, c, m, :], q[:, (1 - c if m % 2 and c < 2 else c), :]))
                H = [X[:, c, 2:4, :] for c in range(3)]

                def sign_of_bit(src, bit):
                    link(dve.tensor_scalar(M[:, :, :], src, 31 - bit, 31, ALU.logical_shift_left,
                                           ALU.arith_shift_right))

                for bit in range(BITS - 1, 0, -1):
                    low = (1 << bit) - 1
                    sign_of_bit(H[0], bit)
                    link(dve.scalar_tensor_tensor(H[0], M[:, :, :], low, H[0], ALU.bitwise_and, ALU.bitwise_xor))
                    for c in (1, 2):
                        sign_of_bit(H[c], bit)
                        link(dve.tensor_scalar(N[:, :, :], M[:, :, :], -1, low, ALU.bitwise_xor, ALU.bitwise_and))
                        link(dve.tensor_tensor(T[:, :, :], H[0], H[c], ALU.bitwise_xor))
                        link(dve.tensor_tensor(T[:, :, :], T[:, :, :], N[:, :, :], ALU.bitwise_and))
                        link(dve.scalar_tensor_tensor(M[:, :, :], M[:, :, :], low, H[0], ALU.bitwise_and,
                                                      ALU.bitwise_xor))
                        link(dve.tensor_tensor(H[0], M[:, :, :], T[:, :, :], ALU.bitwise_xor))
                        link(dve.tensor_tensor(H[c], H[c], T[:, :, :], ALU.bitwise_xor))
                link(dve.tensor_tensor(H[1], H[1], H[0], ALU.bitwise_xor))
                link(dve.tensor_tensor(H[2], H[2], H[1], ALU.bitwise_xor))
                link(dve.memset(T[:, :, :], 0))
                for bit in range(BITS - 1, 0, -1):
                    sign_of_bit(H[2], bit)
                    link(dve.scalar_tensor_tensor(T[:, :, :], M[:, :, :], (1 << bit) - 1, T[:, :, :],
                                                  ALU.bitwise_and, ALU.bitwise_xor))
                for c in range(3):
                    link(dve.tensor_tensor(H[c], H[c], T[:, :, :], ALU.bitwise_xor))
                for shift, keep in ((16, 0x030000FF), (8, 0x0300F00F), (4, 0x030C30C3), (2, 0x09249249)):
                    link(dve.scalar_tensor_tensor(S[:, :, :, :], X[:, :, :, :], shift, X[:, :, :, :],
                                                  ALU.logical_shift_left, ALU.bitwise_or))
                    link(dve.tensor_scalar(X[:, :, :, :], S[:, :, :, :], keep, None, ALU.bitwise_and))
                link(dve.scalar_tensor_tensor(K[:, :, :], X[:, 0, :, :], 1, X[:, 1, :, :],
                                              ALU.logical_shift_left, ALU.bitwise_or))
                link(dve.scalar_tensor_tensor(K[:, :, :], K[:, :, :], 1, X[:, 2, :, :],
                                              ALU.logical_shift_left, ALU.bitwise_or))
                link(dve.tensor_scalar(KH[:, :, :], K[:, :, :], 15, None, ALU.logical_shift_right))
                link(dve.tensor_scalar(KL[:, :, :], K[:, :, :], 32767, 9, ALU.bitwise_and,
                                       ALU.logical_shift_left))
                link(dve.tensor_tensor(KL[:, :, :], KL[:, :, :],
                                       nidx[:, None, :].broadcast_to([P, METHODS, NC8]), ALU.bitwise_or))
                link(dve.tensor_scalar(FH[:, :, :], KH[:, :, :], float(2 ** 24), None, ALU.mult))
                dve.tensor_scalar(FL[:, :, :], KL[:, :, :], -1.0, None, ALU.mult).then_inc(s.keyed, 1)

            @block.tensor
            def _(pe):
                pe.wait_ge(s.back, 32)
                n = LAT * METHODS
                for half in range(2):
                    for c in range(NCH):
                        ins = pe.transpose(g.ps[:, half, c * n:(c + 1) * n], rows[:, half, c * P:(c + 1) * P],
                                           g.ident[0:n, 0:n])
                ins.then_inc(s.turned, 1)

            @block.scalar
            def _(act):
                n = LAT * METHODS
                act.wait_ge(s.turned, 1)
                act.copy(g.key_hi[:, :, :], g.ps[:, 0, 0:NCH * n].rearrange("p (c n) -> p c n", c=NCH))
                act.mul(g.key_lo[:, :, :], g.ps[:, 1, 0:NCH * n].rearrange("p (c n) -> p c n", c=NCH), -1.0)
        release(nc, s)


def graph_weights(nc, g, d, w):
    with ExitStack() as st:
        s = semaphores(nc, st, "gw", "loaded step zeroed multiplied split")
        e, rows = flat(w.e), flat(w.row_hi)
        lin = [e[0:64, 256 * l:256 * (l + 1)].rearrange("p (a n) -> p a n", a=2) for l in range(2)]
        conv = [e[0:64, 512 + P * l:512 + P * (l + 1)] for l in range(2)]
        bias = [e[0:64, 768 + l:769 + l] for l in range(2)]
        cf = [rows[:, 512 * l:512 * (l + 1)].rearrange("p (c o) -> p c o", c=4) for l in range(2)]
        zeroed = (cf[0], cf[1], w.spread, w.x16, w.sorted, w.centre, w.centre16, w.xT)
        with nc.Block() as block:
            @block.sync
            def _(sp):
                for l in range(2):
                    sp.dma_start(lin[l], d.all[f"lin{l}"]).then_inc(s.loaded, 16)
                    sp.dma_start(conv[l], d.all[f"conv{l}"]).then_inc(s.loaded, 16)
                    sp.dma_start(bias[l], d.all[f"lbias{l}"]).then_inc(s.loaded, 16)
                sp.dma_start(w.w3a[:, :], d.w3a).then_inc(s.loaded, 16)
                sp.dma_start(w.w3b[:, :], d.w3b).then_inc(s.loaded, 16)
                sp.dma_start(w.w3c[:, :, :], d.w3c).then_inc(s.loaded, 16)

            @block.gpsimd
            def _(pool):
                for t in zeroed:
                    pool.memset(flat(t), 0.0).then_inc(s.zeroed, 1)
                pool.memset(w.half[:, :], -0.5)

            @block.tensor
            def _(pe):
                pe.wait_ge(s.loaded, 16 * 9)
                for l in range(2):
                    for half in range(2):
                        pe.matmul(g.ps[:, 2 * l + half, 0:OUTS[l]], lin[l][:, half, :], conv[l][:, 0:OUTS[l]],
                                  start=True, stop=True)
                    ins = pe.matmul(g.ps[:, 4 + l, 0:1], conv[l], bias[l], start=True, stop=True)
                ins.then_inc(s.multiplied, 1)

            @block.vector
            def _(dve):
                link = chain(dve, s.step)
                dve.wait_ge(s.multiplied, 1)
                dve.wait_ge(s.zeroed, len(zeroed))
                for l in range(2):
                    o = OUTS[l]
                    link(dve.tensor_copy(w.bias[:, l:l + 1], g.ps[:, 4 + l, 0:1]))
                    link(dve.tensor_copy(w.wnei[l][:, :], g.ps[:, 2 * l + 1, 0:o]))
                    for h in range(HEADS):
                        at = (h * o) % P
                        link(dve.tensor_copy(cf[l][:, h, at:at + o], g.ps[:, 2 * l, 0:o]))
                    whole, parts = flat(cf[l]), w.wcen[l]
                    for p in range(3):
                        link(dve.tensor_copy(flat(parts[:, p]), whole))
                        if p < 2:
                            link(dve.tensor_tensor(whole, whole, flat(parts[:, p]), ALU.subtract))
        release(nc, s)


def flat(t):
    ap = t if isinstance(t, bass.AP) else t[tuple([slice(None)] * len(t.shape))]
    names = "abcdef"[:len(ap.shape) - 1]
    return ap if len(names) == 1 else ap.rearrange(f"p {' '.join(names)} -> p ({' '.join(names)})")


def graph_layers(nc, g, d):
    with ExitStack() as st:
        w = named(tensors(nc, st, "a", (
            ("w3a", [P, 32], F32), ("w3b", [P, 32], F32), ("w3c", [P, 2, 32], F32), ("bias", [P, 2], F32),
            ("spread", [P, 3, NCH, METHODS, P], BF16),
            ("x16", [P, 2, U_MAX, 4, HD], F16),
            ("xT", [P, 3, U_MAX, P], F16),
            ("sorted", [P, 2, F_COLS], F32),
            ("first", [P, 2, HEAD_POINTS, KNN], F32),
            ("centre", [P, 2, NS, DIM + 8], F32), ("centre16", [P, 2, DIM + 8], F16),
            ("perm", [P, NS, METHODS, NCH, DIM + EXTRA], BF16),
            ("row_hi", [P, METHODS, DIM], F32), ("row_lo", [P, METHODS, DIM], F32),
            ("key_b", [P, 2, NCH, METHODS], F32), ("above", [P, 2, DIM], F32), ("less", [P, 2, DIM], BF16),
            ("rank", [P, METHODS * NCH], F32),
            ("fn", [P, NS, NCH, C_IN], F32), ("rest", [P, NCH, C_IN], F32), ("parts", [P, 3, NCH, C_IN], BF16),
            ("e", [P, 2, SC], F32),
            ("pair", [P, 2, SC], F32), ("pairT", [P, 2, SC], F32),
            ("rmax", [P, 2, SC // HD], F32), ("rsum", [P, 2, SC // HD], F32),
            ("att", [P, 2, 4, U_MAX, HD], F32),
            ("low", [P, 2, 4, U_MAX // 2, HD], F32),
            ("cterm", [P, 2, 2, 132], F32),
            ("h", [P, 2, U_MAX * BLK], F32),
            ("stats", [P, 2, 2, NB, 6], F32), ("mv", [P, 2, 2], F32), ("mean", [P, 1], F32), ("meanb", [P, 1], F32),
            ("dev", [P, 2, 2], F32), ("var", [P, 1], F32), ("rstd", [P, 1], F32), ("half", [P, 1], F32),
            ("peak", [P, 2, 2, 3 * (U_ALL + 1)], F32), ("f", [P, 2, P], F32),
            ("o32", [32, 2, DIM], F32), ("st3", [32, 6], F32), ("mv3", [32, 2], F32), ("r3", [32, 1], F32))))
        w.wnei = [st.enter_context(nc.sbuf_tensor(f"a_wnei{l}", [P, OUTS[l]], F32)) for l in range(2)]
        w.wcen = [st.enter_context(nc.sbuf_tensor(f"a_wcen{l}", [P, 3, 4, P], BF16)) for l in range(2)]
        graph_weights(nc, g, d, w)
        for x in range(NS):
            s = semaphores(nc, st, f"rank{x}", "rows keyb step ranked perm")
            with nc.Block() as block:
                @block.sync
                def _(sp):
                    load_rows(sp, d, w, s, x)

                @block.vector
                def _(dve):
                    key_columns(dve, g, w, s, x, 0)
                    for i in range(METHODS * NCH):
                        rank_unit(dve, g, w, s, x, i, 0)
            release(nc, s)
        s = semaphores(nc, st, "graph", "gathered sorted x16 turned xT scored shifted exped normed hi lo attn part lows "
                       "summed b7w b7r moments dev var rstd f parts spread rows_of dstep pstep rows keyb ranked perm out stored")
        with nc.Fori(0, LAT // NS) as it:
            graph_rows(nc, g, d, w, s, it)


def load_rows(sp, d, w, s, b):
    sp.dma_start(w.row_hi[:, :, :], bcast_rows(d.keys_hi, b)).then_inc(s.rows, 16)
    sp.dma_start(w.row_lo[:, :, :], bcast_rows(d.keys_lo, b)).then_inc(s.rows, 16)


def key_columns(dve, g, w, s, b, n):
    for i, key in enumerate((g.key_hi, g.key_lo)):
        dve.tensor_copy(w.key_b[:, i, :, :], key[:, :, bass.ds(b * METHODS, METHODS)]).then_inc(s.keyb, 1)
    dve.wait_ge(s.keyb, 2 * n + 2)
    dve.wait_ge(s.rows, 32 * (n + 1))


def rank_unit(dve, g, w, s, x, i, n):
    m, c = i // NCH, i % NCH
    count = n * METHODS * NCH + i
    dve.tensor_scalar(w.above[:, i % 2, :], w.row_hi[:, m, :], w.key_b[:, 0, c, m:m + 1], None,
                      ALU.subtract).then_inc(s.ranked, 1)
    dve.wait_ge(s.ranked, 2 * count + 1)
    dve.scalar_tensor_tensor(w.less[:, i % 2, :], w.above[:, i % 2, :], w.key_b[:, 1, c, m:m + 1],
                             w.row_lo[:, m, :], ALU.subtract, ALU.is_lt,
                             accum_out=w.rank[:, i:i + 1]).then_inc(s.ranked, 1)
    dve.wait_ge(s.ranked, 2 * count + 2)
    dve.tensor_scalar(w.perm[:, x, m, c, :], g.targets[:, :], w.rank[:, i:i + 1], None,
                      ALU.is_equal).then_inc(s.perm, 1)


def graph_rows(nc, g, d, w, s, it):
    runs = 2 * NS
    NQ = runs * NB
    steps = NQ + 5
    quarter = U_MAX // 2
    halves = [(q, h) for q in range(NQ) for h in range(2) if BATCH_U[q % NB] > quarter * h]
    upto = [sum(x[0] < q for x in halves) for q in range(NQ + 1)]

    def variances(r):
        return r + 1 + max(0, r - NS)

    def at_step(step):
        r, k = divmod(step, NB)
        return r, k, r - 1 if 1 <= r <= runs else None

    def cols(q, h):
        nu = BATCH_U[q % NB]
        return range(quarter * h, min(quarter * (h + 1), nu))

    with nc.Block() as block:
        @block.sync
        def _(sp):
            for x in range(NS):
                if x:
                    sp.wait_ge(s.ranked, 2 * METHODS * NCH * x)
                load_rows(sp, d, w, s, (it * NS + NS + x) & (LAT - 1))
            for x in range(NS):
                sp.wait_ge(s.out, x + 1)
                sp.dma_start(d.xatt[bass.ds(it * (NS * 32) + x * 32, 32), :], w.o32[:, 1, :]).then_inc(s.stored, 16)
                sp.wait_ge(s.stored, 16 * (x + 1))

        @block.gpsimd
        def _(pool):
            link = chain(pool, s.pstep)

            def spread(r):
                pool.wait_ge(s.parts, r + 1)
                for p in range(3):
                    for m in range(METHODS):
                        dst = custom(w.spread[:, p], m * P + m * 8, [[METHODS * P, NCH], [32, HEADS], [1, 8]])
                        src = custom(w.parts[:, p], 0, [[C_IN, NCH], [8, HEADS], [1, 8]])
                        ins = pool.tensor_copy(dst, src)
                ins.then_inc(s.spread, 1)

            def differences(q):
                r, k = divmod(q, NB)
                l, x = r // NS, r % NS
                nu, at = BATCH_U[k], 3 * U_MAX * k
                if k == 0:
                    pool.wait_ge(s.sorted, r + 1)
                if q >= 2:
                    pool.wait_ge(s.scored, q - 1)
                for c in range(4):
                    ins = pool.tensor_tensor(
                        custom(w.x16[:, q % 2], HD * c, [[4 * HD, nu], [KNN, 3], [1, KNN]]),
                        custom(w.sorted[:, r % 2], P * c + at, [[3, nu], [1, 3], [1, KNN]]),
                        custom(w.centre[:, l, x], P * c + at, [[3, nu], [1, 3], [0, KNN]]), ALU.subtract)
                if k == 0:
                    link(ins)
                    for u, n in ((0, 3), (1, HEAD_POINTS - 3)):
                        ins = pool.tensor_tensor(
                            custom(w.x16[:, q % 2], 4 * HD * u, [[KNN, n], [1, KNN]]),
                            w.first[:, r % 2, 3 * u:3 * u + n, :],
                            custom(w.centre[:, l, x], 3 * u, [[1, n], [0, KNN]]), ALU.subtract)
                ins.then_inc(s.x16, 1)

            spread(0)
            differences(0)
            for step in range(steps):
                r, k, done = at_step(step)
                ahead = step + 1 < NQ
                if ahead and k < NB - 1:
                    differences(step + 1)
                if k == 3 and done is not None:
                    pool.wait_ge(s.var, variances(done))
                    pool.tensor_tensor(w.rstd[:, :], w.var[:, :], w.half[:, :], ALU.pow).then_inc(s.rstd, 1)
                if step < NQ:
                    pool.wait_ge(s.hi, step + 1)
                    pair = w.pair[:, step % 2].bitcast(F16).rearrange("p (n a) -> p n a", a=2)
                    pool.tensor_tensor(pair[:, :, 1], w.e[:, step % 2, :], pair[:, :, 0],
                                       ALU.subtract).then_inc(s.lo, 1)
                if k == 4 and done is not None and done >= NS:
                    pool.wait_ge(s.var, variances(done) + 1)
                    pool.tensor_tensor(w.r3[:, :], w.mv3[:, 1:2], w.half[0:32, :], ALU.pow).then_inc(s.rstd, 1)
                if k == 4 and r + 1 < runs:
                    spread(r + 1)
                if ahead and k == NB - 1:
                    differences(step + 1)

        @block.scalar
        def _(act):
            def keep_gathered(r):
                l, x = r // NS, r % NS
                act.wait_ge(s.gathered, r + 1)
                act.copy(w.sorted[:, r % 2, F_LEFT:F_LEFT + DIM], g.ps[:, 0, :])
                act.copy(w.sorted[:, r % 2, F_LEFT + DIM:F_LEFT + DIM + TAIL], g.ps[:, 6, 0:TAIL])
                act.copy(flat(w.first[:, r % 2]), g.ps[:, 6, TAIL:EXTRA])
                act.copy(w.centre16[:, r % 2, 0:DIM], g.ps[:, 1, :])
                act.copy(w.centre[:, l, x, 0:DIM], g.ps[:, 1, :]).then_inc(s.sorted, 1)

            def keep_low(q, h):
                if not 0 <= q < NQ or (q, h) not in halves:
                    return
                i, n = halves.index((q, h)), len(cols(q, h))
                act.wait_ge(s.part, i + 1)
                if i >= 2:
                    act.wait_ge(s.summed, i - 1)
                act.copy(w.low[:, i % 2, :, 0:n, :],
                         custom(g.ps[:, 4, :], HD, [[quarter * 2 * HD, 4], [2 * HD, n], [1, HD]])).then_inc(s.lows, 1)

            keep_gathered(0)
            for step in range(steps):
                r, k, done = at_step(step)
                keep_low(step - 2, 0)
                if step < NQ:
                    n = BATCH_U[k] * P
                    act.wait_ge(s.turned, step + 1)
                    if step >= 3:
                        act.wait_ge(s.part, upto[step - 2])
                    act.copy(flat(w.xT[:, step % 3])[:, 0:n], g.ps[:, 6, :].bitcast(F16)[:, 0:n]).then_inc(s.xT, 1)
                    act.wait_ge(s.shifted, step + 1)
                    act.activation(w.e[:, step % 2, :], w.e[:, step % 2, :], ACT.Exp,
                                   scale=INV_SQRT_HD).then_inc(s.exped, 1)
                keep_low(step - 2, 1)
                if step < NQ:
                    act.wait_ge(s.normed, step + 1)
                    pair = w.pair[:, step % 2].bitcast(F16).rearrange("p (n a) -> p n a", a=2)
                    act.copy(pair[:, :, 0], w.e[:, step % 2, :]).then_inc(s.hi, 1)
                if k == NB - 1 and r + 1 < runs:
                    keep_gathered(r + 1)

        @block.tensor
        def _(pe):
            writes = [0]

            def bank7():
                if writes[0]:
                    pe.wait_ge(s.b7r, writes[0])
                writes[0] += 1

            fences = [0]

            def fenced(ins):
                fences[0] += 1
                ins.then_inc(s.rows_of, 1)

            def fence(i):
                pe.wait_ge(s.rows_of, fences[0] - 1 + i)

            def gather(r):
                l, x = r // NS, r % NS
                pe.wait_ge(s.spread, r + 1)
                if r:
                    pe.wait_ge(s.shifted, r * NB - 1)
                    pe.wait_ge(s.xT, r * NB)
                order = [(p, m, c) for p in range(3) for m in range(METHODS) for c in range(NCH)]
                for i, (p, m, c) in enumerate(order):
                    for bank, a, n in ((0, 0, DIM), (6, DIM, EXTRA)):
                        pe.matmul(g.ps[:, bank, 0:n], w.spread[:, p, c, m, :], w.perm[:, x, m, c, a:a + n],
                                  start=(i == 0), stop=(i == len(order) - 1))
                order = [(p, m) for p in range(3) for m in range(METHODS)]
                for c in range(NCH):
                    for i, (p, m) in enumerate(order):
                        ins = pe.matmul(g.ps[:, 1, c * P:(c + 1) * P], w.spread[:, p, c, m, :], g.identb[:, :],
                                        start=(i == 0), stop=(i == len(order) - 1))
                ins.then_inc(s.gathered, 1)

            def centre_term(r):
                l = r // NS
                pe.wait_ge(s.sorted, r + 1)
                bank7()
                for half in range(l + 1):
                    quads = range(4) if l == 0 else (2 * half, 2 * half + 1)
                    order = [(p, c) for p in range(3) for c in quads]
                    for i, (p, c) in enumerate(order):
                        ins = pe.matmul(g.ps[:, 7, 256 * half:256 * half + P + 1], w.wcen[l][:, p, c, :],
                                        w.centre16[:, r % 2, P * c:P * c + P + 1], start=(i == 0),
                                        stop=(i == len(order) - 1))
                ins.then_inc(s.b7w, 1)

            def turn(q):
                k = q % NB
                pe.wait_ge(s.x16, q + 1)
                if q:
                    pe.wait_ge(s.xT, q)
                if k == 0:
                    pe.wait_ge(s.sorted, q // NB + 1)
                for u in range(BATCH_U[k]):
                    ins = pe.transpose(g.ps[:, 6, :].bitcast(F16)[:, P * u:P * (u + 1)], flat(w.x16[:, q % 2, u]),
                                       g.ident16[:, :])
                ins.then_inc(s.turned, 1)

            def scores(q):
                if q >= 2:
                    pe.wait_ge(s.shifted, q - 1)
                base = 2 * (q % 2)
                for i in range(2):
                    pe.matmul(g.ps[:, base + i, :], g.identb[:, :], flat(g.mask), start=True, stop=False,
                              skip_group_check=True)
                nu = BATCH_U[q % NB]
                for h in range(HEADS):
                    if h >= 2:
                        fence(h - 2)
                    for u in range(nu):
                        at = (h // 2 * U_MAX + u) * HD
                        for c in range(4):
                            v = w.x16[HD * h:HD * (h + 1), q % 2, u, c, :]
                            ins = pe.matmul(g.ps[HD * c:HD * (c + 1), base + h % 2, at:at + HD], v, v,
                                            start=False, stop=(u == nu - 1), skip_group_check=True)
                    if h < 2:
                        fenced(ins)
                ins.then_inc(s.scored, 1)

            def attention(q, h):
                if not 0 <= q < NQ or (q, h) not in halves:
                    return
                i = halves.index((q, h))
                pe.wait_ge(s.attn, q + 1)
                pe.wait_ge(s.xT, q + 1)
                if i:
                    pe.wait_ge(s.summed, i)
                weights = w.pairT[:, q % 2].bitcast(F16)
                for c in range(4):
                    rows = slice(HD * c, HD * (c + 1))
                    if c >= 2:
                        fence(c - 2)
                    for u in cols(q, h):
                        for a in range(HEADS):
                            group = ((a % 2) * 2 + a // 2) * U_MAX + u
                            at = ((c // 2) * quarter + u % quarter) * 2 * HD
                            ins = pe.matmul(g.ps[HD * a:HD * (a + 1), 4 + c % 2, at:at + 2 * HD],
                                            w.xT[rows, q % 3, u, HD * a:HD * (a + 1)],
                                            custom(weights[rows], 2 * HD * group, [[1, 2], [2, HD]]),
                                            start=True, stop=True, skip_group_check=True)
                    if c < 2:
                        fenced(ins)
                ins.then_inc(s.part, 1)

            def outputs(q):
                if not 0 <= q < NQ:
                    return
                l, nu = q // NB // NS, BATCH_U[q % NB]
                pe.wait_ge(s.summed, upto[q + 1])
                bank7()
                for c in range(4):
                    o = OUTS[l]
                    row = c * o % P
                    at = c * o // P * 256
                    ins = pe.matmul(g.ps[row:row + o, 7, at:at + nu * HD], w.wnei[l][:, :],
                                    flat(w.att[:, q % 2, c % 2 * 2 + c // 2, 0:nu, :]), start=True, stop=True, skip_group_check=True)
                ins.then_inc(s.b7w, 1)

            def average(l, src):
                bank7()
                avg = g.avg2 if l else g.avg1
                for half in range(l + 1):
                    ins = pe.matmul(g.ps[:, 7, 0:1], avg[:, :], src(half), start=(half == 0), stop=(half == l))
                ins.then_inc(s.b7w, 1)

            def turn_features(r):
                pe.wait_ge(s.f, r + 1)
                bank7()
                pe.transpose(g.ps[:, 7, 0:P], w.f[:, 0, :], g.ident[:, :]).then_inc(s.b7w, 1)

            def convolve(r):
                x = r % NS
                pe.wait_ge(s.f, r + 1)
                bank7()
                out = g.ps[0:32, 7, :]
                pe.matmul(out, w.w3a[:, :], w.centre[:, 0, x, 0:DIM], start=True, stop=False, skip_group_check=True)
                pe.matmul(out, w.w3b[:, :], w.centre[:, 1, x, 0:DIM], start=False, stop=False, skip_group_check=True)
                for half in range(2):
                    for c in range(2):
                        at = P * (2 * half + c)
                        ins = pe.matmul(out[:, at:at + P], w.w3c[:, c, :], w.f[:, half, :], start=False,
                                        stop=(half == 1 and c == 1), skip_group_check=True)
                ins.then_inc(s.b7w, 1)

            gather(0)
            for step in range(steps):
                r, k, done = at_step(step)
                attention(step - 2, 0)
                if k == 3 and done is not None:
                    pe.wait_ge(s.moments, done + 1)
                    average(done // NS, lambda half: w.mv[:, half, 0:1])
                if step < NQ:
                    turn(step)
                    scores(step)
                if k == 3 and done is not None:
                    pe.wait_ge(s.dev, done + 1)
                    average(done // NS, lambda half: w.dev[:, half, 1:2])
                attention(step - 2, 1)
                if k == 0 and r < runs:
                    centre_term(r)
                outputs(step - 3)
                if k == 4 and done is not None:
                    if done < NS:
                        turn_features(done)
                    else:
                        convolve(done)
                if k == NB - 1 and r + 1 < runs:
                    gather(r + 1)

        @block.vector
        def _(dve):
            link = chain(dve, s.dstep)
            reads = [0]

            def bank7():
                reads[0] += 1
                dve.wait_ge(s.b7w, reads[0])

            def features(x):
                link(dve.tensor_copy(w.fn[:, x, :, :], g.xnT[:, :, bass.ds(it * (NS * C_IN) + x * C_IN, C_IN)]))

            def split(r):
                if r:
                    dve.wait_ge(s.spread, r)
                src = w.fn[:, r % NS]
                for p in range(3):
                    ins = dve.tensor_copy(flat(w.parts[:, p]), flat(src))
                    if p == 2:
                        ins.then_inc(s.parts, 1)
                        return
                    link(ins)
                    link(dve.tensor_tensor(flat(w.rest), flat(src), flat(w.parts[:, p]), ALU.subtract))
                    src = w.rest

            def add_parts(q, h):
                if not 0 <= q < NQ or (q, h) not in halves:
                    return
                i, us = halves.index((q, h)), cols(q, h)
                dve.wait_ge(s.lows, i + 1)
                dve.tensor_tensor(
                    custom(w.att[:, q % 2], us[0] * HD, [[U_MAX * HD, 4], [HD, len(us)], [1, HD]]),
                    custom(g.ps[:, 4, :], 0, [[quarter * 2 * HD, 4], [2 * HD, len(us)], [1, HD]]),
                    w.low[:, i % 2, :, 0:len(us), :], ALU.add).then_inc(s.summed, 1)

            def shift(q):
                dve.wait_ge(s.scored, q + 1)
                sc = g.ps[:, 2 * (q % 2):2 * (q % 2) + 2, :].rearrange("p a (u j) -> p (a u) j", j=HD)
                e = w.e[:, q % 2, :].rearrange("p (u j) -> p u j", j=HD)
                n = SC // HD
                link(dve.tensor_reduce(w.rmax[:, q % 2, :], sc, AX.X, ALU.max))
                dve.tensor_tensor(e, sc, w.rmax[:, q % 2, :, None].broadcast_to([P, n, HD]),
                                  ALU.subtract).then_inc(s.shifted, 1)

            def normalise(q):
                e = w.e[:, q % 2, :].rearrange("p (u j) -> p u j", j=HD)
                n = SC // HD
                dve.wait_ge(s.exped, q + 1)
                link(dve.tensor_reduce(w.rsum[:, q % 2, :], e, AX.X, ALU.add))
                link(dve.reciprocal(w.rsum[:, q % 2, :], w.rsum[:, q % 2, :]))
                dve.tensor_tensor(e, e, w.rsum[:, q % 2, :, None].broadcast_to([P, n, HD]),
                                  ALU.mult).then_inc(s.normed, 1)

            def turn_weights(q):
                if not 0 <= q < NQ:
                    return
                dve.wait_ge(s.lo, q + 1)
                dve.transpose(w.pairT[:, q % 2, :], w.pair[:, q % 2, :]).then_inc(s.attn, 1)

            def keep_outputs(q):
                if not 0 <= q < NQ:
                    return
                r, k = divmod(q, NB)
                l, nu = r // NS, BATCH_U[k]
                bank7()
                for half in range(l + 1):
                    ins = dve.tensor_tensor(
                        custom(w.h[:, half], 0, [[BLK, nu], [KNN, 3], [1, KNN]]),
                        custom(g.ps[:, 7, :], 256 * half, [[HD, nu], [KNN, 3], [1, KNN]]),
                        custom(w.cterm[:, r % 2, half], 3 * U_MAX * k, [[3, nu], [1, 3], [0, KNN]]), ALU.add)
                    if half < l:
                        link(ins)
                ins.then_inc(s.b7r, 1)
                dve.wait_ge(s.b7r, reads[0])
                n = nu * BLK if k < NB - 1 else (P * KNN - U_MAX * BLK * k)
                for half in range(l + 1):
                    link(dve.bn_stats(w.stats[:, r % 2, half, k, :], w.h[:, half, 0:n]))
                    link(dve.tensor_reduce(w.peak[:, r % 2, half, 3 * U_MAX * k:3 * (U_MAX * k + nu)],
                                           w.h[:, half, 0:nu * BLK].rearrange("p (n j) -> p n j", j=KNN), AX.X, ALU.max))

            def moments(r):
                l = r // NS
                for half in range(l + 1):
                    ins = dve.bn_aggr(w.mv[:, half, :], flat(w.stats[:, r % 2, half]))
                    if half < l:
                        link(ins)
                ins.then_inc(s.moments, 1)
                dve.wait_ge(s.moments, r + 1)

            def deviations(r):
                l = r // NS
                bank7()
                dve.tensor_copy(w.mean[:, :], g.ps[:, 7, 0:1]).then_inc(s.b7r, 1)
                dve.wait_ge(s.b7r, reads[0])
                link(dve.tensor_scalar(w.dev[:, 0:l + 1, 0], w.mv[:, 0:l + 1, 0], w.mean[:, 0:1], None, ALU.subtract))
                link(dve.tensor_tensor(w.dev[:, 0:l + 1, 0], w.dev[:, 0:l + 1, 0], w.dev[:, 0:l + 1, 0], ALU.mult))
                dve.tensor_tensor(w.dev[:, 0:l + 1, 1], w.dev[:, 0:l + 1, 0], w.mv[:, 0:l + 1, 1],
                                  ALU.add).then_inc(s.dev, 1)

            def variance(r):
                bank7()
                dve.tensor_scalar(w.var[:, :], g.ps[:, 7, 0:1], LN_EPS, None, ALU.add).then_inc(s.b7r, 1)
                dve.wait_ge(s.b7r, reads[0])
                dve.sem_inc(s.var)

            def normalise_features(r):
                l = r // NS
                f = w.f[:, 0:l + 1, :]
                link(dve.tensor_scalar(w.meanb[:, :], w.mean[:, :], w.bias[:, l:l + 1], None, ALU.add))
                link(dve.tensor_scalar(f, w.peak[:, r % 2, 0:l + 1, 0:P], w.bias[:, l:l + 1], w.meanb[:, 0:1],
                                       ALU.add, ALU.subtract))
                dve.wait_ge(s.rstd, variances(r))
                link(dve.tensor_scalar(f, f, w.rstd[:, 0:1], None, ALU.mult))
                dve.scalar_tensor_tensor(flat(f), flat(f), 0.2, flat(f), ALU.mult, ALU.max).then_inc(s.f, 1)

            def finish_rows(r):
                x = r - NS
                bank7()
                link(dve.bn_stats(w.st3[:, :], g.ps[0:32, 7, :]))
                link(dve.bn_aggr(w.mv3[:, :], w.st3[:, :]))
                dve.tensor_scalar(w.mv3[:, 1:2], w.mv3[:, 1:2], LN_EPS, None, ALU.add).then_inc(s.var, 1)
                if x:
                    dve.wait_ge(s.stored, 16 * x)
                dve.tensor_scalar(w.o32[:, 0, :], g.ps[0:32, 7, :], w.mv3[:, 0:1], None,
                                  ALU.subtract).then_inc(s.b7r, 1)
                dve.wait_ge(s.b7r, reads[0])
                dve.wait_ge(s.rstd, variances(r) + 1)
                link(dve.tensor_scalar(w.o32[:, 0, :], w.o32[:, 0, :], w.r3[:, 0:1], None, ALU.mult))
                dve.scalar_tensor_tensor(w.o32[:, 1, :], w.o32[:, 0, :], 0.2, w.o32[:, 0, :], ALU.mult,
                                         ALU.max).then_inc(s.out, 1)

            features(0)
            split(0)
            for step in range(steps):
                r, k, done = at_step(step)
                add_parts(step - 2, 0)
                if k == 3 and done is not None:
                    deviations(done)
                if step < NQ:
                    shift(step)
                if k == 3 and done is not None:
                    variance(done)
                add_parts(step - 2, 1)
                if k == 0 and r < runs:
                    bank7()
                    l = r // NS
                    dve.tensor_copy(w.cterm[:, r % 2, 0:l + 1, 0:P + 1],
                                    g.ps[:, 7, :].rearrange("p (a n) -> p a n", a=2)[:, 0:l + 1, 0:P + 1])\
                       .then_inc(s.b7r, 1)
                turn_weights(step - 1)
                if step < NQ:
                    normalise(step)
                keep_outputs(step - 3)
                if k == 2 and done is not None:
                    moments(done)
                if k == 3 and done is not None:
                    normalise_features(done)
                if k == 4 and done is not None:
                    if done < NS:
                        bank7()
                        dve.tensor_copy(flat(w.fn[:, done % NS]), g.ps[:, 7, 0:P]).then_inc(s.b7r, 1)
                        dve.wait_ge(s.b7r, reads[0])
                    else:
                        finish_rows(done)
                if k == 4 and r + 1 < runs:
                    if r + 1 < NS:
                        features(r + 1)
                    split(r + 1)
                if NS <= r < runs:
                    if k == 0:
                        key_columns(dve, g, w, s, (it * NS + r) & (LAT - 1), r - NS)
                    for i in range(METHODS * NCH * k // NB, METHODS * NCH * (k + 1) // NB):
                        rank_unit(dve, g, w, s, r - NS, i, r - NS)
    release(nc, s)


def bcast_rows(keys, b):
    return keys[bass.ds(b, 1), :, :].rearrange("a m n -> (a m) n").partition_broadcast(P)


def add_point_attention(nc, g, d):
    with ExitStack() as st:
        s = semaphores(nc, st, "addp", "loaded added")
        y = st.enter_context(nc.sbuf_tensor("addp_y", [P, NT, DIM], F32))
        with nc.Block() as block:
            @block.sync
            def _(sp):
                for t in range(NT):
                    sp.dma_start(y[:, t, :], d.xatt[t * P:(t + 1) * P, :]).then_inc(s.loaded, 16)

            @block.vector
            def _(dve):
                dve.wait_ge(s.loaded, 16 * NT)
                dve.tensor_tensor(flat(g.x), flat(g.x), flat(y), ALU.add).then_inc(s.added, 1)
        release(nc, s)


def bound_attention(nc, g, d):
    with ExitStack() as st:
        def sb(name, shape, dt=F32):
            return st.enter_context(nc.sbuf_tensor("ba_" + name, shape, dt))
        s = semaphores(nc, st, "ba", "loaded step signs bound turned query values scored gate masked mixed added")
        vec = sb("vec", [NCH, 3, P])
        sgn = sb("sgn", [NCH, 3, P])
        zero = sb("zero", [NCH, 3, P])
        alpha = sb("alpha", [NCH, 3])
        sel = sb("sel", [NCH, NCH, P])
        causal = sb("causal", [P, P])
        qk = sb("qk", [P, NCH])
        qc = sb("qc", [P, NCH])
        query = sb("query", [P, NCH, ROWS])
        value = sb("value", [P, NT, DIM])
        gate = sb("gate", [P, NT, NCH, P])
        with nc.Block() as block:
            @block.sync
            def _(sp):
                sp.dma_start(vec[:, :, :], d.bind).then_inc(s.loaded, 16)
                sp.dma_start(sel[:, :, :], d.sel4).then_inc(s.loaded, 16)
                sp.dma_start(causal[:, :], d.causal).then_inc(s.loaded, 16)

            @block.scalar
            def _(act):
                act.wait_ge(s.loaded, 48)
                act.sign(sgn[:, :, :], vec[:, :, :]).then_inc(s.signs, 1)
                for t in range(NT):
                    act.wait_ge(s.scored, t + 1)
                    act.activation(flat(gate[:, t]), g.ps[:, 2 + t, :], ACT.Sigmoid,
                                   scale=4.0 * float(P) ** -0.5).then_inc(s.gate, 1)

            @block.tensor
            def _(pe):
                pe.wait_ge(s.bound, 1)
                pe.transpose(g.ps[:, 0, 0:NCH], vec[:, 0, :], g.ident[0:NCH, 0:NCH])
                pe.transpose(g.ps[:, 0, NCH:2 * NCH], vec[:, 1, :], g.ident[0:NCH, 0:NCH])
                for h in range(NCH):
                    ins = pe.matmul(g.ps[:, 1, h * P:(h + 1) * P], sel[:, h, :], vec[:, 2, :], start=True, stop=True)
                ins.then_inc(s.turned, 1)
                for t in range(NT):
                    pe.wait_ge(s.query, NCH)
                    for h in range(NCH):
                        ins = pe.matmul(g.ps[:, 2 + t, h * P:(h + 1) * P], g.xnT[:, h, t * P:(t + 1) * P],
                                        query[:, h, t * P:(t + 1) * P], start=True, stop=True)
                    ins.then_inc(s.scored, 1)
                for t in range(NT):
                    pe.wait_ge(s.masked, t + 1)
                    pe.wait_ge(s.values, NT)
                    if t >= 2:
                        pe.wait_ge(s.added, t - 1)
                    for h in range(NCH):
                        ins = pe.matmul(g.ps[:, 6 + t % 2, h * P:(h + 1) * P], gate[:, t, h, :],
                                        value[:, t, h * P:(h + 1) * P], start=True, stop=True)
                    ins.then_inc(s.mixed, 1)

            @block.vector
            def _(dve):
                link = chain(dve, s.step)
                dve.wait_ge(s.loaded, 48)
                link(dve.tensor_reduce(alpha[:, :], vec[:, :, :], AX.X, ALU.add, apply_absolute_value=True))
                link(dve.tensor_scalar(alpha[:, :], alpha[:, :], 1.0 / P, None, ALU.mult))
                dve.wait_ge(s.signs, 1)
                mean = alpha[:, :, None].broadcast_to([NCH, 3, P])
                link(dve.tensor_tensor(sgn[:, :, :], sgn[:, :, :], mean, ALU.mult))
                link(dve.tensor_scalar(zero[:, :, :], sgn[:, :, :], 0.0, None, ALU.is_equal))
                link(dve.tensor_tensor(zero[:, :, :], zero[:, :, :], mean, ALU.mult))
                link(dve.tensor_tensor(sgn[:, :, :], sgn[:, :, :], zero[:, :, :], ALU.add))
                link(dve.tensor_tensor(sgn[:, :, :], sgn[:, :, :], vec[:, :, :], ALU.subtract))
                dve.tensor_tensor(vec[:, :, :], sgn[:, :, :], vec[:, :, :], ALU.add).then_inc(s.bound, 1)
                dve.wait_ge(s.turned, 1)
                link(dve.tensor_copy(qc[:, :], g.ps[:, 0, 0:NCH]))
                link(dve.tensor_tensor(qk[:, :], qc[:, :], g.ps[:, 0, NCH:2 * NCH], ALU.mult))
                for h in range(NCH):
                    dve.tensor_scalar(query[:, h, :], g.xnT[:, h, :], qk[:, h:h + 1], None,
                                      ALU.mult).then_inc(s.query, 1)
                for t in range(NT):
                    dve.tensor_tensor(value[:, t, :], g.xn[:, t, :], g.ps[:, 1, :], ALU.mult).then_inc(s.values, 1)
                for t in range(NT):
                    dve.wait_ge(s.gate, t + 1)
                    dve.tensor_tensor(gate[:, t], gate[:, t], causal[:, None, :].broadcast_to([P, NCH, P]),
                                      ALU.mult).then_inc(s.masked, 1)
                for t in range(NT):
                    dve.wait_ge(s.mixed, t + 1)
                    dve.tensor_tensor(g.x[:, t, :], g.x[:, t, :], g.ps[:, 6 + t % 2, :], ALU.add).then_inc(s.added, 1)
        release(nc, s)


EXPERTS, RANK = 8, 16


def experts(nc, g, d, name, hidden, scale, capacity):
    G = hidden or EXPERTS
    n_rows = 4 if hidden else 1
    with ExitStack() as st:
        def sb(nm, shape, dt=F32):
            return st.enter_context(nc.sbuf_tensor(f"{name}_{nm}", shape, dt))
        s = semaphores(nc, st, name, "loaded step projected hmom hroot hidden hturned hback gates top expo chosen counted "
                 "weighted turned low out added")
        wa = sb("wa", [P, NCH, G + P])
        wb = sb("wb", [P, NCH, DIM])
        lb = sb("lb", [P, DIM])
        brow = sb("brow", [1, DIM])
        ones = sb("ones", [P, P])
        iota = sb("iota", [P, EXPERTS])
        low = sb("low", [P, NT, P])
        lowT = sb("lowT", [P, NT, P])
        lg = sb("lg", [P, NT, EXPERTS])
        top = sb("top", [P, NT, 8])
        idx = sb("idx", [P, NT, 8], U32)
        idf = sb("idf", [P, NT, 8])
        hot = sb("hot", [P, NT, 2, EXPERTS])
        dlt = sb("dlt", [P, NT])
        ex = sb("ex", [P, NT])
        w01 = sb("w01", [P, NT, 2])
        ok = sb("ok", [P, 2, EXPERTS])
        w2 = sb("w2", [P, NT, 2, EXPERTS])
        wfull = sb("wfull", [P, NT, EXPERTS])
        if hidden:
            rowv = sb("rowv", [P, 3, hidden])
            gb2 = sb("gb2", [P, EXPERTS])
            gw2 = sb("gw2", [hidden, EXPERTS])
            hh = sb("hh", [P, NT, hidden])
            hst = sb("hst", [P, NT, 6])
            hmv = sb("hmv", [P, NT, 2])
            hr = sb("hr", [P, NT])
            hT = sb("hT", [hidden, NT, P])
        with nc.Block() as block:
            @block.sync
            def _(sp):
                sp.dma_start(wa[:, :, :], d.all[name + "_wa"]).then_inc(s.loaded, 16)
                sp.dma_start(iota[:, :], d.iota8.partition_broadcast(P)).then_inc(s.loaded, 16)
                sp.dma_start(brow[:, :], d.all[name + "_bias"]).then_inc(s.loaded, 16)
                sp.dma_start(wb[:, :, :], d.all[name + "_wb"]).then_inc(s.loaded, 16)
                sp.dma_start(lb[:, :], d.all[name + "_lb"]).then_inc(s.loaded, 16)
                if hidden:
                    sp.dma_start(rowv[:, :, :], d.all[name + "_rows"].partition_broadcast(P)).then_inc(s.loaded, 16)
                    sp.dma_start(gb2[:, :], d.all[name + "_gb2"].partition_broadcast(P)).then_inc(s.loaded, 16)
                    sp.dma_start(gw2[:, :], d.all[name + "_gw2"]).then_inc(s.loaded, 16)

            loads = 16 * (8 if hidden else 5)

            @block.tensor
            def _(pe):
                pe.wait_ge(s.loaded, loads)
                for t in range(NT):
                    for c in range(NCH):
                        ins = pe.matmul(g.ps[:, t, 0:G + P], g.xnT[:, c, t * P:(t + 1) * P], wa[:, c, :],
                                        start=(c == 0), stop=(c == NCH - 1))
                    ins.then_inc(s.projected, 1)
                if hidden:
                    pe.wait_ge(s.hidden, 1)
                    for t in range(NT):
                        ins = pe.transpose(g.ps[0:hidden, 4, t * P:(t + 1) * P], hh[:, t, :], g.ident[:, :])
                    ins.then_inc(s.hturned, 1)
                    pe.wait_ge(s.hback, 1)
                    for t in range(NT):
                        ins = pe.matmul(g.ps[:, 5, t * EXPERTS:(t + 1) * EXPERTS], hT[:, t, :], gw2[:, :],
                                        start=True, stop=True)
                    ins.then_inc(s.gates, 1)
                if capacity:
                    pe.wait_ge(s.chosen, 1)
                    for t in range(NT):
                        ins = pe.matmul(g.ps[:, 6, 0:2 * EXPERTS], ones[:, :], flat(hot[:, t]),
                                        start=(t == 0), stop=(t == NT - 1))
                    ins.then_inc(s.counted, 1)
                for t in range(NT):
                    pe.wait_ge(s.weighted, t + 1)
                    pe.transpose(g.ps[:, 7, t * P:(t + 1) * P], low[:, t, :], g.ident[:, :]).then_inc(s.turned, 1)
                for t in range(NT):
                    for c in range(NCH):
                        pe.matmul(g.ps[:, t, :], g.xnT[:, c, t * P:(t + 1) * P], wb[:, c, :],
                                  start=(c == 0), stop=False)
                    pe.matmul(g.ps[:, t, :], ones[0:1, :], brow[:, :], start=False, stop=False)
                    pe.wait_ge(s.low, 1)
                    pe.matmul(g.ps[:, t, :], lowT[:, t, :], lb[:, :], start=False, stop=True).then_inc(s.out, 1)

            @block.scalar
            def _(act):
                if hidden:
                    act.wait_ge(s.hmom, 1)
                    act.activation(hr[:, :], hmv[:, :, 1], ACT.Sqrt, bias=g.eps[:, 0:1]).then_inc(s.hroot, 1)
                    act.wait_ge(s.hturned, 1)
                    act.copy(flat(hT), g.ps[0:hidden, 4, :]).then_inc(s.hback, 1)
                act.wait_ge(s.top, 1)
                act.activation(ex[:, :], dlt[:, :], ACT.Exp).then_inc(s.expo, 1)
                act.wait_ge(s.turned, NT)
                act.copy(flat(lowT), g.ps[:, 7, :]).then_inc(s.low, 1)

            @block.vector
            def _(dve):
                link = chain(dve, s.step)
                link(dve.memset(ones[:, :], 1.0))
                dve.wait_ge(s.loaded, loads)
                dve.wait_ge(s.projected, NT)
                if hidden:
                    link(dve.tensor_tensor(hh[:, :, :], g.ps[:, 0:NT, 0:G],
                                           rowv[:, 0:1, :].broadcast_to([P, NT, G]), ALU.add))
                    for t in range(NT):
                        link(dve.bn_stats(hst[:, t, :], hh[:, t, :]))
                    for t in range(NT):
                        ins = dve.bn_aggr(hmv[:, t, :], hst[:, t, :])
                        if t < NT - 1:
                            link(ins)
                    ins.then_inc(s.hmom, 1)
                    dve.wait_ge(s.hmom, 1)
                    dve.wait_ge(s.hroot, 1)
                    link(dve.reciprocal(hr[:, :], hr[:, :]))
                    for t in range(NT):
                        link(dve.tensor_scalar(hh[:, t, :], hh[:, t, :], hmv[:, t, 0:1], hr[:, t:t + 1],
                                               ALU.subtract, ALU.mult))
                    link(dve.tensor_tensor(hh[:, :, :], hh[:, :, :], rowv[:, 1:2, :].broadcast_to([P, NT, G]), ALU.mult))
                    link(dve.tensor_tensor(hh[:, :, :], hh[:, :, :], rowv[:, 2:3, :].broadcast_to([P, NT, G]), ALU.add))
                    dve.tensor_scalar(hh[:, :, :], hh[:, :, :], 0.0, None, ALU.max).then_inc(s.hidden, 1)
                    dve.wait_ge(s.gates, 1)
                    link(dve.tensor_tensor(lg[:, :, :], g.ps[:, 5, 0:NT * EXPERTS].rearrange("p (t e) -> p t e", t=NT),
                                           gb2[:, None, :].broadcast_to([P, NT, EXPERTS]), ALU.add))
                else:
                    link(dve.tensor_copy(lg[:, :, :], g.ps[:, 0:NT, 0:G]))
                for t in range(NT):
                    link(dve.max(top[:, t, :], lg[:, t, :]))
                for t in range(NT):
                    link(dve.max_index(idx[:, t, :], top[:, t, :], lg[:, t, :]))
                dve.tensor_tensor(dlt[:, :], top[:, :, 1], top[:, :, 0], ALU.subtract).then_inc(s.top, 1)
                link(dve.tensor_copy(idf[:, :, :], idx[:, :, :]))
                ins = dve.tensor_tensor(hot[:, :, :, :], iota[:, None, None, :].broadcast_to([P, NT, 2, EXPERTS]),
                                        idf[:, :, 0:2, None].broadcast_to([P, NT, 2, EXPERTS]), ALU.is_equal)
                ins.then_inc(s.chosen, 1)
                dve.wait_ge(s.chosen, 1)
                dve.wait_ge(s.expo, 1)
                link(dve.tensor_scalar(w01[:, :, 0], ex[:, :], 1.0, None, ALU.add))
                link(dve.reciprocal(w01[:, :, 0], w01[:, :, 0]))
                link(dve.tensor_scalar(w01[:, :, 0], w01[:, :, 0], scale, None, ALU.mult))
                link(dve.tensor_tensor(w01[:, :, 1], w01[:, :, 0], ex[:, :], ALU.mult))
                if capacity:
                    dve.wait_ge(s.counted, 1)
                    link(dve.tensor_scalar(flat(ok), g.ps[:, 6, 0:2 * EXPERTS], float(capacity), None, ALU.is_le))
                    for t in range(NT):
                        link(dve.tensor_tensor(hot[:, t], hot[:, t], ok[:, :, :], ALU.mult))
                link(dve.tensor_tensor(w2[:, :, :, :], hot[:, :, :, :],
                                       w01[:, :, :, None].broadcast_to([P, NT, 2, EXPERTS]), ALU.mult))
                link(dve.tensor_tensor(wfull[:, :, :], w2[:, :, 0, :], w2[:, :, 1, :], ALU.add))
                for t in range(NT):
                    dve.tensor_tensor(low[:, t, :].rearrange("p (e r) -> p e r", e=EXPERTS),
                                      g.ps[:, t, G:G + P].rearrange("p (e r) -> p e r", e=EXPERTS),
                                      wfull[:, t, :, None].broadcast_to([P, EXPERTS, RANK]),
                                      ALU.mult).then_inc(s.weighted, 1)
                for t in range(NT):
                    dve.wait_ge(s.out, t + 1)
                    dve.tensor_tensor(g.x[:, t, :], g.x[:, t, :], g.ps[:, t, :], ALU.add).then_inc(s.added, 1)
        release(nc, s)


Q_HEADS, KV_HEADS, GROUP = 32, 8, 4
CTX = 512
KV = CTX + TOK
RMS_EPS = 1e-6
ATT_SCALE = float(P) ** -0.5


def cross_attention(nc, g, d):
    with ExitStack() as st:
        def sb(name, shape, dt=F32):
            return st.enter_context(nc.sbuf_tensor("ca_" + name, shape, dt))
        w = named({})
        w.qT = sb("qT", [P, Q_HEADS, ROWS])
        w.klat = sb("klat", [P, KV_HEADS, ROWS])
        w.wk = sb("wk", [P, NCH, KV_HEADS * P])
        w.wv = sb("wv", [P, NCH, KV_HEADS * P])
        w.mean = sb("mean", [P, P])
        w.nw = sb("nw", [P, 3])
        w.eps = sb("eps", [P, 1])
        with ExitStack() as s1:
            project_latents(nc, g, d, w, s1)
        with ExitStack() as s2:
            attend(nc, g, d, w, s2)
        with ExitStack() as s3:
            project_out(nc, g, d, w, s3)


def project_latents(nc, g, d, w, st):
    def sb(name, shape, dt=F32):
        return st.enter_context(nc.sbuf_tensor("pl_" + name, shape, dt))
    s = semaphores(nc, st, "pl", "kw q0 q1 consts step q sq ms root rstd done kv kvout vst0 vst1")
    wq = sb("wq", [P, 2, NCH, GROUP * P])
    sq = sb("sq", [P, 2, ROWS])
    root = sb("root", [P, 2, ROWS])
    vout = sb("vout", [P, 2, 512])
    s_q, s_v = (s.q0, s.q1), (s.vst0, s.vst1)
    n_kv = KV_HEADS + NT * 2
    with nc.Block() as block:
        @block.sync
        def _(sp):
            sp.dma_start(w.mean[:, :], d.mean128).then_inc(s.kw, 16)
            sp.dma_start(w.nw[:, 0:2], d.qk_norm).then_inc(s.kw, 16)
            for k in range(KV_HEADS):
                if k >= 2:
                    sp.wait_ge(s.q, GROUP * (k - 1))
                sp.dma_start(wq[:, k % 2, :, :], d.wq[:, :, k * GROUP * P:(k + 1) * GROUP * P]).then_inc(s_q[k % 2], 16)
            sp.dma_start(w.wk[:, :, :], d.wk).then_inc(s.kw, 16)
            sp.dma_start(w.wv[:, :, :], d.wv).then_inc(s.kw, 16)
            for i in range(NT * 2):
                sp.wait_ge(s.kvout, KV_HEADS + i + 1)
                t, half = i // 2, i % 2
                sp.dma_start(d.v_lat[t * P:(t + 1) * P, half * 512:(half + 1) * 512], vout[:, i % 2, :]).then_inc(s_v[i % 2], 16)
            for sem in s_v:
                sp.wait_ge(sem, 16 * NT)

        @block.tensor
        def _(pe):
            pe.wait_ge(s.kw, 32)

            def mean_square(h):
                pe.wait_ge(s.sq, h + 1)
                if h >= 2:
                    pe.wait_ge(s.root, h - 1)
                pe.matmul(g.ps[:, 3 + h % 2, :], w.mean[:, :], sq[:, h % 2, :], start=True, stop=True).then_inc(s.ms, 1)

            for h in range(Q_HEADS):
                k = h // GROUP
                if h % GROUP == 0:
                    pe.wait_ge(s_q[k % 2], 16 * (k // 2 + 1))
                if h >= 3:
                    pe.wait_ge(s.done, h - 2)
                for c in range(NCH):
                    ins = pe.matmul(g.ps[:, h % 3, :], wq[:, k % 2, c, (h % GROUP) * P:(h % GROUP + 1) * P],
                                    g.xnT[:, c, :], start=(c == 0), stop=(c == NCH - 1))
                ins.then_inc(s.q, 1)
                if h >= 1:
                    mean_square(h - 1)
            mean_square(Q_HEADS - 1)
            pe.wait_ge(s.kw, 64)
            for i in range(n_kv):
                if i >= 2:
                    pe.wait_ge(s.kvout, i - 1)
                for c in range(NCH):
                    if i < KV_HEADS:
                        lhs, rhs = w.wk[:, c, i * P:(i + 1) * P], g.xnT[:, c, :]
                    else:
                        t, half = (i - KV_HEADS) // 2, i % 2
                        lhs, rhs = g.xnT[:, c, t * P:(t + 1) * P], w.wv[:, c, half * 512:(half + 1) * 512]
                    ins = pe.matmul(g.ps[:, 5 + i % 2, :], lhs, rhs, start=(c == 0), stop=(c == NCH - 1))
                ins.then_inc(s.kv, 1)

        @block.scalar
        def _(act):
            act.wait_ge(s.consts, 1)
            for h in range(Q_HEADS + 1):
                if h < Q_HEADS:
                    act.wait_ge(s.q, h + 1)
                    if h >= 2:
                        act.wait_ge(s.ms, h - 1)
                    act.activation(sq[:, h % 2, :], g.ps[:, h % 3, :], ACT.Square).then_inc(s.sq, 1)
                if h >= 1:
                    act.wait_ge(s.ms, h)
                    if h >= 3:
                        act.wait_ge(s.done, h - 2)
                    act.activation(root[:, (h - 1) % 2, :], g.ps[:, 3 + (h - 1) % 2, :], ACT.Sqrt,
                                   bias=w.eps[:, 0:1]).then_inc(s.root, 1)
            for i in range(n_kv):
                act.wait_ge(s.kv, i + 1)
                if i < KV_HEADS:
                    dst = w.klat[:, i, :]
                else:
                    j = i - KV_HEADS
                    if j >= 2:
                        act.wait_ge(s_v[j % 2], 16 * (j // 2))
                    dst = vout[:, j % 2, :]
                act.copy(dst, g.ps[:, 5 + i % 2, :]).then_inc(s.kvout, 1)

        @block.vector
        def _(dve):
            link = chain(dve, s.step)
            link(dve.memset(w.eps[:, :], RMS_EPS))
            dve.wait_ge(s.kw, 32)
            dve.tensor_tensor(w.nw[:, 2:3], w.nw[:, 0:1], w.nw[:, 1:2], ALU.mult).then_inc(s.consts, 1)
            dve.wait_ge(s.consts, 1)
            for h in range(Q_HEADS):
                dve.wait_ge(s.root, h + 1)
                link(dve.reciprocal(root[:, h % 2, :], root[:, h % 2, :]))
                dve.scalar_tensor_tensor(w.qT[:, h, :], g.ps[:, h % 3, :], w.nw[:, 2:3], root[:, h % 2, :],
                                         ALU.mult, ALU.mult).then_inc(s.done, 1)
    release(nc, s)


def attend(nc, g, d, w, st):
    def sb(name, shape, dt=F32):
        return st.enter_context(nc.sbuf_tensor("at_" + name, shape, dt))
    s = semaphores(nc, st, "at", "ctx vl step qb kl klsq k kc sq ms msl root rootl rstd v vc s scaled nmax expd norm prob "
             "turned pt mixed ot zero")
    t = named({})
    t.ctx = g.xn
    t.kT = sb("kT", [P, KV_HEADS, KV])
    t.R = sb("R", [P, KV_HEADS, KV])
    t.V = sb("V", [P, CTX // P + 1, KV_HEADS * P])
    t.sq = sb("sq", [P, 2, CTX])
    t.sql = sb("sql", [P, KV_HEADS, TOK])
    t.qb = sb("qb", [P, KV_HEADS, GROUP, TOK])
    t.pr = sb("pr", [P, 2, KV])
    t.mx = sb("mx", [P, 2, 2])
    t.sum = sb("sum", [P, 2, 2])
    t.PT = sb("PT", [P, CTX // P + 1, P])
    NB = CTX // P
    with nc.Block() as block:
        @block.gpsimd
        def _(pool):
            pool.memset(t.V[:, NB, :], 0.0)
            pool.memset(t.PT[:, NB, :], 0.0)
    release(nc, s)
    with nc.Fori(0, LAT) as b:
        with nc.Block() as block:
            @block.sync
            def _(sp):
                sp.dma_start(t.ctx[:, :, :], d.ctxT[bass.ds(b, 1), :, :, :].rearrange("b p c n -> (b p) c n")).then_inc(s.ctx, 16)
                sp.dma_start(t.V[0:TOK, NB, :], d.v_lat[bass.ds(b * TOK, TOK), :]).then_inc(s.vl, 16)

            @block.gpsimd
            def _(pool):
                pool.tensor_copy(flat_heads(t.qb), w.qT[:, :, bass.ds(b * TOK, TOK)]).then_inc(s.qb, 1)
                pool.tensor_copy(t.kT[:, :, CTX:KV], w.klat[:, :, bass.ds(b * TOK, TOK)]).then_inc(s.kl, 1)
                pool.wait_ge(s.kl, 1)
                pool.tensor_tensor(t.sql[:, :, :], t.kT[:, :, CTX:KV], t.kT[:, :, CTX:KV], ALU.mult).then_inc(s.klsq, 1)
                for h in range(KV_HEADS):
                    pool.wait_ge(s.norm, h + 1)
                    pool.tensor_scalar(t.pr[:, h % 2, :], t.pr[:, h % 2, :], t.sum[:, h % 2, 1:2], None,
                                       ALU.mult).then_inc(s.prob, 1)

            @block.tensor
            def _(pe):
                def mean_square(h):
                    pe.wait_ge(s.sq, h + 1)
                    if h >= 1:
                        pe.wait_ge(s.root, h)
                    pe.matmul(g.ps[:, 2, :], w.mean[:, :], t.sq[:, h % 2, :], start=True, stop=True).then_inc(s.ms, 1)

                pe.wait_ge(s.ctx, 16)
                for h in range(KV_HEADS):
                    if h >= 2:
                        pe.wait_ge(s.sq, h - 1)
                    for c in range(NCH):
                        ins = pe.matmul(g.ps[:, h % 2, :], w.wk[:, c, h * P:(h + 1) * P], t.ctx[:, c, :],
                                        start=(c == 0), stop=(c == NCH - 1))
                    ins.then_inc(s.k, 1)
                    if h == 0:
                        pe.wait_ge(s.klsq, 1)
                        pe.matmul(g.ps[:, 3, 0:KV_HEADS * TOK], w.mean[:, :], flat(t.sql), start=True,
                                  stop=True).then_inc(s.msl, 1)
                    else:
                        mean_square(h - 1)
                mean_square(KV_HEADS - 1)

                def score(h):
                    pe.wait_ge(s.qb, 1)
                    pe.wait_ge(s.kc, h + 1)
                    if h >= 1:
                        pe.wait_ge(s.scaled, h)
                    pe.matmul(g.ps[:, 4, :], flat(t.qb[:, h]), t.kT[:, h, 0:CTX], start=True, stop=True)
                    pe.matmul(g.ps[:, 5, 0:TOK], flat(t.qb[:, h]), t.kT[:, h, CTX:KV], start=True,
                              stop=True).then_inc(s.s, 1)

                def value(i):
                    n, half = i // 2, i % 2
                    if i < 2:
                        pe.wait_ge(s.sq, KV_HEADS)
                    else:
                        pe.wait_ge(s.vc, i - 1)
                    for c in range(NCH):
                        ins = pe.matmul(g.ps[:, i % 2, :], t.ctx[:, c, n * P:(n + 1) * P],
                                        w.wv[:, c, half * 512:(half + 1) * 512], start=(c == 0), stop=(c == NCH - 1))
                    ins.then_inc(s.v, 1)

                def turn(h):
                    pe.wait_ge(s.prob, h + 1)
                    if h >= 1:
                        pe.wait_ge(s.ot, h)
                    for n in range(NB):
                        pe.transpose(g.ps[:, 6, n * P:(n + 1) * P], t.pr[:, h % 2, n * P:(n + 1) * P], g.ident[:, :])
                    pe.transpose(g.ps[0:TOK, 7, 0:P], t.pr[:, h % 2, CTX:KV], g.ident[:, :]).then_inc(s.turned, 1)

                def mix(h):
                    pe.wait_ge(s.pt, h + 1)
                    if h == 0:
                        pe.wait_ge(s.vc, 2 * NB)
                        pe.wait_ge(s.vl, 16)
                    for n in range(NB + 1):
                        ins = pe.matmul(g.ps[:, 7, P:2 * P], t.V[:, n, h * P:(h + 1) * P], t.PT[:, n, :],
                                        start=(n == 0), stop=(n == NB))
                    ins.then_inc(s.mixed, 1)

                score(0)
                for i in range(NB * 2):
                    value(i)
                for h in range(KV_HEADS):
                    if h + 1 < KV_HEADS:
                        score(h + 1)
                    turn(h)
                    mix(h)

            @block.scalar
            def _(act):
                def copy_key(h):
                    act.wait_ge(s.k, h + 1)
                    act.copy(t.kT[:, h, 0:CTX], g.ps[:, h % 2, :]).then_inc(s.kc, 1)
                    if h >= 2:
                        act.wait_ge(s.ms, h - 1)
                    act.activation(t.sq[:, h % 2, :], g.ps[:, h % 2, :], ACT.Square).then_inc(s.sq, 1)

                def root(h):
                    act.wait_ge(s.ms, h + 1)
                    act.activation(t.R[:, h, 0:CTX], g.ps[:, 2, :], ACT.Sqrt, bias=w.eps[:, 0:1]).then_inc(s.root, 1)

                def copy_turned(h):
                    act.wait_ge(s.turned, h + 1)
                    if h >= 1:
                        act.wait_ge(s.mixed, h)
                    act.copy(flat(t.PT[:, 0:NB]), g.ps[:, 6, :])
                    act.copy(t.PT[0:TOK, NB, :], g.ps[0:TOK, 7, 0:P]).then_inc(s.pt, 1)

                copy_key(0)
                act.wait_ge(s.msl, 1)
                act.activation(t.R[:, :, CTX:KV], g.ps[:, 3, 0:KV_HEADS * TOK].rearrange("p (h n) -> p h n", n=TOK),
                               ACT.Sqrt, bias=w.eps[:, 0:1]).then_inc(s.rootl, 1)
                for h in range(1, KV_HEADS):
                    copy_key(h)
                    root(h - 1)
                root(KV_HEADS - 1)
                for i in range(NB * 2):
                    n, half = i // 2, i % 2
                    act.wait_ge(s.v, i + 1)
                    act.copy(t.V[:, n, half * 512:(half + 1) * 512], g.ps[:, i % 2, :]).then_inc(s.vc, 1)
                for h in range(KV_HEADS):
                    act.wait_ge(s.nmax, h + 1)
                    act.activation(t.pr[:, h % 2, :], t.pr[:, h % 2, :], ACT.Exp, bias=t.mx[:, h % 2, 1:2],
                                   scale=ATT_SCALE, accum_out=t.sum[:, h % 2, 0:1]).then_inc(s.expd, 1)
                    if h >= 1:
                        copy_turned(h - 1)
                copy_turned(KV_HEADS - 1)

            @block.vector
            def _(dve):
                link = chain(dve, s.step)
                dve.wait_ge(s.rootl, 1)
                for h in range(KV_HEADS):
                    dve.wait_ge(s.root, h + 1)
                    dve.reciprocal(t.R[:, h, :], t.R[:, h, :]).then_inc(s.rstd, 1)

                def scale(h):
                    dve.wait_ge(s.rstd, h + 1)
                    dve.wait_ge(s.s, h + 1)
                    if h >= 2:
                        dve.wait_ge(s.turned, h - 1)
                    link(dve.tensor_tensor(t.pr[:, h % 2, CTX:KV], g.ps[:, 5, 0:TOK], t.R[:, h, CTX:KV], ALU.mult))
                    dve.tensor_tensor(t.pr[:, h % 2, 0:CTX], g.ps[:, 4, :], t.R[:, h, 0:CTX],
                                      ALU.mult).then_inc(s.scaled, 1)
                    dve.wait_ge(s.scaled, h + 1)
                    link(dve.tensor_reduce(t.mx[:, h % 2, 0:1], t.pr[:, h % 2, :], AX.X, ALU.max))
                    dve.tensor_scalar(t.mx[:, h % 2, 1:2], t.mx[:, h % 2, 0:1], -ATT_SCALE, None,
                                      ALU.mult).then_inc(s.nmax, 1)

                def store(h):
                    dve.wait_ge(s.mixed, h + 1)
                    dve.tensor_copy(w.qT[:, h * GROUP:(h + 1) * GROUP, bass.ds(b * TOK, TOK)],
                                    g.ps[:, 7, P:2 * P].rearrange("p (a q) -> p a q", a=GROUP)).then_inc(s.ot, 1)

                scale(0)
                for h in range(KV_HEADS):
                    dve.wait_ge(s.expd, h + 1)
                    dve.reciprocal(t.sum[:, h % 2, 1:2], t.sum[:, h % 2, 0:1]).then_inc(s.norm, 1)
                    if h + 1 < KV_HEADS:
                        scale(h + 1)
                    store(h)
        release(nc, s)


def flat_heads(t):
    return t[:, :, :, :].rearrange("p k a q -> p (k a) q")


def project_out(nc, g, d, w, st):
    s = semaphores(nc, st, "po", "w0 w1 used out added")
    wo = st.enter_context(nc.sbuf_tensor("po_wo", [P, 2, GROUP, DIM], F32))
    s_w = (s.w0, s.w1)
    with nc.Block() as block:
        @block.sync
        def _(sp):
            for k in range(KV_HEADS):
                if k >= 2:
                    sp.wait_ge(s.used, k - 1)
                sp.dma_start(wo[:, k % 2, :, :], d.wo[:, k * GROUP:(k + 1) * GROUP, :]).then_inc(s_w[k % 2], 16)

        @block.tensor
        def _(pe):
            for k in range(KV_HEADS):
                pe.wait_ge(s_w[k % 2], 16 * (k // 2 + 1))
                for t in range(NT):
                    for a in range(GROUP):
                        h = k * GROUP + a
                        ins = pe.matmul(g.ps[:, t, :], w.qT[:, h, t * P:(t + 1) * P], wo[:, k % 2, a, :],
                                        start=(h == 0), stop=(h == Q_HEADS - 1))
                ins.then_inc(s.used, 1)

        @block.vector
        def _(dve):
            dve.wait_ge(s.used, KV_HEADS)
            for t in range(NT):
                dve.tensor_tensor(g.x[:, t, :], g.x[:, t, :], g.ps[:, t, :], ALU.add).then_inc(s.added, 1)
    release(nc, s)


HM, HIN, NST, NHH, HP, TAPS = 128, 256, 16, 4, 64, 7
SEQ, NSEQ = LAT, TOK
PAD = TAPS - 1
HYDRA_EPS = 1e-5


def hydra(nc, g, d):
    with ExitStack() as st:
        def sb(name, shape, dt=F32):
            return st.enter_context(nc.sbuf_tensor("hy_" + name, shape, dt))
        w = named({name: sb(name, shape) for name, shape in (
                            ("wd", [P, NCH, HM]), ("bd", [P, 1]), ("gate", [P, 1]), ("wu", [HM, DIM]), ("bu", [1, DIM]),
                            ("wx", [HM, HIN]), ("wbc", [HM, 48]), ("wz", [HM, HIN + 2 * NHH]), ("cw", [P, 3, TAPS]),
                            ("cb", [P, 3]), ("dtb", [P, 2 * NHH]), ("alog", [P, 2 * NHH]), ("D", [P, NHH]),
                            ("fcD", [P, 2, NHH]), ("nw", [P, 2]), ("wo", [P, 2, HM]), ("same", [P, P]),
                            ("at", [P, 2, SEQ]), ("past", [P, 2, SEQ]))})
        names = list(w.all)
        w.ones = sb("ones", [1, P])
        w.xmid = sb("xmid", [HM, ROWS])
        w.u = sb("u", [HM, ROWS])
        w.A = sb("A", [P, 2 * NHH])
        w.alpha = sb("alpha", [P, 1])
        w.cp = sb("cp", [P, 3, NSEQ, PAD + SEQ])
        w.acc = sb("acc", [P, 3, ROWS])
        w.c0 = sb("c0", [NST, ROWS])
        w.xtok = sb("xtok", [P, NT, HIN])
        w.sz = sb("sz", [P, NT, HIN])
        w.yz = sb("yz", [P, NT, HIN])
        w.y2 = sb("y2", [P, NT, HIN])
        w.ynT = sb("ynT", [P, 2, ROWS])
        w.dt = sb("dt", [P, NT, 2 * NHH])
        w.sp = sb("sp", [P, 4, NT * 2 * NHH])
        w.dA = sb("dA", [P, NT, 2 * NHH])
        w.spread = sb("spread", [P, NT, 2, NHH, SEQ])
        w.d0 = sb("d0", [P, NT, 2, NHH, SEQ])
        w.d1 = sb("d1", [P, NT, 2, NHH, SEQ])
        w.L = sb("L", [P, NT, 2, NHH, SEQ])
        w.Gm = sb("Gm", [P, NT, P])
        w.Mf = sb("Mf", [P, 2, NHH, P])
        w.Mb = sb("Mb", [P, 2, NHH, P])
        w.f = sb("f", [P, NT, NHH])
        w.ms = sb("ms", [P, NT])
        w.eps = sb("eps", [P, 1])

        s = semaphores(nc, st, "hy0", "loaded step down gelu consts")
        with nc.Block() as block:
            @block.sync
            def _(sp):
                for n in names:
                    src = d.all["hy_" + n]
                    if n in ("gate", "dtb", "alog", "D"):
                        src = src.partition_broadcast(P)
                    t = w.all[n]
                    sp.dma_start(t[tuple([slice(None)] * len(t.shape))], src).then_inc(s.loaded, 16)

            @block.gpsimd
            def _(pool):
                for t in (w.cp, w.Mf, w.Mb):
                    pool.memset(flat(t), 0.0)
                pool.memset(w.ones[:, :], 1.0)
                pool.memset(w.eps[:, :], HYDRA_EPS)

            @block.tensor
            def _(pe):
                pe.wait_ge(s.loaded, 16 * len(names))
                for c in range(NCH):
                    ins = pe.matmul(g.ps[:, 0, :], w.wd[:, c, :], g.xnT[:, c, :], start=(c == 0), stop=(c == NCH - 1))
                ins.then_inc(s.down, 1)

            @block.scalar
            def _(act):
                act.wait_ge(s.loaded, 16 * len(names))
                act.activation(w.A[:, :], w.alog[:, :], ACT.Exp).then_inc(s.consts, 1)
                act.activation(w.alpha[:, :], w.gate[:, :], ACT.Sigmoid).then_inc(s.consts, 1)
                act.wait_ge(s.down, 1)
                act.activation(w.xmid[:, :].rearrange("p (b l) -> p b l", b=NSEQ),
                               g.ps[:, 0, :].rearrange("p (l b) -> p b l", b=NSEQ), ACT.Gelu,
                               bias=w.bd[:, 0:1]).then_inc(s.gelu, 1)

            @block.vector
            def _(dve):
                dve.wait_ge(s.consts, 1)
                dve.tensor_scalar(w.A[:, :], w.A[:, :], -1.0, None, ALU.mult).then_inc(s.step, 1)
        release(nc, s)
        hydra_pass(nc, g, w, "hy1", w.xmid)
        hydra_pass(nc, g, w, "hy2", w.u)

        s = semaphores(nc, st, "hy3", "step blended up added")
        with nc.Block() as block:
            @block.vector
            def _(dve):
                link = chain(dve, s.step)
                link(dve.tensor_scalar(w.ynT[:, 0, :], w.xmid[:, :], w.alpha[:, 0:1], None, ALU.mult))
                link(dve.tensor_scalar(w.ms[:, 0:1], w.alpha[:, :], -1.0, 1.0, ALU.mult, ALU.add))
                link(dve.scalar_tensor_tensor(w.ynT[:, 1, :], w.u[:, :], w.ms[:, 0:1], w.ynT[:, 0, :],
                                              ALU.mult, ALU.add))
                dve.tensor_tensor(w.ynT[:, 0, :].rearrange("p (l b) -> p b l", b=NSEQ),
                                  w.ynT[:, 1, :].rearrange("p (b l) -> p b l", b=NSEQ),
                                  w.xmid[:, :].rearrange("p (b l) -> p b l", b=NSEQ), ALU.add).then_inc(s.blended, 1)
                link(dve.tensor_tensor(flat(g.x), flat(g.x), flat(g.xn), ALU.add))
                for t in range(NT):
                    dve.wait_ge(s.up, t + 1)
                    dve.tensor_tensor(g.x[:, t, :], g.x[:, t, :], g.ps[:, t, :], ALU.add).then_inc(s.added, 1)

            @block.tensor
            def _(pe):
                pe.wait_ge(s.blended, 1)
                for t in range(NT):
                    pe.matmul(g.ps[:, t, :], w.ynT[:, 0, t * P:(t + 1) * P], w.wu[:, :], start=True, stop=False)
                    pe.matmul(g.ps[:, t, :], w.ones[:, :], w.bu[:, :], start=False, stop=True).then_inc(s.up, 1)
        release(nc, s)


def hydra_pass(nc, g, w, name, src):
    with ExitStack() as st:
        s = semaphores(nc, st, name, "step xbc z dt cp e1 e2 sp da spread dab conv silu c0 xst xtok sz gram masked mat "
                 "y gated ms root yn yt ynT out")
        lanes = (P, P, 48)
        with nc.Block() as block:
            @block.tensor
            def _(pe):
                for i in range(2):
                    pe.matmul(g.ps[:, i, :], w.wx[:, i * P:(i + 1) * P], src[:, :], start=True,
                              stop=True).then_inc(s.xbc, 1)
                pe.matmul(g.ps[0:48, 2, :], w.wbc[:, :], src[:, :], start=True, stop=True).then_inc(s.xbc, 1)
                for t in range(NT):
                    pe.matmul(g.ps[:, 4 + t, 0:HIN + 2 * NHH], src[:, t * P:(t + 1) * P], w.wz[:, :], start=True,
                              stop=True).then_inc(s.z, 1)
                pe.wait_ge(s.spread, 1)
                pe.matmul(g.ps[:, 3, :], w.same[:, :], flat(w.spread), start=True, stop=True).then_inc(s.dab, 1)
                pe.wait_ge(s.silu, 2)
                for t in range(NT):
                    for i in range(2):
                        ins = pe.transpose(g.ps[:, t // 2, (t % 2) * HIN + i * P:(t % 2) * HIN + (i + 1) * P],
                                           w.acc[:, i, t * P:(t + 1) * P], g.ident[:, :])
                ins.then_inc(s.xst, 1)
                pe.wait_ge(s.c0, 1)
                for t in range(NT):
                    ins = pe.matmul(g.ps[:, 2, t * P:(t + 1) * P], w.acc[0:NST, 2, t * P:(t + 1) * P],
                                    w.c0[:, t * P:(t + 1) * P], start=True, stop=True)
                ins.then_inc(s.gram, 1)
                pe.wait_ge(s.sz, NT)
                pe.wait_ge(s.xtok, 1)
                for t in range(NT):
                    for i in range(2):
                        pe.matmul(g.ps[:, 4 + t, HIN:HIN + NHH], w.acc[:, i, t * P:(t + 1) * P], w.fcD[:, i, :],
                                  start=(i == 0), stop=(i == 1))
                    pe.wait_ge(s.mat, t + 1)
                    for h in range(NHH):
                        for n, M in enumerate((w.Mf, w.Mb)):
                            ins = pe.matmul(g.ps[:, 4 + t, h * HP:(h + 1) * HP], M[:, t % 2, h, :],
                                            w.xtok[:, t, h * HP:(h + 1) * HP], start=(n == 0), stop=(n == 1))
                    ins.then_inc(s.y, 1)
                for t in range(NT):
                    pe.wait_ge(s.yn, t + 1)
                    for i in range(2):
                        ins = pe.transpose(g.ps[:, i, t * P:(t + 1) * P], w.yz[:, t, i * P:(i + 1) * P], g.ident[:, :])
                ins.then_inc(s.yt, 1)
                for i in range(2):
                    pe.wait_ge(s.ynT, i + 1)
                    ins = pe.matmul(g.ps[:, 2, :], w.wo[:, i, :], w.ynT[:, i, :], start=(i == 0), stop=(i == 1))
                ins.then_inc(s.out, 1)

            @block.scalar
            def _(act):
                for i, n in enumerate(lanes):
                    act.wait_ge(s.xbc, i + 1)
                    act.copy(w.cp[0:n, i, :, PAD:], g.ps[0:n, i, :].rearrange("p (b l) -> p b l", l=SEQ)).then_inc(s.cp, 1)
                act.wait_ge(s.e1, 1)
                act.activation(w.sp[:, 1, :], w.sp[:, 0, :], ACT.Exp, scale=-1.0).then_inc(s.e2, 1)
                act.wait_ge(s.sp, 1)
                act.activation(flat(w.dA), w.sp[:, 3, :], ACT.Exp).then_inc(s.da, 1)
                act.wait_ge(s.dt, 1)
                for t in range(NT):
                    act.activation(w.sz[:, t, :], g.ps[:, 4 + t, 0:HIN], ACT.Silu).then_inc(s.sz, 1)
                for i, n in ((0, P), (1, P), (2, 48)):
                    act.wait_ge(s.conv, i + 1)
                    act.activation(w.acc[0:n, i, :], w.acc[0:n, i, :], ACT.Silu, bias=w.cb[0:n, i:i + 1]).then_inc(s.silu, 1)
                act.wait_ge(s.silu, 3)
                act.copy(w.c0[:, :], w.acc[32:32 + NST, 2, :]).then_inc(s.c0, 1)
                act.wait_ge(s.xst, 1)
                act.copy(w.xtok[:, :, :].rearrange("p (a t) n -> p a (t n)", a=2), g.ps[:, 0:2, :]).then_inc(s.xtok, 1)
                act.wait_ge(s.ms, 1)
                act.activation(w.ms[:, :], w.ms[:, :], ACT.Sqrt, scale=1.0 / HIN, bias=w.eps[:, 0:1]).then_inc(s.root, 1)
                act.wait_ge(s.yt, 1)
                for i in range(2):
                    act.activation(w.ynT[:, i, :], g.ps[:, i, :], ACT.Copy, scale=w.nw[:, i:i + 1]).then_inc(s.ynT, 1)
                act.wait_ge(s.out, 1)
                act.copy(w.u[:, :], g.ps[:, 2, :])

            @block.vector
            def _(dve):
                link = chain(dve, s.step)
                n8 = 2 * NHH
                rows = [w.sp[:, i, :] for i in range(4)]
                tiled = [r.rearrange("p (t k) -> p t k", t=NT) for r in rows]
                dve.wait_ge(s.z, NT)
                dve.tensor_tensor(w.dt[:, :, :], g.ps[:, 4:8, HIN:HIN + n8],
                                  w.dtb[:, None, :].broadcast_to([P, NT, n8]), ALU.add).then_inc(s.dt, 1)
                dve.wait_ge(s.dt, 1)
                dve.scalar_tensor_tensor(rows[0], flat(w.dt), -1.0, flat(w.dt), ALU.mult, ALU.max).then_inc(s.e1, 1)
                dve.wait_ge(s.e2, 1)
                link(dve.tensor_scalar(rows[2], rows[1], 2.0, None, ALU.add))
                link(dve.reciprocal(rows[2], rows[2]))
                link(dve.tensor_tensor(rows[1], rows[1], rows[2], ALU.mult))
                link(dve.tensor_tensor(rows[2], rows[1], rows[1], ALU.mult))
                link(dve.tensor_scalar(rows[3], rows[2], 1.0 / 15, 1.0 / 13, ALU.mult, ALU.add))
                for k in (11, 9, 7, 5, 3, 1):
                    link(dve.tensor_tensor(rows[3], rows[3], rows[2], ALU.mult))
                    link(dve.tensor_scalar(rows[3], rows[3], 1.0 / k, None, ALU.add))
                link(dve.scalar_tensor_tensor(rows[3], rows[3], 2.0, rows[1], ALU.mult, ALU.mult))
                link(dve.scalar_tensor_tensor(flat(w.dt), flat(w.dt), 0.0, rows[3], ALU.max, ALU.add))
                dve.tensor_tensor(tiled[3], w.dt[:, :, :], w.A[:, None, :].broadcast_to([P, NT, n8]),
                                  ALU.mult).then_inc(s.sp, 1)
                dve.wait_ge(s.da, 1)
                for way in range(2):
                    ins = dve.tensor_tensor(
                        w.spread[:, :, way, :, :],
                        w.dA[:, :, way * NHH:(way + 1) * NHH, None].broadcast_to([P, NT, NHH, SEQ]),
                        w.at[:, way:way + 1, None, :].broadcast_to([P, NT, NHH, SEQ]), ALU.mult)
                    if way == 0:
                        link(ins)
                ins.then_inc(s.spread, 1)
                for i, n in enumerate(lanes):
                    dve.wait_ge(s.cp, i + 1)
                    acc = w.acc[0:n, i, :].rearrange("p (b l) -> p b l", l=SEQ)
                    link(dve.tensor_scalar(acc, w.cp[0:n, i, :, 0:SEQ], w.cw[0:n, i, 0:1], None, ALU.mult))
                    for k in range(1, TAPS):
                        ins = dve.scalar_tensor_tensor(acc, w.cp[0:n, i, :, k:k + SEQ], w.cw[0:n, i, k:k + 1], acc,
                                                       ALU.mult, ALU.add)
                        if k < TAPS - 1:
                            link(ins)
                    ins.then_inc(s.conv, 1)
                dve.wait_ge(s.dab, 1)
                dab = g.ps[:, 3, :].rearrange("p (t w h l) -> p t w h l", t=NT, w=2, h=NHH)
                for way in range(2):
                    link(dve.tensor_tensor(w.d0[:, :, way, :, :], dab[:, :, way, :, :],
                                           w.past[:, way:way + 1, None, :].broadcast_to([P, NT, NHH, SEQ]), ALU.mult))
                    link(dve.tensor_tensor(
                        w.d1[:, :, way, :, :],
                        w.dt[:, :, way * NHH:(way + 1) * NHH, None].broadcast_to([P, NT, NHH, SEQ]),
                        w.at[:, way:way + 1, None, :].broadcast_to([P, NT, NHH, SEQ]), ALU.mult))
                link(dve.tensor_tensor_scan(flat(w.L), flat(w.d0), flat(w.d1), 0.0, ALU.mult, ALU.add))
                dve.wait_ge(s.gram, 1)
                dve.tensor_tensor(w.Gm[:, :, :], g.ps[:, 2, :].rearrange("p (t n) -> p t n", t=NT),
                                  w.same[:, None, :].broadcast_to([P, NT, P]), ALU.mult).then_inc(s.masked, 1)
                dve.wait_ge(s.masked, 1)
                for t in range(NT):
                    if t >= 2:
                        dve.wait_ge(s.y, t - 1)
                    dims = [NHH, 8, SEQ - 1]
                    dve.tensor_tensor(custom(w.Mf[:, t % 2], 1, [[P, NHH], [SEQ, 8], [1, SEQ - 1]]),
                                      custom(w.Gm[:, t], 0, [[0, NHH], [SEQ, 8], [1, SEQ - 1]]),
                                      custom(w.L[:, t, 0], 0, [[SEQ, NHH], [0, 8], [1, SEQ - 1]]), ALU.mult)
                    dve.tensor_tensor(custom(w.Mb[:, t % 2], 0, [[P, NHH], [SEQ, 8], [1, SEQ - 1]]),
                                      custom(w.Gm[:, t], 1, [[0, NHH], [SEQ, 8], [1, SEQ - 1]]),
                                      custom(w.L[:, t, 1], SEQ - 2, [[SEQ, NHH], [0, 8], [-1, SEQ - 1]]),
                                      ALU.mult).then_inc(s.mat, 1)
                dve.wait_ge(s.y, NT)
                dve.wait_ge(s.xtok, 1)
                dve.wait_ge(s.sz, NT)
                heads = lambda a: a.rearrange("p t (h n) -> p (t h) n", h=NHH)
                link(dve.tensor_tensor(w.f[:, :, :], g.ps[:, 4:8, HIN:HIN + NHH],
                                       w.D[:, None, :].broadcast_to([P, NT, NHH]), ALU.add))
                link(dve.tensor_tensor(heads(w.yz[:, :, :]), heads(w.xtok[:, :, :]),
                                       flat(w.f)[:, :, None].broadcast_to([P, NT * NHH, HP]), ALU.mult))
                link(dve.tensor_tensor(w.yz[:, :, :], w.yz[:, :, :], g.ps[:, 4:8, 0:HIN], ALU.add))
                link(dve.tensor_tensor(w.yz[:, :, :], w.yz[:, :, :], w.sz[:, :, :], ALU.mult))
                link(dve.tensor_tensor(w.y2[:, :, :], w.yz[:, :, :], w.yz[:, :, :], ALU.mult))
                dve.tensor_reduce(w.ms[:, :], w.y2[:, :, :], AX.X, ALU.add).then_inc(s.ms, 1)
                dve.wait_ge(s.root, 1)
                link(dve.reciprocal(w.ms[:, :], w.ms[:, :]))
                for t in range(NT):
                    dve.tensor_scalar(w.yz[:, t, :], w.yz[:, t, :], w.ms[:, t:t + 1], None, ALU.mult).then_inc(s.yn, 1)
        release(nc, s)


def store_result(nc, g, d):
    with ExitStack() as st:
        s = semaphores(nc, st, "fin", "stored")
        with nc.Block() as block:
            @block.sync
            def _(sp):
                for t in range(NT):
                    sp.dma_start(d.out[t * P:(t + 1) * P, :], g.x[:, t, :]).then_inc(s.stored, 16)
                sp.wait_ge(s.stored, 16 * NT)


_SCRATCH = {
    "q_scratch": ((LAT, 3, DIM), "int32"),
    "keys_hi": ((LAT, METHODS, DIM), "float32"),
    "keys_lo": ((LAT, METHODS, DIM), "float32"),
    "xatt": ((ROWS, DIM), "float32"),
    "v_lat": ((ROWS, KV_HEADS * P), "float32"),
}


def program(nc, d):
    with ExitStack() as st:
        shared = tensors(nc, st, "g", (("x", [P, NT, DIM], F32), ("xn", [P, NT, DIM], F32), ("xnT", [P, NCH, ROWS], F32),
                                ("ident", [P, P], F32), ("identb", [P, P], BF16), ("eps", [P, 1], F32)))
        shared["ps"] = st.enter_context(nc.psum_tensor("ps", [P, 8, 512], F32))
        with ExitStack() as sa:
            g = named(shared | tensors(nc, sa, "g", (("targets", [P, DIM + EXTRA], F16), ("mask", [P, 2 * U_MAX, HD], BF16),
                                    ("ident16", [P, P], F16),
                                    ("avg1", [P, P], F32), ("avg2", [P, P], F32),
                                    ("key_hi", [P, NCH, LAT * METHODS], F32),
                                    ("key_lo", [P, NCH, LAT * METHODS], F32))))
            load_constants(nc, g, d)
            layernorm_and_turn(nc, g, "ln0")
            curve_keys(nc, g, d)
            graph_layers(nc, g, d)
        g = named(shared)
        add_point_attention(nc, g, d)
        layernorm_and_turn(nc, g, "ln1")
        bound_attention(nc, g, d)
        layernorm_and_turn(nc, g, "ln2")
        experts(nc, g, d, "e0", 0, 2.0, None)
        layernorm_and_turn(nc, g, "ln3")
        cross_attention(nc, g, d)
        layernorm_and_turn(nc, g, "ln4")
        hydra(nc, g, d)
        layernorm_and_turn(nc, g, "ln5")
        experts(nc, g, d, "e1", 4 * EXPERTS, 1.0 / RANK, 3 * ROWS // EXPERTS)
        store_result(nc, g, d)


def _layout(i):
    f = np.float32
    out = {}
    out["x"] = np.asarray(i["x"]).reshape(ROWS, DIM)
    out["coords"] = np.ascontiguousarray(np.asarray(i["ctx_4096"])[:, 0:3, :])
    out["ident"] = np.eye(P, dtype=f)
    t = list(range(DIM)) + [DIM - 1] * TAIL
    for n in range(HEAD_POINTS):
        t += [min(j, n + KNN // 2) for j in range(KNN)]
    out["targets"] = np.array(t, f)
    j = np.arange(HD) // KNN
    out["pointmask"] = np.where(j[np.arange(P) % HD][:, None] == j[None, :], 0.0, -BIG).astype(f)
    q = np.arange(P)
    out["avg1"] = (0.25 * (q[:, None] % 32 == q[None, :] % 32)).astype(f)
    out["avg2"] = (0.25 * (q[:, None] % 64 == q[None, :] % 64)).astype(f)
    out["nidx"] = ((q % 8)[:, None] * 64 + np.arange(64)[None, :]).astype(np.int32)
    for l, (perm, name) in enumerate((([2, 0, 3, 1], "1"), ([1, 3, 0, 2], "2"))):
        place = [perm.index(m) for m in range(METHODS)]
        lin = np.asarray(i[f"L0_xattn_W_lin{name}"]).reshape(64, 2, HEADS, 8, METHODS)
        out[f"lin{l}"] = np.ascontiguousarray(lin[:, :, :, :, place].transpose(0, 1, 2, 4, 3).reshape(64, 2, P))
        conv = np.asarray(i[f"L0_xattn_W_conv{name}"])
        out[f"conv{l}"] = np.ascontiguousarray(np.tile(conv.T, (1, P // OUTS[l])))
        out[f"lbias{l}"] = np.asarray(i[f"L0_xattn_b_lin{name}"]).reshape(64, 1)
    w3 = np.asarray(i["L0_xattn_W_conv3"])
    for name, at in (("w3a", 0), ("w3b", 32)):
        z = np.zeros((HEADS, METHODS, 8, 32), f)
        z[:, 0] = w3[:, at:at + 32].T.reshape(HEADS, 8, 32)
        out[name] = z.reshape(P, 32)
    z = np.zeros((2, 64, 2, 32), f)
    for c in range(2):
        z[c, :, c, :] = w3[:, 64:].T
    out["w3c"] = z.reshape(P, 2, 32)
    A = lambda n: np.asarray(i[n])

    def chunked(wt):
        return np.ascontiguousarray(wt.reshape(NCH, P, -1).transpose(1, 0, 2))

    out["bind"] = np.ascontiguousarray(np.stack([A("L0_attn_bv_q"), A("L0_attn_bv_k"), A("L0_attn_bv_v")], 1))
    out["sel4"] = np.ascontiguousarray(np.broadcast_to(np.eye(NCH, dtype=f)[:, :, None], (NCH, NCH, P)))
    out["causal"] = ((q[:, None] // TOK == q[None, :] // TOK) & (q[:, None] <= q[None, :])).astype(f)
    out["iota8"] = np.arange(EXPERTS).astype(f)
    out["e0_wa"] = chunked(np.concatenate([A("L0_ffn_gate_w").T, A("L0_ffn_lora_A").reshape(P, DIM).T], 1))
    out["e0_wb"] = chunked(A("L0_ffn_base_w").T)
    out["e0_bias"] = A("L0_ffn_base_b").reshape(1, DIM)
    out["e0_lb"] = np.ascontiguousarray(A("L0_ffn_lora_B").transpose(0, 2, 1).reshape(P, DIM))
    out["e1_wa"] = chunked(np.concatenate([A("L1_ffn_gw1").T, A("L1_ffn_lora_A").transpose(1, 0, 2).reshape(DIM, P)], 1))
    out["e1_wb"] = chunked(A("L1_ffn_weight").T)
    out["e1_bias"] = np.zeros((1, DIM), f)
    out["e1_lb"] = np.ascontiguousarray(A("L1_ffn_lora_B").reshape(P, DIM))
    out["e1_rows"] = np.stack([A("L1_ffn_gb1"), A("L1_ffn_ln_gamma"), A("L1_ffn_ln_beta")])
    out["e1_gb2"] = A("L1_ffn_gb2")
    out["e1_gw2"] = np.ascontiguousarray(A("L1_ffn_gw2").T)
    out["ctxT"] = np.ascontiguousarray(A("ctx_4096").transpose(0, 2, 1).reshape(LAT, NCH, P, CTX).transpose(0, 2, 1, 3))
    out["wq"], out["wk"], out["wv"] = (chunked(A("L1_xattn_" + n)) for n in ("Wq", "Wk", "Wv"))
    out["wo"] = np.ascontiguousarray(A("L1_xattn_Wo").reshape(Q_HEADS, P, DIM).transpose(1, 0, 2))
    out["qk_norm"] = np.ascontiguousarray(np.stack([A("L1_xattn_q_norm_w"), A("L1_xattn_k_norm_w")], 1))
    out["mean128"] = np.full((P, P), 1.0 / P, f)
    H = lambda n: A("L1_attn_" + n)
    out["hy_wd"] = chunked(H("w_down").T)
    out["hy_bd"] = H("b_down").reshape(HM, 1)
    out["hy_gate"] = H("gate1").reshape(1)
    out["hy_wu"] = np.ascontiguousarray(H("w_up").T)
    out["hy_bu"] = H("b_up").reshape(1, DIM)
    win = H("hy_in_w").T
    X0, B0, C0, D0 = HIN, 2 * HIN, 2 * HIN + NST, 2 * HIN + 2 * NST
    gap = np.zeros((HM, 32 - NST), f)
    out["hy_wx"] = np.ascontiguousarray(win[:, X0:B0])
    out["hy_wbc"] = np.concatenate([win[:, B0:C0], gap, win[:, C0:D0]], 1)
    out["hy_wz"] = np.concatenate([win[:, 0:X0], win[:, D0:]], 1)

    def channels(v):
        z = np.zeros((P, 3, v.shape[1]), f)
        z[:, 0], z[:, 1] = v[0:P], v[P:2 * P]
        z[0:NST, 2], z[32:32 + NST, 2] = v[HIN:HIN + NST], v[HIN + NST:]
        return z
    out["hy_cw"] = channels(H("hy_conv_w")[:, 0, :])
    out["hy_cb"] = channels(H("hy_conv_b")[:, None])[:, :, 0]
    out["hy_dtb"] = np.tile(H("hy_dt_bias"), 2)
    out["hy_alog"] = np.tile(H("hy_A_log"), 2)
    out["hy_D"] = H("hy_D")
    out["hy_fcD"] = np.ascontiguousarray(H("hy_fcD_w").T.reshape(2, P, NHH).transpose(1, 0, 2))
    out["hy_nw"] = np.ascontiguousarray(H("hy_norm_w").reshape(2, P).T)
    out["hy_wo"] = np.ascontiguousarray(H("hy_out_w").T.reshape(2, P, HM).transpose(1, 0, 2))
    out["hy_same"] = (q[:, None] // SEQ == q[None, :] // SEQ).astype(f)
    pos, col = (q % SEQ)[:, None], np.arange(SEQ)[None, :]
    out["hy_at"] = np.stack([pos == col, pos == SEQ - 1 - col], 1).astype(f)
    out["hy_past"] = np.stack([col > pos, SEQ - 1 - col < pos], 1).astype(f)
    return out


def kernel(**inputs):
    import concourse.bacc as _bacc
    from concourse.bass_utils import run_bass_kernel_spmd as _run

    nc = _bacc.Bacc("TRN2", target_bir_lowering=False, num_devices=1)
    tensor, arrays = {}, {}
    for name, a in _layout(inputs).items():
        arrays["in_" + name] = a
        tensor[name] = nc.dram_tensor("in_" + name, a.shape, mybir.dt.from_np(a.dtype), kind="ExternalInput").ap()
    for name, (shape, dt) in _SCRATCH.items():
        tensor[name] = nc.dram_tensor("scratch_" + name, shape, mybir.dt.from_np(np.dtype(dt)), kind="Internal").ap()
    tensor["out"] = nc.dram_tensor("out_0_dram", (ROWS, DIM), F32, kind="ExternalOutput").ap()
    program(nc, named(tensor))
    r = _run(nc, [arrays], core_ids=[0])
    return r.results[0]["out_0_dram"].reshape(LAT, TOK, DIM)
```

```python
from contextlib import ExitStack

import numpy as np

import concourse.bass as bass
from concourse import mybir

F32 = mybir.dt.float32
F16 = mybir.dt.float16
BF16 = mybir.dt.bfloat16
I32 = mybir.dt.int32
U32 = mybir.dt.uint32
ALU = mybir.AluOpType
ACT = mybir.ActivationFunctionType
AX = mybir.AxisListType

P = 128
LAT, TOK, DIM = 16, 32, 512
ROWS = LAT * TOK
NT = ROWS // P
NCH = DIM // P
LN_EPS = 1e-5

BITS = 10
METHODS = 4
KNN = 10
C_IN = 32
HEADS = 4
HD = 32
NS = 2
PAIRS = 2
U_ALL = 43
BATCH_U = (8, 8, 8, 8, 8, 3)
U_MAX = 8
NB = len(BATCH_U)
SC = HEADS * U_MAX * HD
BLK = 3 * KNN
F_LEFT = KNN // 2
F_COLS = F_LEFT + DIM + 8
TAIL = KNN // 2 - 1
HEAD_POINTS = KNN // 2
EXTRA = TAIL + HEAD_POINTS * KNN
BIG = float(2 ** 20)
OUTS = (32, 64)
INV_SQRT_HD = float(1.0 / np.sqrt(np.float32(HD)))


def chain(eng, sem):
    count = [0]

    def link(ins):
        count[0] += 1
        ins.then_inc(sem, 1)
        eng.wait_ge(sem, count[0])
    return link


def named(items):
    return type("Named", (), {"all": items, **items})


def semaphores(nc, stack, stage, names):
    return named({n: stack.enter_context(nc.semaphore(f"{stage}_{n}")) for n in names.split()})


def tensors(nc, stack, stage, specs):
    return {n: stack.enter_context(nc.sbuf_tensor(f"{stage}_{n}", shape, dt)) for n, shape, dt in specs}


def release(nc, s):
    numbers = sorted(sem.num for sem in s.all.values())
    first = numbers[0]
    for n, after in zip(numbers, numbers[1:] + [None]):
        if after != n + 1:
            nc.sync.sem_clear(range(first, n + 1))
            first = after
    nc.all_engine_barrier()


def custom(ap, offset, dims):
    return bass.AP(ap.tensor, ap.offset + offset, [list(ap.ap[0])] + dims)


def load_constants(nc, g, d):
    with ExitStack() as st:
        s = semaphores(nc, st, "const", "loaded step")
        tgt_f = st.enter_context(nc.sbuf_tensor("tgt_f", [P, DIM + EXTRA], F32))
        msk_f = st.enter_context(nc.sbuf_tensor("msk_f", [P, HD], F32))
        with nc.Block() as block:
            @block.sync
            def _(sp):
                sp.dma_start(g.ident[:, :], d.ident).then_inc(s.loaded, 16)
                sp.dma_start(tgt_f[:, :], d.targets.partition_broadcast(P)).then_inc(s.loaded, 16)
                sp.dma_start(msk_f[:, :], d.pointmask).then_inc(s.loaded, 16)
                sp.dma_start(g.avg1[:, :], d.avg1).then_inc(s.loaded, 16)
                sp.dma_start(g.avg2[:, :], d.avg2).then_inc(s.loaded, 16)
                for t in range(NT):
                    sp.dma_start(g.x[:, t, :], d.x[t * P:(t + 1) * P, :]).then_inc(s.loaded, 16)

            @block.vector
            def _(dve):
                dve.memset(g.eps[:, :], LN_EPS).then_inc(s.step, 1)
                dve.wait_ge(s.loaded, 16 * (5 + NT))
                dve.tensor_copy(g.identb[:, :], g.ident[:, :]).then_inc(s.step, 1)
                dve.tensor_copy(g.ident16[:, :], g.ident[:, :]).then_inc(s.step, 1)
                dve.tensor_copy(g.targets[:, :], tgt_f[:, :]).then_inc(s.step, 1)
                dve.tensor_copy(g.mask[:, :, :],
                                msk_f[:, None, :].broadcast_to([P, 2 * U_MAX, HD])).then_inc(s.step, 1)
        release(nc, s)


def layernorm_and_turn(nc, g, name):
    with ExitStack() as st:
        s = semaphores(nc, st, name, "step var root rstd normed turned copied")
        stats = st.enter_context(nc.sbuf_tensor(f"{name}_stats", [P, NT, 6], F32))
        mv = st.enter_context(nc.sbuf_tensor(f"{name}_mv", [P, NT, 2], F32))
        root = st.enter_context(nc.sbuf_tensor(f"{name}_root", [P, NT], F32))
        rstd = st.enter_context(nc.sbuf_tensor(f"{name}_rstd", [P, NT], F32))
        with nc.Block() as block:
            @block.vector
            def _(dve):
                for t in range(NT):
                    dve.bn_stats(stats[:, t, :], g.x[:, t, :]).then_inc(s.step, 1)
                for t in range(NT):
                    dve.wait_ge(s.step, t + 1)
                    dve.bn_aggr(mv[:, t, :], stats[:, t, :]).then_inc(s.var, 1)
                dve.wait_ge(s.root, 1)
                dve.wait_ge(s.var, NT)
                dve.reciprocal(rstd[:, :], root[:, :]).then_inc(s.rstd, 1)
                dve.wait_ge(s.rstd, 1)
                for t in range(NT):
                    dve.tensor_scalar(g.xn[:, t, :], g.x[:, t, :], mv[:, t, 0:1], rstd[:, t:t + 1],
                                      ALU.subtract, ALU.mult).then_inc(s.normed, 1)

            @block.scalar
            def _(act):
                act.wait_ge(s.var, NT)
                act.activation(root[:, :], mv[:, :, 1], ACT.Sqrt, bias=g.eps[:, 0:1]).then_inc(s.root, 1)
                for t in range(NT):
                    act.wait_ge(s.turned, t + 1)
                    act.copy(g.xnT[:, :, t * P:(t + 1) * P],
                             g.ps[:, t, :].rearrange("p (c r) -> p c r", c=NCH)).then_inc(s.copied, 1)

            @block.tensor
            def _(pe):
                for t in range(NT):
                    pe.wait_ge(s.normed, t + 1)
                    for c in range(NCH):
                        ins = pe.transpose(g.ps[:, t, c * P:(c + 1) * P], g.xn[:, t, c * P:(c + 1) * P],
                                           g.ident[:, :])
                    ins.then_inc(s.turned, 1)
        release(nc, s)


def curve_keys(nc, g, d):
    B, N8, NC8 = LAT, 8, DIM // 8
    with ExitStack() as st:
        def sb(name, shape, dt):
            return st.enter_context(nc.sbuf_tensor(name, shape, dt))
        s = semaphores(nc, st, "keys", "loaded step stored quantised reloaded keyed written back turned")
        co = sb("co", [B, 3, DIM], F32)
        lo = sb("c_lo", [B, 3], F32)
        hi = sb("c_hi", [B, 3], F32)
        w = sb("c_w", [B, 12, 3], F32)
        fl = sb("c_fl", [B, 3, DIM], F32)
        gt = sb("c_gt", [B, 3, DIM], F32)
        qi = sb("c_qi", [B, 3, DIM], I32)
        q = sb("q8", [P, 3, NC8], I32)
        nidx = sb("nidx", [P, NC8], I32)
        X = sb("hX", [P, 3, METHODS, NC8], I32)
        M = sb("hM", [P, 2, NC8], I32)
        N = sb("hN", [P, 2, NC8], I32)
        T = sb("hT", [P, 2, NC8], I32)
        S = sb("hS", [P, 3, METHODS, NC8], I32)
        K = sb("hK", [P, METHODS, NC8], I32)
        KH = sb("hKH", [P, METHODS, NC8], I32)
        KL = sb("hKL", [P, METHODS, NC8], I32)
        FH = sb("fH", [P, METHODS, NC8], F32)
        FL = sb("fL", [P, METHODS, NC8], F32)
        rows = sb("krows", [LAT * METHODS, 2, DIM], F32)
        with nc.Block() as block:
            @block.sync
            def _(sp):
                sp.dma_start(co[:, :, :], d.coords).then_inc(s.loaded, 16)
                sp.dma_start(nidx[:, :], d.nidx).then_inc(s.loaded, 16)
                sp.wait_ge(s.quantised, 1)
                sp.dma_start(d.q_scratch, qi[:, :, :]).then_inc(s.stored, 16)
                sp.wait_ge(s.stored, 16)
                for b in range(B):
                    sp.dma_start(q[b * N8:(b + 1) * N8, :, :],
                                 d.q_scratch[b].rearrange("c (a n) -> a c n", a=N8)).then_inc(s.reloaded, 16)
                sp.wait_ge(s.keyed, 1)
                for b in range(B):
                    sp.dma_start(d.keys_hi[b].rearrange("m (a n) -> a m n", a=N8),
                                 FH[b * N8:(b + 1) * N8, :, :]).then_inc(s.written, 16)
                    sp.dma_start(d.keys_lo[b].rearrange("m (a n) -> a m n", a=N8),
                                 FL[b * N8:(b + 1) * N8, :, :]).then_inc(s.written, 16)
                sp.wait_ge(s.written, 32 * B)
                sp.dma_start(rows[:, 0, :], d.keys_hi.rearrange("b m n -> (b m) n")).then_inc(s.back, 16)
                sp.dma_start(rows[:, 1, :], d.keys_lo.rearrange("b m n -> (b m) n")).then_inc(s.back, 16)

            @block.vector
            def _(dve):
                link = chain(dve, s.step)
                dve.wait_ge(s.loaded, 32)
                link(dve.tensor_reduce(lo[:, :], co[:, :, :], AX.X, ALU.min))
                link(dve.tensor_reduce(hi[:, :], co[:, :, :], AX.X, ALU.max))
                den, r, q0, qh, ql, dh, dl, e = (w[:, i, :] for i in range(8))
                link(dve.tensor_tensor(hi[:, :], hi[:, :], lo[:, :], ALU.subtract))
                link(dve.tensor_scalar(den, hi[:, :], 1e-6, None, ALU.add))
                link(dve.reciprocal(r, den))
                link(dve.tensor_scalar(q0, r, float(2 ** BITS - 1), None, ALU.mult))
                for whole, high, low in ((q0, qh, ql), (den, dh, dl)):
                    link(dve.tensor_scalar(high.bitcast(I32), whole.bitcast(I32), -4096, None,
                                           ALU.bitwise_and))
                    link(dve.tensor_tensor(low, whole, high, ALU.subtract))
                link(dve.tensor_tensor(e, qh, dh, ALU.mult))
                link(dve.tensor_scalar(e, e, -1.0, float(2 ** BITS - 1), ALU.mult, ALU.add))
                for a, b in ((qh, dl), (ql, dh), (ql, dl)):
                    link(dve.tensor_tensor(w[:, 8, :], a, b, ALU.mult))
                    link(dve.tensor_tensor(e, e, w[:, 8, :], ALU.subtract))
                link(dve.tensor_tensor(e, e, r, ALU.mult))
                link(dve.tensor_tensor(q0, q0, e, ALU.add))
                for c in range(3):
                    link(dve.tensor_scalar(co[:, c, :], co[:, c, :], lo[:, c:c + 1], w[:, 2, c:c + 1],
                                           ALU.subtract, ALU.mult))
                link(dve.tensor_copy(qi[:, :, :], co[:, :, :]))
                link(dve.tensor_copy(fl[:, :, :], qi[:, :, :]))
                link(dve.tensor_tensor(gt[:, :, :], fl[:, :, :], co[:, :, :], ALU.is_gt))
                link(dve.tensor_tensor(fl[:, :, :], fl[:, :, :], gt[:, :, :], ALU.subtract))
                link(dve.tensor_scalar(fl[:, :, :], fl[:, :, :], 0.0, float(2 ** BITS - 1), ALU.max, ALU.min))
                dve.tensor_copy(qi[:, :, :], fl[:, :, :]).then_inc(s.quantised, 1)
                dve.wait_ge(s.reloaded, 16 * B)
                for m in range(METHODS):
                    for c in range(3):
                        link(dve.tensor_copy(X[:, c, m, :], q[:, (1 - c if m % 2 and c < 2 else c), :]))
                H = [X[:, c, 2:4, :] for c in range(3)]

                def sign_of_bit(src, bit):
                    link(dve.tensor_scalar(M[:, :, :], src, 31 - bit, 31, ALU.logical_shift_left,
                                           ALU.arith_shift_right))

                for bit in range(BITS - 1, 0, -1):
                    low = (1 << bit) - 1
                    sign_of_bit(H[0], bit)
                    link(dve.scalar_tensor_tensor(H[0], M[:, :, :], low, H[0], ALU.bitwise_and, ALU.bitwise_xor))
                    for c in (1, 2):
                        sign_of_bit(H[c], bit)
                        link(dve.tensor_scalar(N[:, :, :], M[:, :, :], -1, low, ALU.bitwise_xor, ALU.bitwise_and))
                        link(dve.tensor_tensor(T[:, :, :], H[0], H[c], ALU.bitwise_xor))
                        link(dve.tensor_tensor(T[:, :, :], T[:, :, :], N[:, :, :], ALU.bitwise_and))
                        link(dve.scalar_tensor_tensor(M[:, :, :], M[:, :, :], low, H[0], ALU.bitwise_and,
                                                      ALU.bitwise_xor))
                        link(dve.tensor_tensor(H[0], M[:, :, :], T[:, :, :], ALU.bitwise_xor))
                        link(dve.tensor_tensor(H[c], H[c], T[:, :, :], ALU.bitwise_xor))
                link(dve.tensor_tensor(H[1], H[1], H[0], ALU.bitwise_xor))
                link(dve.tensor_tensor(H[2], H[2], H[1], ALU.bitwise_xor))
                link(dve.memset(T[:, :, :], 0))
                for bit in range(BITS - 1, 0, -1):
                    sign_of_bit(H[2], bit)
                    link(dve.scalar_tensor_tensor(T[:, :, :], M[:, :, :], (1 << bit) - 1, T[:, :, :],
                                                  ALU.bitwise_and, ALU.bitwise_xor))
                for c in range(3):
                    link(dve.tensor_tensor(H[c], H[c], T[:, :, :], ALU.bitwise_xor))
                for shift, keep in ((16, 0x030000FF), (8, 0x0300F00F), (4, 0x030C30C3), (2, 0x09249249)):
                    link(dve.scalar_tensor_tensor(S[:, :, :, :], X[:, :, :, :], shift, X[:, :, :, :],
                                                  ALU.logical_shift_left, ALU.bitwise_or))
                    link(dve.tensor_scalar(X[:, :, :, :], S[:, :, :, :], keep, None, ALU.bitwise_and))
                link(dve.scalar_tensor_tensor(K[:, :, :], X[:, 0, :, :], 1, X[:, 1, :, :],
                                              ALU.logical_shift_left, ALU.bitwise_or))
                link(dve.scalar_tensor_tensor(K[:, :, :], K[:, :, :], 1, X[:, 2, :, :],
                                              ALU.logical_shift_left, ALU.bitwise_or))
                link(dve.tensor_scalar(KH[:, :, :], K[:, :, :], 15, None, ALU.logical_shift_right))
                link(dve.tensor_scalar(KL[:, :, :], K[:, :, :], 32767, 9, ALU.bitwise_and,
                                       ALU.logical_shift_left))
                link(dve.tensor_tensor(KL[:, :, :], KL[:, :, :],
                                       nidx[:, None, :].broadcast_to([P, METHODS, NC8]), ALU.bitwise_or))
                link(dve.tensor_scalar(FH[:, :, :], KH[:, :, :], float(2 ** 24), None, ALU.mult))
                dve.tensor_scalar(FL[:, :, :], KL[:, :, :], -1.0, None, ALU.mult).then_inc(s.keyed, 1)

            @block.tensor
            def _(pe):
                pe.wait_ge(s.back, 32)
                n = LAT * METHODS
                for half in range(2):
                    for c in range(NCH):
                        ins = pe.transpose(g.ps[:, half, c * n:(c + 1) * n], rows[:, half, c * P:(c + 1) * P],
                                           g.ident[0:n, 0:n])
                ins.then_inc(s.turned, 1)

            @block.scalar
            def _(act):
                n = LAT * METHODS
                act.wait_ge(s.turned, 1)
                act.copy(g.key_hi[:, :, :], g.ps[:, 0, 0:NCH * n].rearrange("p (c n) -> p c n", c=NCH))
                act.mul(g.key_lo[:, :, :], g.ps[:, 1, 0:NCH * n].rearrange("p (c n) -> p c n", c=NCH), -1.0)
        release(nc, s)


def graph_weights(nc, g, d, w):
    with ExitStack() as st:
        s = semaphores(nc, st, "gw", "loaded step zeroed multiplied split")
        e, rows = flat(w.e), flat(w.row_hi)
        lin = [e[0:64, 256 * l:256 * (l + 1)].rearrange("p (a n) -> p a n", a=2) for l in range(2)]
        conv = [e[0:64, 512 + P * l:512 + P * (l + 1)] for l in range(2)]
        bias = [e[0:64, 768 + l:769 + l] for l in range(2)]
        cf = [rows[:, 512 * l:512 * (l + 1)].rearrange("p (c o) -> p c o", c=4) for l in range(2)]
        zeroed = (cf[0], cf[1], w.spread, w.x16, w.sorted, w.centre, w.centre16, w.xT)
        with nc.Block() as block:
            @block.sync
            def _(sp):
                for l in range(2):
                    sp.dma_start(lin[l], d.all[f"lin{l}"]).then_inc(s.loaded, 16)
                    sp.dma_start(conv[l], d.all[f"conv{l}"]).then_inc(s.loaded, 16)
                    sp.dma_start(bias[l], d.all[f"lbias{l}"]).then_inc(s.loaded, 16)
                sp.dma_start(w.w3a[:, :], d.w3a).then_inc(s.loaded, 16)
                sp.dma_start(w.w3b[:, :], d.w3b).then_inc(s.loaded, 16)
                sp.dma_start(w.w3c[:, :, :], d.w3c).then_inc(s.loaded, 16)

            @block.gpsimd
            def _(pool):
                for t in zeroed[4:]:
                    pool.memset(flat(t), 0.0).then_inc(s.zeroed, 1)
                pool.memset(w.half[:, :], -0.5)

            @block.tensor
            def _(pe):
                pe.wait_ge(s.loaded, 16 * 9)
                for l in range(2):
                    for half in range(2):
                        pe.matmul(g.ps[:, 2 * l + half, 0:OUTS[l]], lin[l][:, half, :], conv[l][:, 0:OUTS[l]],
                                  start=True, stop=True)
                    ins = pe.matmul(g.ps[:, 4 + l, 0:1], conv[l], bias[l], start=True, stop=True)
                ins.then_inc(s.multiplied, 1)

            @block.vector
            def _(dve):
                link = chain(dve, s.step)
                for t in zeroed[0:4]:
                    dve.memset(flat(t), 0.0).then_inc(s.zeroed, 1)
                dve.wait_ge(s.multiplied, 1)
                dve.wait_ge(s.zeroed, len(zeroed))
                for l in range(2):
                    o = OUTS[l]
                    link(dve.tensor_copy(w.bias[:, l:l + 1], g.ps[:, 4 + l, 0:1]))
                    link(dve.tensor_copy(w.wnei[l][:, :], g.ps[:, 2 * l + 1, 0:o]))
                    for h in range(HEADS):
                        at = (h * o) % P
                        link(dve.tensor_copy(cf[l][:, h, at:at + o], g.ps[:, 2 * l, 0:o]))
                    whole, parts = flat(cf[l]), w.wcen[l]
                    for p in range(3):
                        link(dve.tensor_copy(flat(parts[:, p]), whole))
                        if p < 2:
                            link(dve.tensor_tensor(whole, whole, flat(parts[:, p]), ALU.subtract))
        release(nc, s)


def flat(t):
    ap = t if isinstance(t, bass.AP) else t[tuple([slice(None)] * len(t.shape))]
    names = "abcdef"[:len(ap.shape) - 1]
    return ap if len(names) == 1 else ap.rearrange(f"p {' '.join(names)} -> p ({' '.join(names)})")


def graph_layers(nc, g, d):
    with ExitStack() as st:
        w = named(tensors(nc, st, "a", (
            ("w3a", [P, 32], F32), ("w3b", [P, 32], F32), ("w3c", [P, 2, 32], F32), ("bias", [P, 2], F32),
            ("spread", [P, 3, NCH, METHODS, P], BF16),
            ("x16", [P, 2, U_MAX, 4, HD], F16),
            ("xT", [P, 3, U_MAX, P], F16),
            ("sorted", [P, 2, F_COLS], F32),
            ("first", [P, 2, HEAD_POINTS, KNN], F32),
            ("centre", [P, 2, NS, DIM + 8], F32), ("centre16", [P, 2, DIM + 8], F16),
            ("perm", [P, NS, METHODS, NCH, DIM + EXTRA], BF16),
            ("row_hi", [P, 2, METHODS, DIM], F32), ("row_lo", [P, 2, METHODS, DIM], F32),
            ("key_b", [P, 2, NCH, METHODS], F32), ("above", [P, 3, DIM], F32), ("less", [P, 3, DIM], BF16),
            ("rank", [P, NS, METHODS * NCH], F32),
            ("fn", [P, NS, NCH, C_IN], F32), ("rest", [P, NCH, C_IN], F32), ("parts", [P, 3, NCH, C_IN], BF16),
            ("e", [P, 2, SC], F32),
            ("pair", [P, 2, SC], F32), ("pairT", [P, 2, SC], F32),
            ("rmax", [P, 2, SC // HD], F32), ("rsum", [P, 2, SC // HD], F32),
            ("att", [P, 2, 4, U_MAX, HD], F32),
            ("low", [P, 2, 4, U_MAX // 2, HD], F32),
            ("cterm", [P, 2, 2, 132], F32),
            ("h", [P, 2, U_MAX * BLK], F32),
            ("stats", [P, 2, 2, NB, 6], F32), ("mv", [P, 2, 2], F32), ("mean", [P, 1], F32), ("meanb", [P, 1], F32),
            ("dev", [P, 2, 2], F32), ("var", [P, 1], F32), ("rstd", [P, 1], F32), ("half", [P, 1], F32),
            ("peak", [P, 2, 2, 3 * (U_ALL + 1)], F32), ("f", [P, 2, P], F32),
            ("o32", [32, 2, DIM], F32), ("st3", [32, 6], F32), ("mv3", [32, 2], F32), ("r3", [32, 1], F32))))
        w.wnei = [st.enter_context(nc.sbuf_tensor(f"a_wnei{l}", [P, OUTS[l]], F32)) for l in range(2)]
        w.wcen = [st.enter_context(nc.sbuf_tensor(f"a_wcen{l}", [P, 3, 4, P], BF16)) for l in range(2)]
        graph_weights(nc, g, d, w)
        s = semaphores(nc, st, "rank", "rows0 rows1 keyb step above ranked perm")
        with nc.Block() as block:
            @block.sync
            def _(sp):
                for x in range(NS):
                    load_rows(sp, d, w, s, x, x)

            @block.vector
            def _(dve):
                units = METHODS * NCH
                for x in range(NS):
                    key_columns(dve, g, w, s, x, x)
                    for i in range(units):
                        count_below(dve, w, s, i, x)
                        if i:
                            place(dve, g, w, s, x, i - 1, x)
                    place(dve, g, w, s, x, units - 1, x)

            @block.scalar
            def _(act):
                for x in range(NS):
                    keys_there(act, s, x)
                    for i in range(METHODS * NCH):
                        compare_high(act, w, s, i, x)
        release(nc, s)
        s = semaphores(nc, st, "graph", "gathered sorted x16 turned xT scored shifted exped normed hi lo attn part lows "
                       "summed b7w b7r moments dev var rstd f parts spread rows_of dstep pstep rows0 rows1 keyb above ranked perm out stored")
        graph_rows(nc, g, d, w, s, 0, first=True)
        with nc.Fori(0, LAT // (NS * PAIRS)) as it:
            graph_rows(nc, g, d, w, s, it)


def load_rows(sp, d, w, s, b, n):
    sem = (s.rows0, s.rows1)[n % 2]
    sp.dma_start(w.row_hi[:, n % 2], bcast_rows(d.keys_hi, b)).then_inc(sem, 16)
    sp.dma_start(w.row_lo[:, n % 2], bcast_rows(d.keys_lo, b)).then_inc(sem, 16)


def key_columns(dve, g, w, s, b, n):
    columns = bass.ds(b * METHODS, METHODS)
    dve.tensor_scalar(w.key_b[:, 0, :, :], g.key_hi[:, :, columns], -1.0, None, ALU.mult).then_inc(s.keyb, 1)
    dve.tensor_copy(w.key_b[:, 1, :, :], g.key_lo[:, :, columns]).then_inc(s.keyb, 1)
    keys_there(dve, s, n)


def keys_there(eng, s, n):
    eng.wait_ge(s.keyb, 2 * n + 2)
    eng.wait_ge((s.rows0, s.rows1)[n % 2], 32 * (n // 2 + 1))


def compare_high(act, w, s, i, n):
    m, c = i // NCH, i % NCH
    count = n * METHODS * NCH + i
    if count >= 3:
        act.wait_ge(s.ranked, count - 2)
    act.activation(w.above[:, count % 3, :], w.row_hi[:, n % 2, m, :], ACT.Identity,
                   bias=w.key_b[:, 0, c, m:m + 1]).then_inc(s.above, 1)


def count_below(dve, w, s, i, n):
    m, c = i // NCH, i % NCH
    count = n * METHODS * NCH + i
    dve.wait_ge(s.above, count + 1)
    dve.scalar_tensor_tensor(w.less[:, count % 3, :], w.above[:, count % 3, :], w.key_b[:, 1, c, m:m + 1],
                             w.row_lo[:, n % 2, m, :], ALU.subtract, ALU.is_lt,
                             accum_out=w.rank[:, n % NS, i:i + 1]).then_inc(s.ranked, 1)


def place(dve, g, w, s, x, i, n):
    m, c = i // NCH, i % NCH
    dve.wait_ge(s.ranked, n * METHODS * NCH + i + 1)
    dve.tensor_scalar(w.perm[:, x, m, c, :], g.targets[:, :], w.rank[:, n % NS, i:i + 1], None,
                      ALU.is_equal).then_inc(s.perm, 1)


def graph_rows(nc, g, d, w, s, it, first=False):
    runs = 2 * NS * PAIRS
    NQ = runs * NB
    steps = NQ + 5
    quarter = U_MAX // 2
    halves = [(q, h) for q in range(NQ) for h in range(2) if BATCH_U[q % NB] > quarter * h]
    upto = [sum(x[0] < q for x in halves) for q in range(NQ + 1)]

    def layer(r):
        return r // NS % 2

    def group(r):
        return r // (2 * NS) * NS + r % NS

    def chunks(k):
        return range(2 * k, 2 * k + 2 if k < NB - 1 else METHODS * NCH)

    def variances(r):
        return r + 1 + sum(map(layer, range(r)))

    def made(r):
        return r + 1 if first else r

    def at_step(step):
        r, k = divmod(step, NB)
        return r, k, r - 1 if 1 <= r <= runs else None, k == NB - 1 and r < runs

    def cols(q, h):
        nu = BATCH_U[q % NB]
        return range(quarter * h, min(quarter * (h + 1), nu))

    with nc.Block() as block:
        @block.sync
        def _(sp):
            def store_rows(sp, j):
                sp.wait_ge(s.out, j + 1)
                sp.dma_start(d.xatt[bass.ds(it * (NS * PAIRS * TOK) + j * TOK, TOK), :],
                             w.o32[:, 1, :]).then_inc(s.stored, 16)
                sp.wait_ge(s.stored, 16 * (j + 1))

            for j in () if first else range(NS * PAIRS):
                if j >= 2:
                    sp.wait_ge(s.ranked, METHODS * NCH * (j - 1))
                load_rows(sp, d, w, s, (it * (NS * PAIRS) + NS + j) & (LAT - 1), j)
                if j >= NS:
                    store_rows(sp, j - NS)
            for j in () if first else range(NS * (PAIRS - 1), NS * PAIRS):
                store_rows(sp, j)

        @block.gpsimd
        def _(pool):
            link = chain(pool, s.pstep)

            def differences(q):
                r, k = divmod(q, NB)
                l, x = layer(r), r % NS
                nu, at = BATCH_U[k], 3 * U_MAX * k
                if k == 0:
                    if made(r):
                        pool.wait_ge(s.sorted, made(r))
                if q >= 2:
                    pool.wait_ge(s.scored, q - 1)
                for c in range(4):
                    ins = pool.tensor_tensor(
                        custom(w.x16[:, q % 2], HD * c, [[4 * HD, nu], [KNN, 3], [1, KNN]]),
                        custom(w.sorted[:, r % 2], P * c + at, [[3, nu], [1, 3], [1, KNN]]),
                        custom(w.centre[:, l, x], P * c + at, [[3, nu], [1, 3], [0, KNN]]), ALU.subtract)
                if k == 0:
                    link(ins)
                    for u, n in ((0, 3), (1, HEAD_POINTS - 3)):
                        ins = pool.tensor_tensor(
                            custom(w.x16[:, q % 2], 4 * HD * u, [[KNN, n], [1, KNN]]),
                            w.first[:, r % 2, 3 * u:3 * u + n, :],
                            custom(w.centre[:, l, x], 3 * u, [[1, n], [0, KNN]]), ALU.subtract)
                ins.then_inc(s.x16, 1)

            if first:
                return
            differences(0)
            for step in range(steps):
                r, k, done, last = at_step(step)
                ahead = step + 1 < NQ
                if ahead and k < NB - 1:
                    differences(step + 1)
                if k == 3 and done is not None:
                    pool.wait_ge(s.var, variances(done))
                    pool.tensor_tensor(w.rstd[:, :], w.var[:, :], w.half[:, :], ALU.pow).then_inc(s.rstd, 1)
                if k == 4 and done is not None and layer(done):
                    pool.wait_ge(s.var, variances(done) + 1)
                    pool.tensor_tensor(w.r3[:, :], w.mv3[:, 1:2], w.half[0:32, :], ALU.pow).then_inc(s.rstd, 1)
                if step < NQ:
                    pool.wait_ge(s.hi, step + 1)
                    pair = w.pair[:, step % 2].bitcast(F16).rearrange("p (n a) -> p n a", a=2)
                    pool.tensor_tensor(pair[:, :, 1], w.e[:, step % 2, :], pair[:, :, 0],
                                       ALU.subtract).then_inc(s.lo, 1)
                if ahead and k == NB - 1:
                    differences(step + 1)

        @block.scalar
        def _(act):
            def keep_gathered(r):
                l, x = layer(r), r % NS
                act.wait_ge(s.gathered, made(r))
                act.copy(w.sorted[:, r % 2, F_LEFT:F_LEFT + DIM], g.ps[:, 0, :])
                act.copy(w.sorted[:, r % 2, F_LEFT + DIM:F_LEFT + DIM + TAIL], g.ps[:, 6, 0:TAIL])
                act.copy(flat(w.first[:, r % 2]), g.ps[:, 6, TAIL:EXTRA])
                act.copy(w.centre16[:, r % 2, 0:DIM], g.ps[:, 1, :])
                act.copy(w.centre[:, l, x, 0:DIM], g.ps[:, 1, :]).then_inc(s.sorted, 1)

            def keep_low(q, h):
                if not 0 <= q < NQ or (q, h) not in halves:
                    return
                i, n = halves.index((q, h)), len(cols(q, h))
                act.wait_ge(s.part, i + 1)
                if i >= 2:
                    act.wait_ge(s.summed, i - 1)
                act.copy(w.low[:, i % 2, :, 0:n, :],
                         custom(g.ps[:, 4, :], HD, [[quarter * 2 * HD, 4], [2 * HD, n], [1, HD]])).then_inc(s.lows, 1)

            def spread(r):
                act.wait_ge(s.parts, made(r))
                for p in range(3):
                    for m in range(METHODS):
                        dst = custom(w.spread[:, p], m * P + m * 8, [[METHODS * P, NCH], [32, HEADS], [1, 8]])
                        src = custom(w.parts[:, p], 0, [[C_IN, NCH], [8, HEADS], [1, 8]])
                        ins = act.copy(dst, src)
                ins.then_inc(s.spread, 1)

            if first:
                spread(0)
                keep_gathered(0)
                return
            for step in range(steps):
                r, k, done, last = at_step(step)
                keep_low(step - 2, 0)
                if step < NQ:
                    n = BATCH_U[k] * P
                    act.wait_ge(s.turned, step + 1)
                    if step >= 3:
                        act.wait_ge(s.part, upto[step - 2])
                    act.copy(flat(w.xT[:, step % 3])[:, 0:n], g.ps[:, 6, :].bitcast(F16)[:, 0:n]).then_inc(s.xT, 1)
                if not last:
                    keep_low(step - 2, 1)
                if step < NQ:
                    act.wait_ge(s.shifted, step + 1)
                    act.activation(w.e[:, step % 2, :], w.e[:, step % 2, :], ACT.Exp,
                                   scale=INV_SQRT_HD).then_inc(s.exped, 1)
                    if not layer(r):
                        if k == 0:
                            keys_there(act, s, group(r))
                        for i in chunks(k):
                            compare_high(act, w, s, i, group(r))
                    act.wait_ge(s.normed, step + 1)
                    pair = w.pair[:, step % 2].bitcast(F16).rearrange("p (n a) -> p n a", a=2)
                    act.copy(pair[:, :, 0], w.e[:, step % 2, :]).then_inc(s.hi, 1)
                if k == 4 and r < runs:
                    spread(r + 1)
                if last:
                    keep_gathered(r + 1)
                    keep_low(step - 2, 1)

        @block.tensor
        def _(pe):
            writes = [0]

            def bank7():
                if writes[0]:
                    pe.wait_ge(s.b7r, writes[0])
                writes[0] += 1

            fences = [0]

            def fenced(ins):
                fences[0] += 1
                ins.then_inc(s.rows_of, 1)

            def fence(i):
                pe.wait_ge(s.rows_of, fences[0] - 1 + i)

            def gather(r):
                l, x = layer(r), r % NS
                pe.wait_ge(s.spread, made(r))
                if group(r) >= NS:
                    pe.wait_ge(s.perm, METHODS * NCH * (group(r) - NS + 1))
                if r:
                    pe.wait_ge(s.shifted, r * NB - 1)
                    pe.wait_ge(s.xT, r * NB)
                order = [(p, m, c) for p in range(3) for m in range(METHODS) for c in range(NCH)]
                for i, (p, m, c) in enumerate(order):
                    for bank, a, n in ((0, 0, DIM), (6, DIM, EXTRA)):
                        pe.matmul(g.ps[:, bank, 0:n], w.spread[:, p, c, m, :], w.perm[:, x, m, c, a:a + n],
                                  start=(i == 0), stop=(i == len(order) - 1))
                order = [(p, m) for p in range(3) for m in range(METHODS)]
                for c in range(NCH):
                    for i, (p, m) in enumerate(order):
                        ins = pe.matmul(g.ps[:, 1, c * P:(c + 1) * P], w.spread[:, p, c, m, :], g.identb[:, :],
                                        start=(i == 0), stop=(i == len(order) - 1))
                ins.then_inc(s.gathered, 1)

            def centre_term(r):
                l = layer(r)
                if made(r):
                    pe.wait_ge(s.sorted, made(r))
                bank7()
                for half in range(l + 1):
                    quads = range(4) if l == 0 else (2 * half, 2 * half + 1)
                    order = [(p, c) for p in range(3) for c in quads]
                    for i, (p, c) in enumerate(order):
                        ins = pe.matmul(g.ps[:, 7, 256 * half:256 * half + P + 1], w.wcen[l][:, p, c, :],
                                        w.centre16[:, r % 2, P * c:P * c + P + 1], start=(i == 0),
                                        stop=(i == len(order) - 1))
                ins.then_inc(s.b7w, 1)

            def turn(q):
                k = q % NB
                pe.wait_ge(s.x16, q + 1)
                if q:
                    pe.wait_ge(s.xT, q)
                if k == 0 and made(q // NB):
                    pe.wait_ge(s.sorted, made(q // NB))
                for u in range(BATCH_U[k]):
                    ins = pe.transpose(g.ps[:, 6, :].bitcast(F16)[:, P * u:P * (u + 1)], flat(w.x16[:, q % 2, u]),
                                       g.ident16[:, :])
                ins.then_inc(s.turned, 1)

            def scores(q):
                if q >= 2:
                    pe.wait_ge(s.shifted, q - 1)
                base = 2 * (q % 2)
                for i in range(2):
                    pe.matmul(g.ps[:, base + i, :], g.identb[:, :], flat(g.mask), start=True, stop=False,
                              skip_group_check=True)
                nu = BATCH_U[q % NB]
                for h in range(HEADS):
                    if h >= 2:
                        fence(h - 2)
                    for u in range(nu):
                        at = (h // 2 * U_MAX + u) * HD
                        for c in range(4):
                            v = w.x16[HD * h:HD * (h + 1), q % 2, u, c, :]
                            ins = pe.matmul(g.ps[HD * c:HD * (c + 1), base + h % 2, at:at + HD], v, v,
                                            start=False, stop=(u == nu - 1), skip_group_check=True)
                    if h < 2:
                        fenced(ins)
                ins.then_inc(s.scored, 1)

            def attention(q, h):
                if not 0 <= q < NQ or (q, h) not in halves:
                    return
                i = halves.index((q, h))
                pe.wait_ge(s.attn, q + 1)
                pe.wait_ge(s.xT, q + 1)
                if i:
                    pe.wait_ge(s.summed, i)
                weights = w.pairT[:, q % 2].bitcast(F16)
                for c in range(4):
                    rows = slice(HD * c, HD * (c + 1))
                    if c >= 2:
                        fence(c - 2)
                    for u in cols(q, h):
                        for a in range(HEADS):
                            group = ((a % 2) * 2 + a // 2) * U_MAX + u
                            at = ((c // 2) * quarter + u % quarter) * 2 * HD
                            ins = pe.matmul(g.ps[HD * a:HD * (a + 1), 4 + c % 2, at:at + 2 * HD],
                                            w.xT[rows, q % 3, u, HD * a:HD * (a + 1)],
                                            custom(weights[rows], 2 * HD * group, [[1, 2], [2, HD]]),
                                            start=True, stop=True, skip_group_check=True)
                    if c < 2:
                        fenced(ins)
                ins.then_inc(s.part, 1)

            def outputs(q):
                if not 0 <= q < NQ:
                    return
                l, nu = layer(q // NB), BATCH_U[q % NB]
                pe.wait_ge(s.summed, upto[q + 1])
                bank7()
                for c in range(4):
                    o = OUTS[l]
                    row = c * o % P
                    at = c * o // P * 256
                    ins = pe.matmul(g.ps[row:row + o, 7, at:at + nu * HD], w.wnei[l][:, :],
                                    flat(w.att[:, q % 2, c % 2 * 2 + c // 2, 0:nu, :]), start=True, stop=True, skip_group_check=True)
                ins.then_inc(s.b7w, 1)

            def average(l, src):
                bank7()
                avg = g.avg2 if l else g.avg1
                for half in range(l + 1):
                    ins = pe.matmul(g.ps[:, 7, 0:1], avg[:, :], src(half), start=(half == 0), stop=(half == l))
                ins.then_inc(s.b7w, 1)

            def turn_features(r):
                pe.wait_ge(s.f, r + 1)
                bank7()
                pe.transpose(g.ps[:, 7, 0:P], w.f[:, 0, :], g.ident[:, :]).then_inc(s.b7w, 1)

            def convolve(r):
                x = r % NS
                pe.wait_ge(s.f, r + 1)
                bank7()
                out = g.ps[0:32, 7, :]
                pe.matmul(out, w.w3a[:, :], w.centre[:, 0, x, 0:DIM], start=True, stop=False, skip_group_check=True)
                pe.matmul(out, w.w3b[:, :], w.centre[:, 1, x, 0:DIM], start=False, stop=False, skip_group_check=True)
                for half in range(2):
                    for c in range(2):
                        at = P * (2 * half + c)
                        ins = pe.matmul(out[:, at:at + P], w.w3c[:, c, :], w.f[:, half, :], start=False,
                                        stop=(half == 1 and c == 1), skip_group_check=True)
                ins.then_inc(s.b7w, 1)

            if first:
                gather(0)
                return
            for step in range(steps):
                r, k, done, last = at_step(step)
                attention(step - 2, 0)
                if step < NQ:
                    turn(step)
                    scores(step)
                if k == 3 and done is not None:
                    pe.wait_ge(s.moments, done + 1)
                    average(layer(done), lambda half: w.mv[:, half, 0:1])
                if k == 4 and done is not None:
                    if not layer(done):
                        turn_features(done)
                    else:
                        convolve(done)
                if k == 0 and r < runs:
                    centre_term(r)
                if last:
                    outputs(step - 3)
                    gather(r + 1)
                attention(step - 2, 1)
                if k == 3 and done is not None:
                    pe.wait_ge(s.dev, done + 1)
                    average(layer(done), lambda half: w.dev[:, half, 1:2])
                if not last:
                    outputs(step - 3)

        @block.vector
        def _(dve):
            link = chain(dve, s.dstep)
            reads = [0]

            def bank7():
                reads[0] += 1
                dve.wait_ge(s.b7w, reads[0])

            def features(r):
                at = ((it * (NS * PAIRS) + group(r)) & (LAT - 1)) * C_IN
                link(dve.tensor_copy(w.fn[:, r % NS, :, :], g.xnT[:, :, bass.ds(at, C_IN)]))

            def split(r):
                if made(r) > 1:
                    dve.wait_ge(s.spread, made(r) - 1)
                src = w.fn[:, r % NS]
                for p in range(3):
                    ins = dve.tensor_copy(flat(w.parts[:, p]), flat(src))
                    if p == 2:
                        ins.then_inc(s.parts, 1)
                        return
                    link(ins)
                    link(dve.tensor_tensor(flat(w.rest), flat(src), flat(w.parts[:, p]), ALU.subtract))
                    src = w.rest

            def add_parts(q, h):
                if not 0 <= q < NQ or (q, h) not in halves:
                    return
                i, us = halves.index((q, h)), cols(q, h)
                dve.wait_ge(s.lows, i + 1)
                dve.tensor_tensor(
                    custom(w.att[:, q % 2], us[0] * HD, [[U_MAX * HD, 4], [HD, len(us)], [1, HD]]),
                    custom(g.ps[:, 4, :], 0, [[quarter * 2 * HD, 4], [2 * HD, len(us)], [1, HD]]),
                    w.low[:, i % 2, :, 0:len(us), :], ALU.add).then_inc(s.summed, 1)

            def shift(q):
                dve.wait_ge(s.scored, q + 1)
                sc = g.ps[:, 2 * (q % 2):2 * (q % 2) + 2, :].rearrange("p a (u j) -> p (a u) j", j=HD)
                e = w.e[:, q % 2, :].rearrange("p (u j) -> p u j", j=HD)
                n = SC // HD
                link(dve.tensor_reduce(w.rmax[:, q % 2, :], sc, AX.X, ALU.max))
                dve.tensor_tensor(e, sc, w.rmax[:, q % 2, :, None].broadcast_to([P, n, HD]),
                                  ALU.subtract).then_inc(s.shifted, 1)

            def normalise(q):
                e = w.e[:, q % 2, :].rearrange("p (u j) -> p u j", j=HD)
                n = SC // HD
                dve.wait_ge(s.exped, q + 1)
                link(dve.tensor_reduce(w.rsum[:, q % 2, :], e, AX.X, ALU.add))
                link(dve.reciprocal(w.rsum[:, q % 2, :], w.rsum[:, q % 2, :]))
                dve.tensor_tensor(e, e, w.rsum[:, q % 2, :, None].broadcast_to([P, n, HD]),
                                  ALU.mult).then_inc(s.normed, 1)

            def turn_weights(q):
                if not 0 <= q < NQ:
                    return
                dve.wait_ge(s.lo, q + 1)
                dve.transpose(w.pairT[:, q % 2, :], w.pair[:, q % 2, :]).then_inc(s.attn, 1)

            def keep_outputs(q):
                if not 0 <= q < NQ:
                    return
                r, k = divmod(q, NB)
                l, nu = layer(r), BATCH_U[k]
                bank7()
                for half in range(l + 1):
                    ins = dve.tensor_tensor(
                        custom(w.h[:, half], 0, [[BLK, nu], [KNN, 3], [1, KNN]]),
                        custom(g.ps[:, 7, :], 256 * half, [[HD, nu], [KNN, 3], [1, KNN]]),
                        custom(w.cterm[:, r % 2, half], 3 * U_MAX * k, [[3, nu], [1, 3], [0, KNN]]), ALU.add)
                    if half < l:
                        link(ins)
                ins.then_inc(s.b7r, 1)
                dve.wait_ge(s.b7r, reads[0])
                n = nu * BLK if k < NB - 1 else (P * KNN - U_MAX * BLK * k)
                for half in range(l + 1):
                    link(dve.bn_stats(w.stats[:, r % 2, half, k, :], w.h[:, half, 0:n]))
                    link(dve.tensor_reduce(w.peak[:, r % 2, half, 3 * U_MAX * k:3 * (U_MAX * k + nu)],
                                           w.h[:, half, 0:nu * BLK].rearrange("p (n j) -> p n j", j=KNN), AX.X, ALU.max))

            def moments(r):
                l = layer(r)
                for half in range(l + 1):
                    ins = dve.bn_aggr(w.mv[:, half, :], flat(w.stats[:, r % 2, half]))
                    if half < l:
                        link(ins)
                ins.then_inc(s.moments, 1)
                dve.wait_ge(s.moments, r + 1)

            def deviations(r):
                l = layer(r)
                bank7()
                dve.tensor_copy(w.mean[:, :], g.ps[:, 7, 0:1]).then_inc(s.b7r, 1)
                dve.wait_ge(s.b7r, reads[0])
                link(dve.tensor_scalar(w.dev[:, 0:l + 1, 0], w.mv[:, 0:l + 1, 0], w.mean[:, 0:1], None, ALU.subtract))
                link(dve.tensor_tensor(w.dev[:, 0:l + 1, 0], w.dev[:, 0:l + 1, 0], w.dev[:, 0:l + 1, 0], ALU.mult))
                dve.tensor_tensor(w.dev[:, 0:l + 1, 1], w.dev[:, 0:l + 1, 0], w.mv[:, 0:l + 1, 1],
                                  ALU.add).then_inc(s.dev, 1)

            def variance(r):
                bank7()
                dve.tensor_scalar(w.var[:, :], g.ps[:, 7, 0:1], LN_EPS, None, ALU.add).then_inc(s.b7r, 1)
                dve.wait_ge(s.b7r, reads[0])
                dve.sem_inc(s.var)

            def normalise_features(r):
                l = layer(r)
                f = w.f[:, 0:l + 1, :]
                link(dve.tensor_scalar(w.meanb[:, :], w.mean[:, :], w.bias[:, l:l + 1], None, ALU.add))
                link(dve.tensor_scalar(f, w.peak[:, r % 2, 0:l + 1, 0:P], w.bias[:, l:l + 1], w.meanb[:, 0:1],
                                       ALU.add, ALU.subtract))
                dve.wait_ge(s.rstd, variances(r))
                link(dve.tensor_scalar(f, f, w.rstd[:, 0:1], None, ALU.mult))
                dve.scalar_tensor_tensor(flat(f), flat(f), 0.2, flat(f), ALU.mult, ALU.max).then_inc(s.f, 1)

            def keep_rows():
                bank7()
                link(dve.bn_stats(w.st3[:, :], g.ps[0:32, 7, :]))
                link(dve.bn_aggr(w.mv3[:, :], w.st3[:, :]))
                dve.tensor_scalar(w.mv3[:, 1:2], w.mv3[:, 1:2], LN_EPS, None, ALU.add).then_inc(s.var, 1)
                dve.tensor_scalar(w.o32[:, 0, :], g.ps[0:32, 7, :], w.mv3[:, 0:1], None,
                                  ALU.subtract).then_inc(s.b7r, 1)
                dve.wait_ge(s.b7r, reads[0])

            def finish_rows(r):
                j = group(r)
                dve.wait_ge(s.rstd, variances(r) + 1)
                link(dve.tensor_scalar(w.o32[:, 0, :], w.o32[:, 0, :], w.r3[:, 0:1], None, ALU.mult))
                if j:
                    dve.wait_ge(s.stored, 16 * j)
                dve.scalar_tensor_tensor(w.o32[:, 1, :], w.o32[:, 0, :], 0.2, w.o32[:, 0, :], ALU.mult,
                                         ALU.max).then_inc(s.out, 1)

            if first:
                features(0)
                split(0)
                return
            for step in range(steps):
                r, k, done, last = at_step(step)
                add_parts(step - 2, 0)
                if step < NQ:
                    shift(step)
                if k == 3 and done is not None:
                    deviations(done)
                if k == 4 and done is not None:
                    if not layer(done):
                        bank7()
                        dve.tensor_copy(flat(w.fn[:, done % NS]), g.ps[:, 7, 0:P]).then_inc(s.b7r, 1)
                        dve.wait_ge(s.b7r, reads[0])
                    else:
                        keep_rows()
                if k == 0 and r < runs:
                    if not layer(r):
                        b = it * (NS * PAIRS) + NS + group(r)
                        key_columns(dve, g, w, s, b & (LAT - 1), group(r))
                    bank7()
                    l = layer(r)
                    dve.tensor_copy(w.cterm[:, r % 2, 0:l + 1, 0:P + 1],
                                    g.ps[:, 7, :].rearrange("p (a n) -> p a n", a=2)[:, 0:l + 1, 0:P + 1])\
                       .then_inc(s.b7r, 1)
                if k == 4 and r < runs:
                    if not layer(r + 1):
                        features(r + 1)
                    split(r + 1)
                turn_weights(step - 1)
                if not last:
                    add_parts(step - 2, 1)
                if k == 3 and done is not None:
                    variance(done)
                if step < NQ:
                    normalise(step)
                keep_outputs(step - 3)
                if k == 2 and done is not None:
                    moments(done)
                if k == 3 and done is not None:
                    normalise_features(done)
                if k == 4 and done is not None and layer(done):
                    finish_rows(done)
                if r < runs:
                    for i in chunks(k):
                        if layer(r):
                            place(dve, g, w, s, r % NS, i, group(r))
                        else:
                            count_below(dve, w, s, i, group(r))
                if last:
                    add_parts(step - 2, 1)
    release(nc, s)


def bcast_rows(keys, b):
    return keys[bass.ds(b, 1), :, :].rearrange("a m n -> (a m) n").partition_broadcast(P)


def add_point_attention(nc, g, d):
    with ExitStack() as st:
        s = semaphores(nc, st, "addp", "loaded added")
        y = st.enter_context(nc.sbuf_tensor("addp_y", [P, NT, DIM], F32))
        with nc.Block() as block:
            @block.sync
            def _(sp):
                for t in range(NT):
                    sp.dma_start(y[:, t, :], d.xatt[t * P:(t + 1) * P, :]).then_inc(s.loaded, 16)

            @block.vector
            def _(dve):
                dve.wait_ge(s.loaded, 16 * NT)
                dve.tensor_tensor(flat(g.x), flat(g.x), flat(y), ALU.add).then_inc(s.added, 1)
        release(nc, s)


def bound_attention(nc, g, d):
    with ExitStack() as st:
        def sb(name, shape, dt=F32):
            return st.enter_context(nc.sbuf_tensor("ba_" + name, shape, dt))
        s = semaphores(nc, st, "ba", "loaded step signs bound turned query values scored gate masked mixed added")
        vec = sb("vec", [NCH, 3, P])
        sgn = sb("sgn", [NCH, 3, P])
        zero = sb("zero", [NCH, 3, P])
        alpha = sb("alpha", [NCH, 3])
        sel = sb("sel", [NCH, NCH, P])
        causal = sb("causal", [P, P])
        qk = sb("qk", [P, NCH])
        qc = sb("qc", [P, NCH])
        query = sb("query", [P, NCH, ROWS])
        value = sb("value", [P, NT, DIM])
        gate = sb("gate", [P, NT, NCH, P])
        with nc.Block() as block:
            @block.sync
            def _(sp):
                sp.dma_start(vec[:, :, :], d.bind).then_inc(s.loaded, 16)
                sp.dma_start(sel[:, :, :], d.sel4).then_inc(s.loaded, 16)
                sp.dma_start(causal[:, :], d.causal).then_inc(s.loaded, 16)

            @block.scalar
            def _(act):
                act.wait_ge(s.loaded, 48)
                act.sign(sgn[:, :, :], vec[:, :, :]).then_inc(s.signs, 1)
                for t in range(NT):
                    act.wait_ge(s.scored, t + 1)
                    act.activation(flat(gate[:, t]), g.ps[:, 2 + t, :], ACT.Sigmoid,
                                   scale=4.0 * float(P) ** -0.5).then_inc(s.gate, 1)

            @block.tensor
            def _(pe):
                pe.wait_ge(s.bound, 1)
                pe.transpose(g.ps[:, 0, 0:NCH], vec[:, 0, :], g.ident[0:NCH, 0:NCH])
                pe.transpose(g.ps[:, 0, NCH:2 * NCH], vec[:, 1, :], g.ident[0:NCH, 0:NCH])
                for h in range(NCH):
                    ins = pe.matmul(g.ps[:, 1, h * P:(h + 1) * P], sel[:, h, :], vec[:, 2, :], start=True, stop=True)
                ins.then_inc(s.turned, 1)
                for t in range(NT):
                    pe.wait_ge(s.query, NCH)
                    for h in range(NCH):
                        ins = pe.matmul(g.ps[:, 2 + t, h * P:(h + 1) * P], g.xnT[:, h, t * P:(t + 1) * P],
                                        query[:, h, t * P:(t + 1) * P], start=True, stop=True)
                    ins.then_inc(s.scored, 1)
                for t in range(NT):
                    pe.wait_ge(s.masked, t + 1)
                    pe.wait_ge(s.values, NT)
                    if t >= 2:
                        pe.wait_ge(s.added, t - 1)
                    for h in range(NCH):
                        ins = pe.matmul(g.ps[:, 6 + t % 2, h * P:(h + 1) * P], gate[:, t, h, :],
                                        value[:, t, h * P:(h + 1) * P], start=True, stop=True)
                    ins.then_inc(s.mixed, 1)

            @block.vector
            def _(dve):
                link = chain(dve, s.step)
                dve.wait_ge(s.loaded, 48)
                link(dve.tensor_reduce(alpha[:, :], vec[:, :, :], AX.X, ALU.add, apply_absolute_value=True))
                link(dve.tensor_scalar(alpha[:, :], alpha[:, :], 1.0 / P, None, ALU.mult))
                dve.wait_ge(s.signs, 1)
                mean = alpha[:, :, None].broadcast_to([NCH, 3, P])
                link(dve.tensor_tensor(sgn[:, :, :], sgn[:, :, :], mean, ALU.mult))
                link(dve.tensor_scalar(zero[:, :, :], sgn[:, :, :], 0.0, None, ALU.is_equal))
                link(dve.tensor_tensor(zero[:, :, :], zero[:, :, :], mean, ALU.mult))
                link(dve.tensor_tensor(sgn[:, :, :], sgn[:, :, :], zero[:, :, :], ALU.add))
                link(dve.tensor_tensor(sgn[:, :, :], sgn[:, :, :], vec[:, :, :], ALU.subtract))
                dve.tensor_tensor(vec[:, :, :], sgn[:, :, :], vec[:, :, :], ALU.add).then_inc(s.bound, 1)
                dve.wait_ge(s.turned, 1)
                link(dve.tensor_copy(qc[:, :], g.ps[:, 0, 0:NCH]))
                link(dve.tensor_tensor(qk[:, :], qc[:, :], g.ps[:, 0, NCH:2 * NCH], ALU.mult))
                for h in range(NCH):
                    dve.tensor_scalar(query[:, h, :], g.xnT[:, h, :], qk[:, h:h + 1], None,
                                      ALU.mult).then_inc(s.query, 1)
                for t in range(NT):
                    dve.tensor_tensor(value[:, t, :], g.xn[:, t, :], g.ps[:, 1, :], ALU.mult).then_inc(s.values, 1)
                for t in range(NT):
                    dve.wait_ge(s.gate, t + 1)
                    dve.tensor_tensor(gate[:, t], gate[:, t], causal[:, None, :].broadcast_to([P, NCH, P]),
                                      ALU.mult).then_inc(s.masked, 1)
                for t in range(NT):
                    dve.wait_ge(s.mixed, t + 1)
                    dve.tensor_tensor(g.x[:, t, :], g.x[:, t, :], g.ps[:, 6 + t % 2, :], ALU.add).then_inc(s.added, 1)
        release(nc, s)


EXPERTS, RANK = 8, 16


def experts(nc, g, d, name, hidden, scale, capacity):
    G = hidden or EXPERTS
    n_rows = 4 if hidden else 1
    with ExitStack() as st:
        def sb(nm, shape, dt=F32):
            return st.enter_context(nc.sbuf_tensor(f"{name}_{nm}", shape, dt))
        s = semaphores(nc, st, name, "loaded step projected hmom hroot hidden hturned hback gates top expo chosen counted "
                 "weighted turned low out added")
        wa = sb("wa", [P, NCH, G + P])
        wb = sb("wb", [P, NCH, DIM])
        lb = sb("lb", [P, DIM])
        brow = sb("brow", [1, DIM])
        ones = sb("ones", [P, P])
        iota = sb("iota", [P, EXPERTS])
        low = sb("low", [P, NT, P])
        lowT = sb("lowT", [P, NT, P])
        lg = sb("lg", [P, NT, EXPERTS])
        top = sb("top", [P, NT, 8])
        idx = sb("idx", [P, NT, 8], U32)
        idf = sb("idf", [P, NT, 8])
        hot = sb("hot", [P, NT, 2, EXPERTS])
        dlt = sb("dlt", [P, NT])
        ex = sb("ex", [P, NT])
        w01 = sb("w01", [P, NT, 2])
        ok = sb("ok", [P, 2, EXPERTS])
        w2 = sb("w2", [P, NT, 2, EXPERTS])
        wfull = sb("wfull", [P, NT, EXPERTS])
        if hidden:
            rowv = sb("rowv", [P, 3, hidden])
            gb2 = sb("gb2", [P, EXPERTS])
            gw2 = sb("gw2", [hidden, EXPERTS])
            hh = sb("hh", [P, NT, hidden])
            hst = sb("hst", [P, NT, 6])
            hmv = sb("hmv", [P, NT, 2])
            hr = sb("hr", [P, NT])
            hT = sb("hT", [hidden, NT, P])
        with nc.Block() as block:
            @block.sync
            def _(sp):
                sp.dma_start(wa[:, :, :], d.all[name + "_wa"]).then_inc(s.loaded, 16)
                sp.dma_start(iota[:, :], d.iota8.partition_broadcast(P)).then_inc(s.loaded, 16)
                sp.dma_start(brow[:, :], d.all[name + "_bias"]).then_inc(s.loaded, 16)
                sp.dma_start(wb[:, :, :], d.all[name + "_wb"]).then_inc(s.loaded, 16)
                sp.dma_start(lb[:, :], d.all[name + "_lb"]).then_inc(s.loaded, 16)
                if hidden:
                    sp.dma_start(rowv[:, :, :], d.all[name + "_rows"].partition_broadcast(P)).then_inc(s.loaded, 16)
                    sp.dma_start(gb2[:, :], d.all[name + "_gb2"].partition_broadcast(P)).then_inc(s.loaded, 16)
                    sp.dma_start(gw2[:, :], d.all[name + "_gw2"]).then_inc(s.loaded, 16)

            loads = 16 * (8 if hidden else 5)

            @block.tensor
            def _(pe):
                pe.wait_ge(s.loaded, loads)
                for t in range(NT):
                    for c in range(NCH):
                        ins = pe.matmul(g.ps[:, t, 0:G + P], g.xnT[:, c, t * P:(t + 1) * P], wa[:, c, :],
                                        start=(c == 0), stop=(c == NCH - 1))
                    ins.then_inc(s.projected, 1)
                if hidden:
                    pe.wait_ge(s.hidden, 1)
                    for t in range(NT):
                        ins = pe.transpose(g.ps[0:hidden, 4, t * P:(t + 1) * P], hh[:, t, :], g.ident[:, :])
                    ins.then_inc(s.hturned, 1)
                    pe.wait_ge(s.hback, 1)
                    for t in range(NT):
                        ins = pe.matmul(g.ps[:, 5, t * EXPERTS:(t + 1) * EXPERTS], hT[:, t, :], gw2[:, :],
                                        start=True, stop=True)
                    ins.then_inc(s.gates, 1)
                if capacity:
                    pe.wait_ge(s.chosen, 1)
                    for t in range(NT):
                        ins = pe.matmul(g.ps[:, 6, 0:2 * EXPERTS], ones[:, :], flat(hot[:, t]),
                                        start=(t == 0), stop=(t == NT - 1))
                    ins.then_inc(s.counted, 1)
                for t in range(NT):
                    pe.wait_ge(s.weighted, t + 1)
                    pe.transpose(g.ps[:, 7, t * P:(t + 1) * P], low[:, t, :], g.ident[:, :]).then_inc(s.turned, 1)
                for t in range(NT):
                    for c in range(NCH):
                        pe.matmul(g.ps[:, t, :], g.xnT[:, c, t * P:(t + 1) * P], wb[:, c, :],
                                  start=(c == 0), stop=False)
                    pe.matmul(g.ps[:, t, :], ones[0:1, :], brow[:, :], start=False, stop=False)
                    pe.wait_ge(s.low, 1)
                    pe.matmul(g.ps[:, t, :], lowT[:, t, :], lb[:, :], start=False, stop=True).then_inc(s.out, 1)

            @block.scalar
            def _(act):
                if hidden:
                    act.wait_ge(s.hmom, 1)
                    act.activation(hr[:, :], hmv[:, :, 1], ACT.Sqrt, bias=g.eps[:, 0:1]).then_inc(s.hroot, 1)
                    act.wait_ge(s.hturned, 1)
                    act.copy(flat(hT), g.ps[0:hidden, 4, :]).then_inc(s.hback, 1)
                act.wait_ge(s.top, 1)
                act.activation(ex[:, :], dlt[:, :], ACT.Exp).then_inc(s.expo, 1)
                act.wait_ge(s.turned, NT)
                act.copy(flat(lowT), g.ps[:, 7, :]).then_inc(s.low, 1)

            @block.vector
            def _(dve):
                link = chain(dve, s.step)
                link(dve.memset(ones[:, :], 1.0))
                dve.wait_ge(s.loaded, loads)
                dve.wait_ge(s.projected, NT)
                if hidden:
                    link(dve.tensor_tensor(hh[:, :, :], g.ps[:, 0:NT, 0:G],
                                           rowv[:, 0:1, :].broadcast_to([P, NT, G]), ALU.add))
                    for t in range(NT):
                        link(dve.bn_stats(hst[:, t, :], hh[:, t, :]))
                    for t in range(NT):
                        ins = dve.bn_aggr(hmv[:, t, :], hst[:, t, :])
                        if t < NT - 1:
                            link(ins)
                    ins.then_inc(s.hmom, 1)
                    dve.wait_ge(s.hmom, 1)
                    dve.wait_ge(s.hroot, 1)
                    link(dve.reciprocal(hr[:, :], hr[:, :]))
                    for t in range(NT):
                        link(dve.tensor_scalar(hh[:, t, :], hh[:, t, :], hmv[:, t, 0:1], hr[:, t:t + 1],
                                               ALU.subtract, ALU.mult))
                    link(dve.tensor_tensor(hh[:, :, :], hh[:, :, :], rowv[:, 1:2, :].broadcast_to([P, NT, G]), ALU.mult))
                    link(dve.tensor_tensor(hh[:, :, :], hh[:, :, :], rowv[:, 2:3, :].broadcast_to([P, NT, G]), ALU.add))
                    dve.tensor_scalar(hh[:, :, :], hh[:, :, :], 0.0, None, ALU.max).then_inc(s.hidden, 1)
                    dve.wait_ge(s.gates, 1)
                    link(dve.tensor_tensor(lg[:, :, :], g.ps[:, 5, 0:NT * EXPERTS].rearrange("p (t e) -> p t e", t=NT),
                                           gb2[:, None, :].broadcast_to([P, NT, EXPERTS]), ALU.add))
                else:
                    link(dve.tensor_copy(lg[:, :, :], g.ps[:, 0:NT, 0:G]))
                for t in range(NT):
                    link(dve.max(top[:, t, :], lg[:, t, :]))
                for t in range(NT):
                    link(dve.max_index(idx[:, t, :], top[:, t, :], lg[:, t, :]))
                dve.tensor_tensor(dlt[:, :], top[:, :, 1], top[:, :, 0], ALU.subtract).then_inc(s.top, 1)
                link(dve.tensor_copy(idf[:, :, :], idx[:, :, :]))
                ins = dve.tensor_tensor(hot[:, :, :, :], iota[:, None, None, :].broadcast_to([P, NT, 2, EXPERTS]),
                                        idf[:, :, 0:2, None].broadcast_to([P, NT, 2, EXPERTS]), ALU.is_equal)
                ins.then_inc(s.chosen, 1)
                dve.wait_ge(s.chosen, 1)
                dve.wait_ge(s.expo, 1)
                link(dve.tensor_scalar(w01[:, :, 0], ex[:, :], 1.0, None, ALU.add))
                link(dve.reciprocal(w01[:, :, 0], w01[:, :, 0]))
                link(dve.tensor_scalar(w01[:, :, 0], w01[:, :, 0], scale, None, ALU.mult))
                link(dve.tensor_tensor(w01[:, :, 1], w01[:, :, 0], ex[:, :], ALU.mult))
                if capacity:
                    dve.wait_ge(s.counted, 1)
                    link(dve.tensor_scalar(flat(ok), g.ps[:, 6, 0:2 * EXPERTS], float(capacity), None, ALU.is_le))
                    for t in range(NT):
                        link(dve.tensor_tensor(hot[:, t], hot[:, t], ok[:, :, :], ALU.mult))
                link(dve.tensor_tensor(w2[:, :, :, :], hot[:, :, :, :],
                                       w01[:, :, :, None].broadcast_to([P, NT, 2, EXPERTS]), ALU.mult))
                link(dve.tensor_tensor(wfull[:, :, :], w2[:, :, 0, :], w2[:, :, 1, :], ALU.add))
                for t in range(NT):
                    dve.tensor_tensor(low[:, t, :].rearrange("p (e r) -> p e r", e=EXPERTS),
                                      g.ps[:, t, G:G + P].rearrange("p (e r) -> p e r", e=EXPERTS),
                                      wfull[:, t, :, None].broadcast_to([P, EXPERTS, RANK]),
                                      ALU.mult).then_inc(s.weighted, 1)
                for t in range(NT):
                    dve.wait_ge(s.out, t + 1)
                    dve.tensor_tensor(g.x[:, t, :], g.x[:, t, :], g.ps[:, t, :], ALU.add).then_inc(s.added, 1)
        release(nc, s)


Q_HEADS, KV_HEADS, GROUP = 32, 8, 4
CTX = 512
KV = CTX + TOK
W_SCALE = 64.0
RMS_EPS = 1e-6
AT_B = 4
ATT_SCALE = float(P) ** -0.5


def cross_attention(nc, g, d):
    with ExitStack() as st:
        def sb(name, shape, dt=F32):
            return st.enter_context(nc.sbuf_tensor("ca_" + name, shape, dt))
        w = named({})
        w.qT = sb("qT", [P, Q_HEADS, ROWS])
        w.klat = sb("klat", [P, KV_HEADS, ROWS])
        w.wk = sb("wk", [P, NCH, KV_HEADS * P])
        w.wv = sb("wv", [P, NCH, KV_HEADS * P])
        w.mean = sb("mean", [P, P])
        w.nw = sb("nw", [P, 3])
        w.eps = sb("eps", [P, 1])
        with ExitStack() as s1:
            project_latents(nc, g, d, w, s1)
        with ExitStack() as s2:
            attend(nc, g, d, w, s2)
        with ExitStack() as s3:
            project_out(nc, g, d, w, s3)


def parts_of(t):
    return t.bitcast(F16).rearrange("p (a n) -> p a n", a=2)


def split_product(pe, out, lhs, rhs):
    last = len(lhs) - 1
    for c in range(len(lhs)):
        pe.matmul(out, lhs[c][0], rhs[c][0], start=(c == 0), stop=False)
        pe.matmul(out, lhs[c][0], rhs[c][1], start=False, stop=False)
        ins = pe.matmul(out, lhs[c][1], rhs[c][0], start=False, stop=(c == last))
    return ins


def project_latents(nc, g, d, w, st):
    def sb(name, shape, dt=F32):
        return st.enter_context(nc.sbuf_tensor("pl_" + name, shape, dt))
    s = semaphores(nc, st, "pl", "kw kvw q0 q1 consts step pstep split q sq ms root rstd done kv kvout vst0 vst1")
    wq = sb("wq", [P, 2, NCH, GROUP * P])
    sq = sb("sq", [P, 2, ROWS])
    root = sb("root", [P, 2, ROWS])
    vout = sb("vout", [P, 2, 512])
    scaled = sb("scaled", [P, KV_HEADS * P])
    x16 = sb("x16", [P, 2, NCH, ROWS], F16)
    s_q, s_v = (s.q0, s.q1), (s.vst0, s.vst1)
    n_kv = KV_HEADS + NT * 2
    with nc.Block() as block:
        @block.sync
        def _(sp):
            sp.dma_start(w.mean[:, :], d.mean128).then_inc(s.kw, 16)
            sp.dma_start(w.nw[:, 0:2], d.qk_norm).then_inc(s.kw, 16)
            for k in range(KV_HEADS):
                if k >= 2:
                    sp.wait_ge(s.q, GROUP * (k - 1))
                sp.dma_start(wq[:, k % 2, :, :], d.wq[:, :, k * GROUP * P:(k + 1) * GROUP * P]).then_inc(s_q[k % 2], 16)
                if k == 1:
                    sp.dma_start(w.wk[:, :, :], d.wk).then_inc(s.kvw, 16)
                    sp.dma_start(w.wv[:, :, :], d.wv).then_inc(s.kvw, 16)
            for i in range(NT * 2):
                sp.wait_ge(s.kvout, KV_HEADS + i + 1)
                t, half = i // 2, i % 2
                sp.dma_start(d.v_lat[t * P:(t + 1) * P, half * 512:(half + 1) * 512], vout[:, i % 2, :]).then_inc(s_v[i % 2], 16)
            for sem in s_v:
                sp.wait_ge(sem, 16 * NT)

        @block.gpsimd
        def _(pool):
            link = chain(pool, s.pstep)
            for c in range(NCH):
                link(pool.tensor_copy(x16[:, 0, c, :], g.xnT[:, c, :]))
                link(pool.tensor_tensor(x16[:, 1, c, :], g.xnT[:, c, :], x16[:, 0, c, :], ALU.subtract))
            pool.wait_ge(s.kvw, 32)
            for weights in (w.wk, w.wv):
                for c in range(NCH):
                    part = parts_of(weights[:, c, :])
                    link(pool.tensor_scalar(scaled[:, :], weights[:, c, :], W_SCALE, None, ALU.mult))
                    link(pool.tensor_copy(part[:, 0, :], scaled[:, :]))
                    link(pool.tensor_tensor(part[:, 1, :], scaled[:, :], part[:, 0, :], ALU.subtract))
            pool.sem_inc(s.split)

        @block.tensor
        def _(pe):
            pe.wait_ge(s.kw, 32)

            def mean_square(h):
                pe.wait_ge(s.sq, h + 1)
                if h >= 2:
                    pe.wait_ge(s.root, h - 1)
                pe.matmul(g.ps[:, 3 + h % 2, :], w.mean[:, :], sq[:, h % 2, :], start=True, stop=True).then_inc(s.ms, 1)

            for h in range(Q_HEADS):
                k = h // GROUP
                if h % GROUP == 0:
                    pe.wait_ge(s_q[k % 2], 16 * (k // 2 + 1))
                if h >= 3:
                    pe.wait_ge(s.done, h - 2)
                for c in range(NCH):
                    ins = pe.matmul(g.ps[:, h % 3, :], wq[:, k % 2, c, (h % GROUP) * P:(h % GROUP + 1) * P],
                                    g.xnT[:, c, :], start=(c == 0), stop=(c == NCH - 1))
                ins.then_inc(s.q, 1)
                if h >= 1:
                    mean_square(h - 1)
            mean_square(Q_HEADS - 1)
            pe.wait_ge(s.split, 1)
            for i in range(n_kv):
                if i >= 2:
                    pe.wait_ge(s.kvout, i - 1)
                if i < KV_HEADS:
                    lhs = [[parts_of(w.wk[:, c, :])[:, a, i * P:(i + 1) * P] for a in range(2)] for c in range(NCH)]
                    rhs = [[x16[:, a, c, :] for a in range(2)] for c in range(NCH)]
                else:
                    t, half = (i - KV_HEADS) // 2, i % 2
                    lhs = [[x16[:, a, c, t * P:(t + 1) * P] for a in range(2)] for c in range(NCH)]
                    rhs = [[parts_of(w.wv[:, c, :])[:, a, half * 512:(half + 1) * 512] for a in range(2)]
                           for c in range(NCH)]
                ins = split_product(pe, g.ps[:, 5 + i % 2, :], lhs, rhs)
                ins.then_inc(s.kv, 1)

        @block.scalar
        def _(act):
            act.wait_ge(s.consts, 1)
            for h in range(Q_HEADS + 1):
                if h < Q_HEADS:
                    act.wait_ge(s.q, h + 1)
                    if h >= 2:
                        act.wait_ge(s.ms, h - 1)
                    act.activation(sq[:, h % 2, :], g.ps[:, h % 3, :], ACT.Square).then_inc(s.sq, 1)
                if h >= 1:
                    act.wait_ge(s.ms, h)
                    if h >= 3:
                        act.wait_ge(s.done, h - 2)
                    act.activation(root[:, (h - 1) % 2, :], g.ps[:, 3 + (h - 1) % 2, :], ACT.Sqrt,
                                   bias=w.eps[:, 0:1]).then_inc(s.root, 1)
            for i in range(n_kv):
                act.wait_ge(s.kv, i + 1)
                if i < KV_HEADS:
                    dst = w.klat[:, i, :]
                else:
                    j = i - KV_HEADS
                    if j >= 2:
                        act.wait_ge(s_v[j % 2], 16 * (j // 2))
                    dst = vout[:, j % 2, :]
                act.activation(dst, g.ps[:, 5 + i % 2, :], ACT.Copy, scale=1.0 / W_SCALE).then_inc(s.kvout, 1)

        @block.vector
        def _(dve):
            link = chain(dve, s.step)
            link(dve.memset(w.eps[:, :], RMS_EPS))
            dve.wait_ge(s.kw, 32)
            dve.tensor_tensor(w.nw[:, 2:3], w.nw[:, 0:1], w.nw[:, 1:2], ALU.mult).then_inc(s.consts, 1)
            dve.wait_ge(s.consts, 1)
            for h in range(Q_HEADS):
                dve.wait_ge(s.root, h + 1)
                link(dve.reciprocal(root[:, h % 2, :], root[:, h % 2, :]))
                dve.scalar_tensor_tensor(w.qT[:, h, :], g.ps[:, h % 3, :], w.nw[:, 2:3], root[:, h % 2, :],
                                         ALU.mult, ALU.mult).then_inc(s.done, 1)
    release(nc, s)


def attend(nc, g, d, w, st):
    def sb(name, shape, dt=F32):
        return st.enter_context(nc.sbuf_tensor("at_" + name, shape, dt))
    s = semaphores(nc, st, "at", "ctx hi split vl0 vl1 step qb kl klsq k kc sq ms msl root rootl v vc s scaled nmax "
                   "expd norm prob turned pt mixed ot")
    NB, HALF = CTX // P, KV_HEADS // 2
    t = named({})
    t.ctx = g.xn
    t.parts = [flat(x).bitcast(F16).rearrange("p (c a n) -> p c a n", c=NCH, a=2)
               for x in (g.xnT, sb("ctx", [P, NCH, CTX]))]
    t.kT = sb("kT", [P, 2, CTX])
    t.R = sb("R", [P, 2, CTX])
    t.V = sb("V", [P, NB + 1, KV_HEADS * P])
    t.sq = sb("sq", [P, 2, CTX])
    t.kl = sb("kl", [P, 2, KV_HEADS, TOK])
    t.sql = sb("sql", [P, KV_HEADS, TOK])
    t.Rl = sb("Rl", [P, 2, KV_HEADS, TOK])
    t.qb = sb("qb", [P, 2, KV_HEADS, GROUP, TOK])
    t.pr = sb("pr", [P, 2, KV])
    t.mx = sb("mx", [P, 2, 2])
    t.sum = sb("sum", [P, 2, 2])
    t.PT = sb("PT", [P, 2, NB + 1, P])
    s_vl = (s.vl0, s.vl1)
    J = KV_HEADS * AT_B
    STEPS = J + 4

    def split_chunk(pool, b, n, c):
        pool.wait_ge(s.ctx, 16 * n)
        part = t.parts[b % 2]
        pool.tensor_copy(part[:, c, 0, :], t.ctx[:, c, :]).then_inc(s.hi, 1)
        pool.wait_ge(s.hi, NCH * (n - 1) + c + 1)
        pool.tensor_tensor(part[:, c, 1, :], t.ctx[:, c, :], part[:, c, 0, :], ALU.subtract).then_inc(s.split, 1)

    with nc.Block() as block:
        @block.sync
        def _(sp):
            sp.dma_start(t.ctx[:, :, :], d.ctxT[0]).then_inc(s.ctx, 16)

        @block.gpsimd
        def _(pool):
            for c in range(NCH):
                split_chunk(pool, 0, 1, c)
            pool.memset(t.V[:, NB, :], 0.0)
            pool.memset(t.PT[:, :, NB, :], 0.0)
    release(nc, s)
    with nc.Fori(0, LAT // AT_B) as it:
        with nc.Block() as block:
            @block.sync
            def _(sp):
                def load_context(b):
                    if b >= 2:
                        sp.wait_ge(s.split, NCH * (b - 1))
                    group = (it * AT_B + b) & (LAT - 1)
                    sp.dma_start(t.ctx[:, :, :], d.ctxT[bass.ds(group, 1), :, :, :]
                                 .rearrange("b p c n -> (b p) c n")).then_inc(s.ctx, 16)

                load_context(1)
                for b in range(AT_B):
                    for half in range(2):
                        if b:
                            sp.wait_ge(s.mixed, KV_HEADS * (b - 1) + HALF * (half + 1))
                        cols = slice(half * 512, (half + 1) * 512)
                        sp.dma_start(t.V[0:TOK, NB, cols],
                                     d.v_lat[bass.ds(it * (AT_B * TOK) + b * TOK, TOK), cols]).then_inc(s_vl[half], 16)
                    if b + 2 <= AT_B:
                        load_context(b + 2)

            @block.gpsimd
            def _(pool):
                def own_keys(b):
                    at = bass.ds(it * (AT_B * TOK) + b * TOK, TOK)
                    if b >= 2:
                        pool.wait_ge(s.s, KV_HEADS * (b - 1))
                    if b:
                        pool.wait_ge(s.msl, b)
                    pool.tensor_copy(t.kl[:, b % 2], w.klat[:, :, at]).then_inc(s.kl, 1)
                    pool.wait_ge(s.kl, b + 1)
                    pool.tensor_tensor(t.sql[:, :, :], t.kl[:, b % 2], t.kl[:, b % 2], ALU.mult).then_inc(s.klsq, 1)

                def own_queries(b):
                    if b >= 2:
                        pool.wait_ge(s.s, KV_HEADS * (b - 1))
                    pool.tensor_copy(flat_heads(t.qb[:, b % 2]),
                                     w.qT[:, :, bass.ds(it * (AT_B * TOK) + b * TOK, TOK)]).then_inc(s.qb, 1)

                own_keys(0)
                own_queries(0)
                for j in range(J):
                    pool.wait_ge(s.norm, j + 1)
                    pool.tensor_scalar(t.pr[:, j % 2, :], t.pr[:, j % 2, :], t.sum[:, j % 2, 1:2], None,
                                       ALU.mult).then_inc(s.prob, 1)
                    b, h = divmod(j, KV_HEADS)
                    if h == 0 and b:
                        pool.wait_ge(s.k, KV_HEADS * b)
                        pool.wait_ge(s.v, KV_HEADS * b)
                    if h < NCH:
                        split_chunk(pool, b + 1, b + 1, h)
                    if h == HALF and b + 1 < AT_B:
                        own_keys(b + 1)
                    if h == HALF + 1 and b + 1 < AT_B:
                        own_queries(b + 1)

            @block.tensor
            def _(pe):
                def keys(j):
                    b, h = divmod(j, KV_HEADS)
                    if b:
                        pe.wait_ge(s.split, NCH * b)
                    if j:
                        pe.wait_ge(s.sq, j)
                    lhs = [[parts_of(w.wk[:, c, :])[:, a, h * P:(h + 1) * P] for a in range(2)] for c in range(NCH)]
                    rhs = [[t.parts[b % 2][:, c, a, :] for a in range(2)] for c in range(NCH)]
                    split_product(pe, g.ps[:, 0, :], lhs, rhs).then_inc(s.k, 1)

                def own_mean_square(b):
                    pe.wait_ge(s.klsq, b + 1)
                    if b:
                        pe.wait_ge(s.root, KV_HEADS * b - 1)
                    pe.matmul(g.ps[:, 2, 0:KV_HEADS * TOK], w.mean[:, :], flat(t.sql), start=True,
                              stop=True).then_inc(s.msl, 1)

                def mean_square(j):
                    pe.wait_ge(s.sq, j + 1)
                    pe.wait_ge(s.rootl, min(AT_B, (j + 1) // KV_HEADS + 1))
                    if j:
                        pe.wait_ge(s.root, j)
                    pe.matmul(g.ps[:, 2, :], w.mean[:, :], t.sq[:, j % 2, :], start=True, stop=True).then_inc(s.ms, 1)

                def score(j):
                    b, h = divmod(j, KV_HEADS)
                    pe.wait_ge(s.qb, b + 1)
                    pe.wait_ge(s.kc, j + 1)
                    if j:
                        pe.wait_ge(s.scaled, j)
                    pe.matmul(g.ps[:, 3, :], flat(t.qb[:, b % 2, h]), t.kT[:, j % 2, :], start=True, stop=True)
                    pe.matmul(g.ps[:, 4, 0:TOK], flat(t.qb[:, b % 2, h]), t.kl[:, b % 2, h, :], start=True,
                              stop=True).then_inc(s.s, 1)

                def values(j):
                    b, i = divmod(j, KV_HEADS)
                    half, n = divmod(i, HALF)
                    if j:
                        pe.wait_ge(s.vc, j)
                    lhs = [[t.parts[b % 2][:, c, a, n * P:(n + 1) * P] for a in range(2)] for c in range(NCH)]
                    rhs = [[parts_of(w.wv[:, c, :])[:, a, half * 512:(half + 1) * 512] for a in range(2)]
                           for c in range(NCH)]
                    split_product(pe, g.ps[:, 1, :], lhs, rhs).then_inc(s.v, 1)

                def turn(j):
                    pe.wait_ge(s.prob, j + 1)
                    if j:
                        pe.wait_ge(s.pt, j)
                    for n in range(NB):
                        pe.transpose(g.ps[:, 5, n * P:(n + 1) * P], t.pr[:, j % 2, n * P:(n + 1) * P], g.ident[:, :])
                    pe.transpose(g.ps[0:TOK, 6, 0:P], t.pr[:, j % 2, CTX:KV], g.ident[:, :]).then_inc(s.turned, 1)

                def mix(j):
                    b, h = divmod(j, KV_HEADS)
                    half = h // HALF
                    pe.wait_ge(s.pt, j + 1)
                    pe.wait_ge(s.vc, KV_HEADS * b + HALF * (half + 1))
                    pe.wait_ge(s_vl[half], 16 * (b + 1))
                    if j:
                        pe.wait_ge(s.ot, j)
                    for n in range(NB + 1):
                        ins = pe.matmul(g.ps[:, 7, 0:P], t.V[:, n, h * P:(h + 1) * P], t.PT[:, j % 2, n, :],
                                        start=(n == 0), stop=(n == NB))
                    ins.then_inc(s.mixed, 1)

                for step in range(STEPS):
                    if step >= 4:
                        mix(step - 4)
                    if step < J:
                        keys(step)
                        if step % KV_HEADS == 0:
                            own_mean_square(step // KV_HEADS)
                    if 1 <= step <= J:
                        mean_square(step - 1)
                        score(step - 1)
                    if step < J:
                        values(step)
                    if 2 <= step <= J + 1:
                        turn(step - 2)

            @block.scalar
            def _(act):
                def exponentials(j):
                    act.wait_ge(s.nmax, j + 1)
                    act.activation(t.pr[:, j % 2, :], t.pr[:, j % 2, :], ACT.Exp, bias=t.mx[:, j % 2, 1:2],
                                   scale=ATT_SCALE, accum_out=t.sum[:, j % 2, 0:1]).then_inc(s.expd, 1)

                def keep_key(j):
                    act.wait_ge(s.k, j + 1)
                    if j >= 2:
                        act.wait_ge(s.s, j - 1)
                        act.wait_ge(s.ms, j - 1)
                    act.activation(t.kT[:, j % 2, :], g.ps[:, 0, :], ACT.Copy, scale=1.0 / W_SCALE).then_inc(s.kc, 1)
                    act.activation(t.sq[:, j % 2, :], g.ps[:, 0, :], ACT.Square, scale=1.0 / W_SCALE).then_inc(s.sq, 1)

                def root(j):
                    act.wait_ge(s.ms, j + 1)
                    if j >= 2:
                        act.wait_ge(s.scaled, j - 1)
                    act.activation(t.R[:, j % 2, :], g.ps[:, 2, :], ACT.Sqrt, bias=w.eps[:, 0:1]).then_inc(s.root, 1)

                def own_root(b):
                    act.wait_ge(s.msl, b + 1)
                    if b >= 2:
                        act.wait_ge(s.scaled, KV_HEADS * (b - 1))
                    act.activation(t.Rl[:, b % 2], g.ps[:, 2, 0:KV_HEADS * TOK].rearrange("p (h n) -> p h n", n=TOK),
                                   ACT.Sqrt, bias=w.eps[:, 0:1]).then_inc(s.rootl, 1)

                def keep_values(j):
                    b, i = divmod(j, KV_HEADS)
                    half, n = divmod(i, HALF)
                    act.wait_ge(s.v, j + 1)
                    if b:
                        act.wait_ge(s.mixed, KV_HEADS * (b - 1) + HALF * (half + 1))
                    act.activation(t.V[:, n, half * 512:(half + 1) * 512], g.ps[:, 1, :], ACT.Copy,
                                   scale=1.0 / W_SCALE).then_inc(s.vc, 1)

                def keep_turned(j):
                    act.wait_ge(s.turned, j + 1)
                    if j >= 2:
                        act.wait_ge(s.mixed, j - 1)
                    act.copy(flat(t.PT[:, j % 2, 0:NB]), g.ps[:, 5, :])
                    act.copy(t.PT[0:TOK, j % 2, NB, :], g.ps[0:TOK, 6, 0:P]).then_inc(s.pt, 1)

                for step in range(STEPS):
                    if 2 <= step <= J + 1:
                        exponentials(step - 2)
                    if step < J:
                        keep_key(step)
                        if step % KV_HEADS == 0:
                            own_root(step // KV_HEADS)
                    if 1 <= step <= J:
                        root(step - 1)
                    if step < J:
                        keep_values(step)
                    if 2 <= step <= J + 1:
                        keep_turned(step - 2)

            @block.vector
            def _(dve):
                link = chain(dve, s.step)

                def scale(j):
                    b, h = divmod(j, KV_HEADS)
                    dve.wait_ge(s.root, j + 1)
                    link(dve.reciprocal(t.R[:, j % 2, :], t.R[:, j % 2, :]))
                    dve.wait_ge(s.s, j + 1)
                    if j >= 2:
                        dve.wait_ge(s.turned, j - 1)
                    link(dve.tensor_tensor(t.pr[:, j % 2, CTX:KV], g.ps[:, 4, 0:TOK], t.Rl[:, b % 2, h, :], ALU.mult))
                    dve.tensor_tensor(t.pr[:, j % 2, 0:CTX], g.ps[:, 3, :], t.R[:, j % 2, :],
                                      ALU.mult).then_inc(s.scaled, 1)
                    dve.wait_ge(s.scaled, j + 1)
                    link(dve.tensor_reduce(t.mx[:, j % 2, 0:1], t.pr[:, j % 2, :], AX.X, ALU.max))
                    dve.tensor_scalar(t.mx[:, j % 2, 1:2], t.mx[:, j % 2, 0:1], -ATT_SCALE, None,
                                      ALU.mult).then_inc(s.nmax, 1)

                def store(j):
                    b, h = divmod(j, KV_HEADS)
                    dve.wait_ge(s.mixed, j + 1)
                    dve.tensor_copy(w.qT[:, h * GROUP:(h + 1) * GROUP, bass.ds(it * (AT_B * TOK) + b * TOK, TOK)],
                                    g.ps[:, 7, 0:P].rearrange("p (a q) -> p a q", a=GROUP)).then_inc(s.ot, 1)

                for step in range(STEPS):
                    if 2 <= step <= J + 1:
                        j = step - 2
                        dve.wait_ge(s.expd, j + 1)
                        dve.reciprocal(t.sum[:, j % 2, 1:2], t.sum[:, j % 2, 0:1]).then_inc(s.norm, 1)
                    if step >= 4:
                        store(step - 4)
                    if step < J and step % KV_HEADS == 0:
                        b = step // KV_HEADS
                        dve.wait_ge(s.rootl, b + 1)
                        link(dve.reciprocal(t.Rl[:, b % 2], t.Rl[:, b % 2]))
                    if 1 <= step <= J:
                        scale(step - 1)
        release(nc, s)


def flat_heads(t):
    return t.rearrange("p k a q -> p (k a) q")


def project_out(nc, g, d, w, st):
    s = semaphores(nc, st, "po", "w0 w1 used out added")
    wo = st.enter_context(nc.sbuf_tensor("po_wo", [P, 2, GROUP, DIM], F32))
    s_w = (s.w0, s.w1)
    with nc.Block() as block:
        @block.sync
        def _(sp):
            for k in range(KV_HEADS):
                if k >= 2:
                    sp.wait_ge(s.used, k - 1)
                sp.dma_start(wo[:, k % 2, :, :], d.wo[:, k * GROUP:(k + 1) * GROUP, :]).then_inc(s_w[k % 2], 16)

        @block.tensor
        def _(pe):
            for k in range(KV_HEADS):
                pe.wait_ge(s_w[k % 2], 16 * (k // 2 + 1))
                for t in range(NT):
                    for a in range(GROUP):
                        h = k * GROUP + a
                        ins = pe.matmul(g.ps[:, t, :], w.qT[:, h, t * P:(t + 1) * P], wo[:, k % 2, a, :],
                                        start=(h == 0), stop=(h == Q_HEADS - 1))
                ins.then_inc(s.used, 1)

        @block.vector
        def _(dve):
            dve.wait_ge(s.used, KV_HEADS)
            for t in range(NT):
                dve.tensor_tensor(g.x[:, t, :], g.x[:, t, :], g.ps[:, t, :], ALU.add).then_inc(s.added, 1)
    release(nc, s)


HM, HIN, NST, NHH, HP, TAPS = 128, 256, 16, 4, 64, 7
SEQ, NSEQ = LAT, TOK
PAD = TAPS - 1
HYDRA_EPS = 1e-5


def hydra(nc, g, d):
    with ExitStack() as st:
        def sb(name, shape, dt=F32):
            return st.enter_context(nc.sbuf_tensor("hy_" + name, shape, dt))
        w = named({name: sb(name, shape) for name, shape in (
                            ("wd", [P, NCH, HM]), ("bd", [P, 1]), ("gate", [P, 1]), ("wu", [HM, DIM]), ("bu", [1, DIM]),
                            ("wx", [HM, HIN]), ("wbc", [HM, 48]), ("wz", [HM, HIN + 2 * NHH]), ("cw", [P, 3, TAPS]),
                            ("cb", [P, 3]), ("dtb", [P, 2 * NHH]), ("alog", [P, 2 * NHH]), ("D", [P, NHH]),
                            ("fcD", [P, 2, NHH]), ("nw", [P, 2]), ("wo", [P, 2, HM]), ("same", [P, P]),
                            ("at", [P, 2, SEQ]), ("past", [P, 2, SEQ]))})
        names = list(w.all)
        w.ones = sb("ones", [1, P])
        w.xmid = sb("xmid", [HM, ROWS])
        w.u = sb("u", [HM, ROWS])
        w.A = sb("A", [P, 2 * NHH])
        w.alpha = sb("alpha", [P, 1])
        w.cp = sb("cp", [P, 3, NSEQ, PAD + SEQ])
        w.acc = sb("acc", [P, 3, ROWS])
        w.c0 = sb("c0", [NST, ROWS])
        w.xtok = sb("xtok", [P, NT, HIN])
        w.sz = sb("sz", [P, NT, HIN])
        w.yz = sb("yz", [P, NT, HIN])
        w.y2 = sb("y2", [P, NT, HIN])
        w.ynT = sb("ynT", [P, 2, ROWS])
        w.dt = sb("dt", [P, NT, 2 * NHH])
        w.sp = sb("sp", [P, 4, NT * 2 * NHH])
        w.dA = sb("dA", [P, NT, 2 * NHH])
        w.spread = sb("spread", [P, NT, 2, NHH, SEQ])
        w.d0 = sb("d0", [P, NT, 2, NHH, SEQ])
        w.d1 = sb("d1", [P, NT, 2, NHH, SEQ])
        w.L = sb("L", [P, NT, 2, NHH, SEQ])
        w.Gm = sb("Gm", [P, NT, P])
        w.Mf = sb("Mf", [P, 2, NHH, P])
        w.Mb = sb("Mb", [P, 2, NHH, P])
        w.f = sb("f", [P, NT, NHH])
        w.ms = sb("ms", [P, NT])
        w.eps = sb("eps", [P, 1])

        s = semaphores(nc, st, "hy0", "loaded step down gelu consts")
        with nc.Block() as block:
            @block.sync
            def _(sp):
                for n in names:
                    src = d.all["hy_" + n]
                    if n in ("gate", "dtb", "alog", "D"):
                        src = src.partition_broadcast(P)
                    t = w.all[n]
                    sp.dma_start(t[tuple([slice(None)] * len(t.shape))], src).then_inc(s.loaded, 16)

            @block.gpsimd
            def _(pool):
                for t in (w.cp, w.Mf, w.Mb):
                    pool.memset(flat(t), 0.0)
                pool.memset(w.ones[:, :], 1.0)
                pool.memset(w.eps[:, :], HYDRA_EPS)

            @block.tensor
            def _(pe):
                pe.wait_ge(s.loaded, 16 * len(names))
                for c in range(NCH):
                    ins = pe.matmul(g.ps[:, 0, :], w.wd[:, c, :], g.xnT[:, c, :], start=(c == 0), stop=(c == NCH - 1))
                ins.then_inc(s.down, 1)

            @block.scalar
            def _(act):
                act.wait_ge(s.loaded, 16 * len(names))
                act.activation(w.A[:, :], w.alog[:, :], ACT.Exp).then_inc(s.consts, 1)
                act.activation(w.alpha[:, :], w.gate[:, :], ACT.Sigmoid).then_inc(s.consts, 1)
                act.wait_ge(s.down, 1)
                act.activation(w.xmid[:, :].rearrange("p (b l) -> p b l", b=NSEQ),
                               g.ps[:, 0, :].rearrange("p (l b) -> p b l", b=NSEQ), ACT.Gelu,
                               bias=w.bd[:, 0:1]).then_inc(s.gelu, 1)

            @block.vector
            def _(dve):
                dve.wait_ge(s.consts, 1)
                dve.tensor_scalar(w.A[:, :], w.A[:, :], -1.0, None, ALU.mult).then_inc(s.step, 1)
        release(nc, s)
        hydra_pass(nc, g, w, "hy1", w.xmid)
        hydra_pass(nc, g, w, "hy2", w.u)

        s = semaphores(nc, st, "hy3", "step blended up added")
        with nc.Block() as block:
            @block.vector
            def _(dve):
                link = chain(dve, s.step)
                link(dve.tensor_scalar(w.ynT[:, 0, :], w.xmid[:, :], w.alpha[:, 0:1], None, ALU.mult))
                link(dve.tensor_scalar(w.ms[:, 0:1], w.alpha[:, :], -1.0, 1.0, ALU.mult, ALU.add))
                link(dve.scalar_tensor_tensor(w.ynT[:, 1, :], w.u[:, :], w.ms[:, 0:1], w.ynT[:, 0, :],
                                              ALU.mult, ALU.add))
                dve.tensor_tensor(w.ynT[:, 0, :].rearrange("p (l b) -> p b l", b=NSEQ),
                                  w.ynT[:, 1, :].rearrange("p (b l) -> p b l", b=NSEQ),
                                  w.xmid[:, :].rearrange("p (b l) -> p b l", b=NSEQ), ALU.add).then_inc(s.blended, 1)
                link(dve.tensor_tensor(flat(g.x), flat(g.x), flat(g.xn), ALU.add))
                for t in range(NT):
                    dve.wait_ge(s.up, t + 1)
                    dve.tensor_tensor(g.x[:, t, :], g.x[:, t, :], g.ps[:, t, :], ALU.add).then_inc(s.added, 1)

            @block.tensor
            def _(pe):
                pe.wait_ge(s.blended, 1)
                for t in range(NT):
                    pe.matmul(g.ps[:, t, :], w.ynT[:, 0, t * P:(t + 1) * P], w.wu[:, :], start=True, stop=False)
                    pe.matmul(g.ps[:, t, :], w.ones[:, :], w.bu[:, :], start=False, stop=True).then_inc(s.up, 1)
        release(nc, s)


def hydra_pass(nc, g, w, name, src):
    with ExitStack() as st:
        s = semaphores(nc, st, name, "step xbc z dt cp e1 e2 sp da spread dab conv silu c0 xst xtok sz gram masked mat "
                 "y gated ms root yn yt ynT out")
        lanes = (P, P, 48)
        with nc.Block() as block:
            @block.tensor
            def _(pe):
                for i in range(2):
                    pe.matmul(g.ps[:, i, :], w.wx[:, i * P:(i + 1) * P], src[:, :], start=True,
                              stop=True).then_inc(s.xbc, 1)
                pe.matmul(g.ps[0:48, 2, :], w.wbc[:, :], src[:, :], start=True, stop=True).then_inc(s.xbc, 1)
                for t in range(NT):
                    pe.matmul(g.ps[:, 4 + t, 0:HIN + 2 * NHH], src[:, t * P:(t + 1) * P], w.wz[:, :], start=True,
                              stop=True).then_inc(s.z, 1)
                pe.wait_ge(s.spread, 1)
                pe.matmul(g.ps[:, 3, :], w.same[:, :], flat(w.spread), start=True, stop=True).then_inc(s.dab, 1)
                pe.wait_ge(s.silu, 2)
                for t in range(NT):
                    for i in range(2):
                        ins = pe.transpose(g.ps[:, t // 2, (t % 2) * HIN + i * P:(t % 2) * HIN + (i + 1) * P],
                                           w.acc[:, i, t * P:(t + 1) * P], g.ident[:, :])
                ins.then_inc(s.xst, 1)
                pe.wait_ge(s.c0, 1)
                for t in range(NT):
                    ins = pe.matmul(g.ps[:, 2, t * P:(t + 1) * P], w.acc[0:NST, 2, t * P:(t + 1) * P],
                                    w.c0[:, t * P:(t + 1) * P], start=True, stop=True)
                ins.then_inc(s.gram, 1)
                pe.wait_ge(s.sz, NT)
                pe.wait_ge(s.xtok, 1)
                for t in range(NT):
                    for i in range(2):
                        pe.matmul(g.ps[:, 4 + t, HIN:HIN + NHH], w.acc[:, i, t * P:(t + 1) * P], w.fcD[:, i, :],
                                  start=(i == 0), stop=(i == 1))
                    pe.wait_ge(s.mat, t + 1)
                    for h in range(NHH):
                        for n, M in enumerate((w.Mf, w.Mb)):
                            ins = pe.matmul(g.ps[:, 4 + t, h * HP:(h + 1) * HP], M[:, t % 2, h, :],
                                            w.xtok[:, t, h * HP:(h + 1) * HP], start=(n == 0), stop=(n == 1))
                    ins.then_inc(s.y, 1)
                for t in range(NT):
                    pe.wait_ge(s.yn, t + 1)
                    for i in range(2):
                        ins = pe.transpose(g.ps[:, i, t * P:(t + 1) * P], w.yz[:, t, i * P:(i + 1) * P], g.ident[:, :])
                ins.then_inc(s.yt, 1)
                for i in range(2):
                    pe.wait_ge(s.ynT, i + 1)
                    ins = pe.matmul(g.ps[:, 2, :], w.wo[:, i, :], w.ynT[:, i, :], start=(i == 0), stop=(i == 1))
                ins.then_inc(s.out, 1)

            @block.scalar
            def _(act):
                for i, n in enumerate(lanes):
                    act.wait_ge(s.xbc, i + 1)
                    act.copy(w.cp[0:n, i, :, PAD:], g.ps[0:n, i, :].rearrange("p (b l) -> p b l", l=SEQ)).then_inc(s.cp, 1)
                act.wait_ge(s.e1, 1)
                act.activation(w.sp[:, 1, :], w.sp[:, 0, :], ACT.Exp, scale=-1.0).then_inc(s.e2, 1)
                act.wait_ge(s.sp, 1)
                act.activation(flat(w.dA), w.sp[:, 3, :], ACT.Exp).then_inc(s.da, 1)
                act.wait_ge(s.dt, 1)
                for t in range(NT):
                    act.activation(w.sz[:, t, :], g.ps[:, 4 + t, 0:HIN], ACT.Silu).then_inc(s.sz, 1)
                for i, n in ((0, P), (1, P), (2, 48)):
                    act.wait_ge(s.conv, i + 1)
                    act.activation(w.acc[0:n, i, :], w.acc[0:n, i, :], ACT.Silu, bias=w.cb[0:n, i:i + 1]).then_inc(s.silu, 1)
                act.wait_ge(s.silu, 3)
                act.copy(w.c0[:, :], w.acc[32:32 + NST, 2, :]).then_inc(s.c0, 1)
                act.wait_ge(s.xst, 1)
                act.copy(w.xtok[:, :, :].rearrange("p (a t) n -> p a (t n)", a=2), g.ps[:, 0:2, :]).then_inc(s.xtok, 1)
                act.wait_ge(s.ms, 1)
                act.activation(w.ms[:, :], w.ms[:, :], ACT.Sqrt, scale=1.0 / HIN, bias=w.eps[:, 0:1]).then_inc(s.root, 1)
                act.wait_ge(s.yt, 1)
                for i in range(2):
                    act.activation(w.ynT[:, i, :], g.ps[:, i, :], ACT.Copy, scale=w.nw[:, i:i + 1]).then_inc(s.ynT, 1)
                act.wait_ge(s.out, 1)
                act.copy(w.u[:, :], g.ps[:, 2, :])

            @block.vector
            def _(dve):
                link = chain(dve, s.step)
                n8 = 2 * NHH
                rows = [w.sp[:, i, :] for i in range(4)]
                tiled = [r.rearrange("p (t k) -> p t k", t=NT) for r in rows]
                dve.wait_ge(s.z, NT)
                dve.tensor_tensor(w.dt[:, :, :], g.ps[:, 4:8, HIN:HIN + n8],
                                  w.dtb[:, None, :].broadcast_to([P, NT, n8]), ALU.add).then_inc(s.dt, 1)
                dve.wait_ge(s.dt, 1)
                dve.scalar_tensor_tensor(rows[0], flat(w.dt), -1.0, flat(w.dt), ALU.mult, ALU.max).then_inc(s.e1, 1)
                dve.wait_ge(s.e2, 1)
                link(dve.tensor_scalar(rows[2], rows[1], 2.0, None, ALU.add))
                link(dve.reciprocal(rows[2], rows[2]))
                link(dve.tensor_tensor(rows[1], rows[1], rows[2], ALU.mult))
                link(dve.tensor_tensor(rows[2], rows[1], rows[1], ALU.mult))
                link(dve.tensor_scalar(rows[3], rows[2], 1.0 / 15, 1.0 / 13, ALU.mult, ALU.add))
                for k in (11, 9, 7, 5, 3, 1):
                    link(dve.tensor_tensor(rows[3], rows[3], rows[2], ALU.mult))
                    link(dve.tensor_scalar(rows[3], rows[3], 1.0 / k, None, ALU.add))
                link(dve.scalar_tensor_tensor(rows[3], rows[3], 2.0, rows[1], ALU.mult, ALU.mult))
                link(dve.scalar_tensor_tensor(flat(w.dt), flat(w.dt), 0.0, rows[3], ALU.max, ALU.add))
                dve.tensor_tensor(tiled[3], w.dt[:, :, :], w.A[:, None, :].broadcast_to([P, NT, n8]),
                                  ALU.mult).then_inc(s.sp, 1)
                dve.wait_ge(s.da, 1)
                for way in range(2):
                    ins = dve.tensor_tensor(
                        w.spread[:, :, way, :, :],
                        w.dA[:, :, way * NHH:(way + 1) * NHH, None].broadcast_to([P, NT, NHH, SEQ]),
                        w.at[:, way:way + 1, None, :].broadcast_to([P, NT, NHH, SEQ]), ALU.mult)
                    if way == 0:
                        link(ins)
                ins.then_inc(s.spread, 1)
                for i, n in enumerate(lanes):
                    dve.wait_ge(s.cp, i + 1)
                    acc = w.acc[0:n, i, :].rearrange("p (b l) -> p b l", l=SEQ)
                    link(dve.tensor_scalar(acc, w.cp[0:n, i, :, 0:SEQ], w.cw[0:n, i, 0:1], None, ALU.mult))
                    for k in range(1, TAPS):
                        ins = dve.scalar_tensor_tensor(acc, w.cp[0:n, i, :, k:k + SEQ], w.cw[0:n, i, k:k + 1], acc,
                                                       ALU.mult, ALU.add)
                        if k < TAPS - 1:
                            link(ins)
                    ins.then_inc(s.conv, 1)
                dve.wait_ge(s.dab, 1)
                dab = g.ps[:, 3, :].rearrange("p (t w h l) -> p t w h l", t=NT, w=2, h=NHH)
                for way in range(2):
                    link(dve.tensor_tensor(w.d0[:, :, way, :, :], dab[:, :, way, :, :],
                                           w.past[:, way:way + 1, None, :].broadcast_to([P, NT, NHH, SEQ]), ALU.mult))
                    link(dve.tensor_tensor(
                        w.d1[:, :, way, :, :],
                        w.dt[:, :, way * NHH:(way + 1) * NHH, None].broadcast_to([P, NT, NHH, SEQ]),
                        w.at[:, way:way + 1, None, :].broadcast_to([P, NT, NHH, SEQ]), ALU.mult))
                link(dve.tensor_tensor_scan(flat(w.L), flat(w.d0), flat(w.d1), 0.0, ALU.mult, ALU.add))
                dve.wait_ge(s.gram, 1)
                dve.tensor_tensor(w.Gm[:, :, :], g.ps[:, 2, :].rearrange("p (t n) -> p t n", t=NT),
                                  w.same[:, None, :].broadcast_to([P, NT, P]), ALU.mult).then_inc(s.masked, 1)
                dve.wait_ge(s.masked, 1)
                for t in range(NT):
                    if t >= 2:
                        dve.wait_ge(s.y, t - 1)
                    dims = [NHH, 8, SEQ - 1]
                    dve.tensor_tensor(custom(w.Mf[:, t % 2], 1, [[P, NHH], [SEQ, 8], [1, SEQ - 1]]),
                                      custom(w.Gm[:, t], 0, [[0, NHH], [SEQ, 8], [1, SEQ - 1]]),
                                      custom(w.L[:, t, 0], 0, [[SEQ, NHH], [0, 8], [1, SEQ - 1]]), ALU.mult)
                    dve.tensor_tensor(custom(w.Mb[:, t % 2], 0, [[P, NHH], [SEQ, 8], [1, SEQ - 1]]),
                                      custom(w.Gm[:, t], 1, [[0, NHH], [SEQ, 8], [1, SEQ - 1]]),
                                      custom(w.L[:, t, 1], SEQ - 2, [[SEQ, NHH], [0, 8], [-1, SEQ - 1]]),
                                      ALU.mult).then_inc(s.mat, 1)
                dve.wait_ge(s.y, NT)
                dve.wait_ge(s.xtok, 1)
                dve.wait_ge(s.sz, NT)
                heads = lambda a: a.rearrange("p t (h n) -> p (t h) n", h=NHH)
                link(dve.tensor_tensor(w.f[:, :, :], g.ps[:, 4:8, HIN:HIN + NHH],
                                       w.D[:, None, :].broadcast_to([P, NT, NHH]), ALU.add))
                link(dve.tensor_tensor(heads(w.yz[:, :, :]), heads(w.xtok[:, :, :]),
                                       flat(w.f)[:, :, None].broadcast_to([P, NT * NHH, HP]), ALU.mult))
                link(dve.tensor_tensor(w.yz[:, :, :], w.yz[:, :, :], g.ps[:, 4:8, 0:HIN], ALU.add))
                link(dve.tensor_tensor(w.yz[:, :, :], w.yz[:, :, :], w.sz[:, :, :], ALU.mult))
                link(dve.tensor_tensor(w.y2[:, :, :], w.yz[:, :, :], w.yz[:, :, :], ALU.mult))
                dve.tensor_reduce(w.ms[:, :], w.y2[:, :, :], AX.X, ALU.add).then_inc(s.ms, 1)
                dve.wait_ge(s.root, 1)
                link(dve.reciprocal(w.ms[:, :], w.ms[:, :]))
                for t in range(NT):
                    dve.tensor_scalar(w.yz[:, t, :], w.yz[:, t, :], w.ms[:, t:t + 1], None, ALU.mult).then_inc(s.yn, 1)
        release(nc, s)


def store_result(nc, g, d):
    with ExitStack() as st:
        s = semaphores(nc, st, "fin", "stored")
        with nc.Block() as block:
            @block.sync
            def _(sp):
                for t in range(NT):
                    sp.dma_start(d.out[t * P:(t + 1) * P, :], g.x[:, t, :]).then_inc(s.stored, 16)
                sp.wait_ge(s.stored, 16 * NT)


_SCRATCH = {
    "q_scratch": ((LAT, 3, DIM), "int32"),
    "keys_hi": ((LAT, METHODS, DIM), "float32"),
    "keys_lo": ((LAT, METHODS, DIM), "float32"),
    "xatt": ((ROWS, DIM), "float32"),
    "v_lat": ((ROWS, KV_HEADS * P), "float32"),
}


def program(nc, d):
    with ExitStack() as st:
        shared = tensors(nc, st, "g", (("x", [P, NT, DIM], F32), ("xn", [P, NT, DIM], F32), ("xnT", [P, NCH, ROWS], F32),
                                ("ident", [P, P], F32), ("identb", [P, P], BF16), ("eps", [P, 1], F32)))
        shared["ps"] = st.enter_context(nc.psum_tensor("ps", [P, 8, 512], F32))
        with ExitStack() as sa:
            g = named(shared | tensors(nc, sa, "g", (("targets", [P, DIM + EXTRA], F16), ("mask", [P, 2 * U_MAX, HD], BF16),
                                    ("ident16", [P, P], F16),
                                    ("avg1", [P, P], F32), ("avg2", [P, P], F32),
                                    ("key_hi", [P, NCH, LAT * METHODS], F32),
                                    ("key_lo", [P, NCH, LAT * METHODS], F32))))
            load_constants(nc, g, d)
            layernorm_and_turn(nc, g, "ln0")
            curve_keys(nc, g, d)
            graph_layers(nc, g, d)
        g = named(shared)
        add_point_attention(nc, g, d)
        layernorm_and_turn(nc, g, "ln1")
        bound_attention(nc, g, d)
        layernorm_and_turn(nc, g, "ln2")
        experts(nc, g, d, "e0", 0, 2.0, None)
        layernorm_and_turn(nc, g, "ln3")
        cross_attention(nc, g, d)
        layernorm_and_turn(nc, g, "ln4")
        hydra(nc, g, d)
        layernorm_and_turn(nc, g, "ln5")
        experts(nc, g, d, "e1", 4 * EXPERTS, 1.0 / RANK, 3 * ROWS // EXPERTS)
        store_result(nc, g, d)


def _layout(i):
    f = np.float32
    out = {}
    out["x"] = np.asarray(i["x"]).reshape(ROWS, DIM)
    out["coords"] = np.ascontiguousarray(np.asarray(i["ctx_4096"])[:, 0:3, :])
    out["ident"] = np.eye(P, dtype=f)
    t = list(range(DIM)) + [DIM - 1] * TAIL
    for n in range(HEAD_POINTS):
        t += [min(j, n + KNN // 2) for j in range(KNN)]
    out["targets"] = np.array(t, f)
    j = np.arange(HD) // KNN
    out["pointmask"] = np.where(j[np.arange(P) % HD][:, None] == j[None, :], 0.0, -BIG).astype(f)
    q = np.arange(P)
    out["avg1"] = (0.25 * (q[:, None] % 32 == q[None, :] % 32)).astype(f)
    out["avg2"] = (0.25 * (q[:, None] % 64 == q[None, :] % 64)).astype(f)
    out["nidx"] = ((q % 8)[:, None] * 64 + np.arange(64)[None, :]).astype(np.int32)
    for l, (perm, name) in enumerate((([2, 0, 3, 1], "1"), ([1, 3, 0, 2], "2"))):
        place = [perm.index(m) for m in range(METHODS)]
        lin = np.asarray(i[f"L0_xattn_W_lin{name}"]).reshape(64, 2, HEADS, 8, METHODS)
        out[f"lin{l}"] = np.ascontiguousarray(lin[:, :, :, :, place].transpose(0, 1, 2, 4, 3).reshape(64, 2, P))
        conv = np.asarray(i[f"L0_xattn_W_conv{name}"])
        out[f"conv{l}"] = np.ascontiguousarray(np.tile(conv.T, (1, P // OUTS[l])))
        out[f"lbias{l}"] = np.asarray(i[f"L0_xattn_b_lin{name}"]).reshape(64, 1)
    w3 = np.asarray(i["L0_xattn_W_conv3"])
    for name, at in (("w3a", 0), ("w3b", 32)):
        z = np.zeros((HEADS, METHODS, 8, 32), f)
        z[:, 0] = w3[:, at:at + 32].T.reshape(HEADS, 8, 32)
        out[name] = z.reshape(P, 32)
    z = np.zeros((2, 64, 2, 32), f)
    for c in range(2):
        z[c, :, c, :] = w3[:, 64:].T
    out["w3c"] = z.reshape(P, 2, 32)
    A = lambda n: np.asarray(i[n])

    def chunked(wt):
        return np.ascontiguousarray(wt.reshape(NCH, P, -1).transpose(1, 0, 2))

    out["bind"] = np.ascontiguousarray(np.stack([A("L0_attn_bv_q"), A("L0_attn_bv_k"), A("L0_attn_bv_v")], 1))
    out["sel4"] = np.ascontiguousarray(np.broadcast_to(np.eye(NCH, dtype=f)[:, :, None], (NCH, NCH, P)))
    out["causal"] = ((q[:, None] // TOK == q[None, :] // TOK) & (q[:, None] <= q[None, :])).astype(f)
    out["iota8"] = np.arange(EXPERTS).astype(f)
    out["e0_wa"] = chunked(np.concatenate([A("L0_ffn_gate_w").T, A("L0_ffn_lora_A").reshape(P, DIM).T], 1))
    out["e0_wb"] = chunked(A("L0_ffn_base_w").T)
    out["e0_bias"] = A("L0_ffn_base_b").reshape(1, DIM)
    out["e0_lb"] = np.ascontiguousarray(A("L0_ffn_lora_B").transpose(0, 2, 1).reshape(P, DIM))
    out["e1_wa"] = chunked(np.concatenate([A("L1_ffn_gw1").T, A("L1_ffn_lora_A").transpose(1, 0, 2).reshape(DIM, P)], 1))
    out["e1_wb"] = chunked(A("L1_ffn_weight").T)
    out["e1_bias"] = np.zeros((1, DIM), f)
    out["e1_lb"] = np.ascontiguousarray(A("L1_ffn_lora_B").reshape(P, DIM))
    out["e1_rows"] = np.stack([A("L1_ffn_gb1"), A("L1_ffn_ln_gamma"), A("L1_ffn_ln_beta")])
    out["e1_gb2"] = A("L1_ffn_gb2")
    out["e1_gw2"] = np.ascontiguousarray(A("L1_ffn_gw2").T)
    out["ctxT"] = np.ascontiguousarray(A("ctx_4096").transpose(0, 2, 1).reshape(LAT, NCH, P, CTX).transpose(0, 2, 1, 3))
    out["wq"], out["wk"], out["wv"] = (chunked(A("L1_xattn_" + n)) for n in ("Wq", "Wk", "Wv"))
    out["wo"] = np.ascontiguousarray(A("L1_xattn_Wo").reshape(Q_HEADS, P, DIM).transpose(1, 0, 2))
    out["qk_norm"] = np.ascontiguousarray(np.stack([A("L1_xattn_q_norm_w"), A("L1_xattn_k_norm_w")], 1))
    out["mean128"] = np.full((P, P), 1.0 / P, f)
    H = lambda n: A("L1_attn_" + n)
    out["hy_wd"] = chunked(H("w_down").T)
    out["hy_bd"] = H("b_down").reshape(HM, 1)
    out["hy_gate"] = H("gate1").reshape(1)
    out["hy_wu"] = np.ascontiguousarray(H("w_up").T)
    out["hy_bu"] = H("b_up").reshape(1, DIM)
    win = H("hy_in_w").T
    X0, B0, C0, D0 = HIN, 2 * HIN, 2 * HIN + NST, 2 * HIN + 2 * NST
    gap = np.zeros((HM, 32 - NST), f)
    out["hy_wx"] = np.ascontiguousarray(win[:, X0:B0])
    out["hy_wbc"] = np.concatenate([win[:, B0:C0], gap, win[:, C0:D0]], 1)
    out["hy_wz"] = np.concatenate([win[:, 0:X0], win[:, D0:]], 1)

    def channels(v):
        z = np.zeros((P, 3, v.shape[1]), f)
        z[:, 0], z[:, 1] = v[0:P], v[P:2 * P]
        z[0:NST, 2], z[32:32 + NST, 2] = v[HIN:HIN + NST], v[HIN + NST:]
        return z
    out["hy_cw"] = channels(H("hy_conv_w")[:, 0, :])
    out["hy_cb"] = channels(H("hy_conv_b")[:, None])[:, :, 0]
    out["hy_dtb"] = np.tile(H("hy_dt_bias"), 2)
    out["hy_alog"] = np.tile(H("hy_A_log"), 2)
    out["hy_D"] = H("hy_D")
    out["hy_fcD"] = np.ascontiguousarray(H("hy_fcD_w").T.reshape(2, P, NHH).transpose(1, 0, 2))
    out["hy_nw"] = np.ascontiguousarray(H("hy_norm_w").reshape(2, P).T)
    out["hy_wo"] = np.ascontiguousarray(H("hy_out_w").T.reshape(2, P, HM).transpose(1, 0, 2))
    out["hy_same"] = (q[:, None] // SEQ == q[None, :] // SEQ).astype(f)
    pos, col = (q % SEQ)[:, None], np.arange(SEQ)[None, :]
    out["hy_at"] = np.stack([pos == col, pos == SEQ - 1 - col], 1).astype(f)
    out["hy_past"] = np.stack([col > pos, SEQ - 1 - col < pos], 1).astype(f)
    return out


def kernel(**inputs):
    import concourse.bacc as _bacc
    from concourse.bass_utils import run_bass_kernel_spmd as _run

    nc = _bacc.Bacc("TRN2", target_bir_lowering=False, num_devices=1)
    tensor, arrays = {}, {}
    for name, a in _layout(inputs).items():
        arrays["in_" + name] = a
        tensor[name] = nc.dram_tensor("in_" + name, a.shape, mybir.dt.from_np(a.dtype), kind="ExternalInput").ap()
    for name, (shape, dt) in _SCRATCH.items():
        tensor[name] = nc.dram_tensor("scratch_" + name, shape, mybir.dt.from_np(np.dtype(dt)), kind="Internal").ap()
    tensor["out"] = nc.dram_tensor("out_0_dram", (ROWS, DIM), F32, kind="ExternalOutput").ap()
    program(nc, named(tensor))
    r = _run(nc, [arrays], core_ids=[0])
    return r.results[0]["out_0_dram"].reshape(LAT, TOK, DIM)
```
